# Optimizing a Trainium2 kernel written in Bass

```python
import numpy as np
import jax
import jax.numpy as jnp

def _softmax(x, axis=-1):
    return jax.nn.softmax(x, axis=axis)

def _gelu(x):
    return jax.nn.gelu(x, approximate=True)

def _silu(x):
    return jax.nn.silu(x)

def _sigmoid(x):
    return jax.nn.sigmoid(x)

def _layernorm(x, axis=-1, eps=1e-05):
    m = jnp.mean(x, axis=axis, keepdims=True)
    v = jnp.var(x, axis=axis, keepdims=True)
    return (x - m) / jnp.sqrt(v + eps)

def _scatter_add(tgt, idx, src, axis=0):
    return tgt.at[idx].add(src)

def _segment_sum(src, seg, n):
    return jax.ops.segment_sum(src, seg, n)
kernel_name = 'mk_gnn_preln_d4_gnn_r32_943648'

def setup_inputs(seed: int=0):
    np.random.seed(seed)
    _w = jnp.asarray

    def _rec_inputs():
        import jax
        import jax.numpy as jnp
        _gk = jax.random.key(seed)
        x = -0.000202 + 1 * jax.random.normal(jax.random.fold_in(_gk, 1), (50000, 128), jnp.float32)
        src = jax.random.randint(jax.random.fold_in(_gk, 2), (50000,), 0, 50000, jnp.int32)
        dst = jnp.minimum((50000 * jax.random.uniform(jax.random.fold_in(_gk, 3), (50000,)) ** 2.0).astype(jnp.int32), 49999)
        _o = jnp.argsort(dst, stable=True)
        src = src[_o]
        dst = dst[_o]
        edge_attr_70 = 0.000111316 + 1.00009 * jax.random.normal(jax.random.fold_in(_gk, 12), (50000, 70), jnp.float32)
        edge_weight = jax.random.uniform(jax.random.fold_in(_gk, 14), (50000,), jnp.float32, 0.0, 0.999998)
        return (x, src, dst, edge_attr_70, edge_weight)
    x, src, dst, edge_attr_70, edge_weight = _rec_inputs()

    def _L0_gnn_setup():
        import jax, jax.numpy as jnp
        import numpy as np
        N_NODES = 50000
        D = 128
        N_EDGES = 25000

        def _sage_layer(h, src, dst, W_self, W_neigh, b):
            msgs = jnp.take(h, src, axis=0)
            agg = jax.ops.segment_sum(msgs, dst, num_segments=N_NODES)
            deg = jax.ops.segment_sum(jnp.ones((src.shape[0],), h.dtype), dst, num_segments=N_NODES)
            h_neigh = agg / jnp.maximum(deg, 1.0)[:, None]
            return h @ W_self + h_neigh @ W_neigh + b
        key = jax.random.key(seed)
        ks = jax.random.split(key, 10)
        h = jax.random.normal(ks[0], (N_NODES, D), dtype=jnp.float32)
        src = jax.random.randint(ks[1], (N_EDGES,), 0, N_NODES)
        dst = jax.random.randint(ks[2], (N_EDGES,), 0, N_NODES)
        s = 1.0 / np.sqrt(D)
        W_self0 = jax.random.uniform(ks[3], (D, D), jnp.float32, -s, s)
        W_neigh0 = jax.random.uniform(ks[4], (D, D), jnp.float32, -s, s)
        b0 = jnp.zeros((D,), jnp.float32)
        W_self1 = jax.random.uniform(ks[5], (D, D), jnp.float32, -s, s)
        W_neigh1 = jax.random.uniform(ks[6], (D, D), jnp.float32, -s, s)
        b1 = jnp.zeros((D,), jnp.float32)
        return {'h': h, 'src': src, 'dst': dst, 'W_self0': W_self0, 'W_neigh0': W_neigh0, 'b0': b0, 'W_self1': W_self1, 'W_neigh1': W_neigh1, 'b1': b1}
    _L0_gnn_all = _L0_gnn_setup()
    _L0_gnn_in = {k: v for k, v in _L0_gnn_all.items() if k in ('W_self0', 'W_neigh0', 'b0', 'W_self1', 'W_neigh1', 'b1')}
    del _L0_gnn_all

    def _L1_gnn_setup():
        import jax, jax.numpy as jnp
        import numpy as np
        N_NODES = 50000
        IN_C = 128
        OUT_C = 128
        EDGE_F = 65
        N_EDGES = 25000
        EDGE_ATTR_COLS = 70
        key = jax.random.key(seed)
        ks = jax.random.split(key, 10)
        fcat = 3 * IN_C + EDGE_F
        sc = lambda d: 1.0 / np.sqrt(d)
        return {'x': jax.random.normal(ks[0], (N_NODES, IN_C), dtype=jnp.float32), 'edge_index': jax.random.randint(ks[1], (2, N_EDGES), 0, N_NODES, dtype=jnp.int32), 'edge_attr': jax.random.normal(ks[2], (N_EDGES, EDGE_ATTR_COLS), dtype=jnp.float32), 'Wf': jax.random.normal(ks[3], (fcat, IN_C), dtype=jnp.float32) * sc(fcat), 'bf': jnp.zeros((IN_C,), dtype=jnp.float32), 'Wq': jax.random.normal(ks[4], (IN_C, IN_C), dtype=jnp.float32) * sc(IN_C), 'Wk': jax.random.normal(ks[5], (IN_C, IN_C), dtype=jnp.float32) * sc(IN_C), 'Wa': jax.random.normal(ks[6], (IN_C, 1), dtype=jnp.float32) * sc(IN_C), 'Wu': jax.random.normal(ks[7], (IN_C, OUT_C), dtype=jnp.float32) * sc(IN_C), 'bu': jnp.zeros((OUT_C,), dtype=jnp.float32)}
    _L1_gnn_all = _L1_gnn_setup()
    _L1_gnn_in = {k: v for k, v in _L1_gnn_all.items() if k in ('Wf', 'bf', 'Wq', 'Wk', 'Wa', 'Wu', 'bu')}
    del _L1_gnn_all

    def _L2_gnn_setup():
        import jax, jax.numpy as jnp
        import numpy as np
        N = 50000
        E = 25000
        NFEAT = 128
        NOUT = 128
        EPS = 1e-05
        key = jax.random.key(seed)
        ks = jax.random.split(key, 6)
        x = jax.random.normal(ks[0], (N, NFEAT), dtype=jnp.float32)
        edge_index = jax.random.randint(ks[1], (2, E), 0, N)
        edge_weight = jax.random.uniform(ks[2], (E,), dtype=jnp.float32)
        W = jax.random.normal(ks[3], (NFEAT, NOUT), dtype=jnp.float32) / np.sqrt(NFEAT).astype(np.float32)
        b = jnp.zeros((NOUT,), jnp.float32)
        bn_gamma = jnp.ones((NOUT,), jnp.float32)
        bn_beta = jnp.zeros((NOUT,), jnp.float32)
        ln_gamma = jnp.ones((NOUT,), jnp.float32)
        ln_beta = jnp.zeros((NOUT,), jnp.float32)
        return {'x': x, 'edge_index': edge_index, 'edge_weight': edge_weight, 'W': W, 'b': b, 'bn_gamma': bn_gamma, 'bn_beta': bn_beta, 'ln_gamma': ln_gamma, 'ln_beta': ln_beta}
    _L2_gnn_all = _L2_gnn_setup()
    _L2_gnn_in = {k: v for k, v in _L2_gnn_all.items() if k in ('W', 'b', 'bn_gamma', 'bn_beta', 'ln_gamma', 'ln_beta')}
    del _L2_gnn_all

    def _L3_gnn_setup():
        import jax, jax.numpy as jnp
        import numpy as np
        N_NODES = 3125
        N_EDGES = 18750
        EMBED = 128
        N_LAYERS = 3
        key = jax.random.key(seed)
        k1, k2, k3 = jax.random.split(key, 3)
        embeddings = jax.random.normal(k1, (N_NODES, EMBED), dtype=jnp.float32)
        edge_index = jax.random.randint(k2, (2, N_EDGES), 0, N_NODES, dtype=jnp.int64)
        W = jax.random.normal(k3, (N_LAYERS, EMBED, EMBED), dtype=jnp.float32) / np.sqrt(EMBED)
        b = jnp.zeros((N_LAYERS, EMBED), dtype=jnp.float32)
        return {'embeddings': embeddings, 'edge_index': edge_index, 'W': W, 'b': b}
    _L3_gnn_all = _L3_gnn_setup()
    _L3_gnn_in = {k: v for k, v in _L3_gnn_all.items() if k in ('W', 'b')}
    del _L3_gnn_all
    return {'x': x, 'src': src, 'dst': dst, 'edge_attr_70': edge_attr_70, 'edge_weight': edge_weight, 'L0_gnn_W_self0': _L0_gnn_in['W_self0'], 'L0_gnn_W_neigh0': _L0_gnn_in['W_neigh0'], 'L0_gnn_b0': _L0_gnn_in['b0'], 'L0_gnn_W_self1': _L0_gnn_in['W_self1'], 'L0_gnn_W_neigh1': _L0_gnn_in['W_neigh1'], 'L0_gnn_b1': _L0_gnn_in['b1'], 'L1_gnn_Wf': _L1_gnn_in['Wf'], 'L1_gnn_bf': _L1_gnn_in['bf'], 'L1_gnn_Wq': _L1_gnn_in['Wq'], 'L1_gnn_Wk': _L1_gnn_in['Wk'], 'L1_gnn_Wa': _L1_gnn_in['Wa'], 'L1_gnn_Wu': _L1_gnn_in['Wu'], 'L1_gnn_bu': _L1_gnn_in['bu'], 'L2_gnn_W': _L2_gnn_in['W'], 'L2_gnn_b': _L2_gnn_in['b'], 'L2_gnn_bn_gamma': _L2_gnn_in['bn_gamma'], 'L2_gnn_bn_beta': _L2_gnn_in['bn_beta'], 'L2_gnn_ln_gamma': _L2_gnn_in['ln_gamma'], 'L2_gnn_ln_beta': _L2_gnn_in['ln_beta'], 'L3_gnn_W': _L3_gnn_in['W'], 'L3_gnn_b': _L3_gnn_in['b']}

def reference(x, src, dst, edge_attr_70, edge_weight, L0_gnn_W_self0, L0_gnn_W_neigh0, L0_gnn_b0, L0_gnn_W_self1, L0_gnn_W_neigh1, L0_gnn_b1, L1_gnn_Wf, L1_gnn_bf, L1_gnn_Wq, L1_gnn_Wk, L1_gnn_Wa, L1_gnn_Wu, L1_gnn_bu, L2_gnn_W, L2_gnn_b, L2_gnn_bn_gamma, L2_gnn_bn_beta, L2_gnn_ln_gamma, L2_gnn_ln_beta, L3_gnn_W, L3_gnn_b):
    import jax
    import jax.numpy as jnp

    def _L0_gnn_ref(h, src, dst, W_self0, W_neigh0, b0, W_self1, W_neigh1, b1):
        import jax, jax.numpy as jnp
        import numpy as np
        N_NODES = 50000
        D = 128
        N_EDGES = 25000

        def _sage_layer(h, src, dst, W_self, W_neigh, b):
            msgs = jnp.take(h, src, axis=0)
            agg = jax.ops.segment_sum(msgs, dst, num_segments=N_NODES)
            deg = jax.ops.segment_sum(jnp.ones((src.shape[0],), h.dtype), dst, num_segments=N_NODES)
            h_neigh = agg / jnp.maximum(deg, 1.0)[:, None]
            return h @ W_self + h_neigh @ W_neigh + b
        x = _sage_layer(h, src, dst, W_self0, W_neigh0, b0)
        x = jax.nn.relu(x)
        x = _sage_layer(x, src, dst, W_self1, W_neigh1, b1)
        return x

    def _L1_gnn_ref(x, edge_index, edge_attr, Wf, bf, Wq, Wk, Wa, Wu, bu):
        import jax, jax.numpy as jnp
        import numpy as np
        N_NODES = 50000
        IN_C = 128
        OUT_C = 128
        EDGE_F = 65
        N_EDGES = 25000
        EDGE_ATTR_COLS = 70
        src = edge_index[0]
        tgt = edge_index[1]
        ni = x[src]
        nj = x[tgt]
        mask = (edge_attr[:, 0:1] < 8).astype(x.dtype)
        fcat = jnp.concatenate([ni, nj, ni - nj, edge_attr[:, :EDGE_F]], axis=1)
        f = jax.nn.elu(fcat @ Wf + bf) * mask
        scale = IN_C ** (-0.5)
        q = ni @ Wq
        k = f @ Wk
        a = jnp.tanh(q * k * scale @ Wa)
        numerator = jnp.exp(a)
        a_sum = jax.ops.segment_sum(a, src, num_segments=N_NODES)
        denominator = jnp.exp(a_sum)[src]
        s = numerator / denominator
        z = s * f
        aggr = jax.ops.segment_sum(z, src, num_segments=N_NODES)
        return (x + aggr) @ Wu + bu

    def _L2_gnn_ref(x, edge_index, edge_weight, W, b, bn_gamma, bn_beta, ln_gamma, ln_beta):
        import jax, jax.numpy as jnp
        import numpy as np
        N = 50000
        E = 25000
        NFEAT = 128
        NOUT = 128
        EPS = 1e-05
        n = x.shape[0]
        row, col = (edge_index[0], edge_index[1])
        loop = jnp.arange(n)
        row = jnp.concatenate([row, loop])
        col = jnp.concatenate([col, loop])
        ew = jnp.concatenate([edge_weight, jnp.ones((n,), x.dtype)])
        deg = jax.ops.segment_sum(ew, col, num_segments=n)
        dinv = jnp.where(deg > 0, jax.lax.rsqrt(deg), 0.0)
        norm = dinv[row] * ew * dinv[col]
        h = x @ W
        msg = h[row] * norm[:, None]
        out = jax.ops.segment_sum(msg, col, num_segments=n) + b
        out = jax.nn.elu(out)
        mu = out.mean(axis=0)
        var = out.var(axis=0)
        out = (out - mu) * jax.lax.rsqrt(var + EPS) * bn_gamma + bn_beta
        m = out.mean(axis=-1, keepdims=True)
        v = out.var(axis=-1, keepdims=True)
        out = (out - m) * jax.lax.rsqrt(v + EPS) * ln_gamma + ln_beta
        return out

    def _L3_gnn_ref(embeddings, edge_index, W, b):
        import jax, jax.numpy as jnp
        import numpy as np
        N_NODES = 3125
        N_EDGES = 18750
        EMBED = 128
        N_LAYERS = 3
        "Stack of GCNConv layers (PyG semantics): x' = D^{-1/2}(A+I)D^{-1/2} x W + b."
        n = embeddings.shape[0]
        loops = jnp.arange(n, dtype=edge_index.dtype)
        src = jnp.concatenate([edge_index[0], loops])
        dst = jnp.concatenate([edge_index[1], loops])
        deg = jax.ops.segment_sum(jnp.ones_like(dst, dtype=embeddings.dtype), dst, num_segments=n)
        deg_inv_sqrt = jnp.where(deg > 0, jax.lax.rsqrt(deg), 0.0)
        norm = deg_inv_sqrt[src] * deg_inv_sqrt[dst]
        x = embeddings
        for l in range(W.shape[0]):
            h = x @ W[l]
            msgs = h[src] * norm[:, None]
            x = jax.ops.segment_sum(msgs, dst, num_segments=n) + b[l]
        return x
    edge_index = jnp.stack([src, dst])
    h = jnp.maximum(_layernorm(x, axis=-1), 0.0)
    x = x + _L0_gnn_ref(h, src, dst, L0_gnn_W_self0, L0_gnn_W_neigh0, L0_gnn_b0, L0_gnn_W_self1, L0_gnn_W_neigh1, L0_gnn_b1)
    h = jnp.maximum(_layernorm(x, axis=-1), 0.0)
    x = x + _L1_gnn_ref(h, edge_index, edge_attr_70, L1_gnn_Wf, L1_gnn_bf, L1_gnn_Wq, L1_gnn_Wk, L1_gnn_Wa, L1_gnn_Wu, L1_gnn_bu)
    h = jnp.maximum(_layernorm(x, axis=-1), 0.0)
    x = x + _L2_gnn_ref(h, edge_index, edge_weight, L2_gnn_W, L2_gnn_b, L2_gnn_bn_gamma, L2_gnn_bn_beta, L2_gnn_ln_gamma, L2_gnn_ln_beta)
    h = jnp.maximum(_layernorm(x, axis=-1), 0.0)
    x = x + _L3_gnn_ref(h, edge_index, L3_gnn_W, L3_gnn_b)
    return x

_drawn_inputs = setup_inputs


def setup_inputs(seed=0):
    import zlib

    import numpy as np

    out = dict(_drawn_inputs(seed))
    spreads = {'L0_gnn_b0': (0.0, 0.1),
     'L0_gnn_b1': (0.0, 0.1),
     'L1_gnn_bf': (0.0, 0.1),
     'L1_gnn_bu': (0.0, 0.1),
     'L2_gnn_b': (0.0, 0.671),
     'L2_gnn_bn_gamma': (1.0, 0.2),
     'L2_gnn_bn_beta': (0.0, 0.1),
     'L2_gnn_ln_gamma': (1.0, 0.2),
     'L2_gnn_ln_beta': (0.0, 0.1),
     'L3_gnn_b': (0.0, 0.1)}
    factors = {}
    for name, (base, spread) in spreads.items():
        noise = np.random.default_rng([zlib.crc32(name.encode()), seed]).standard_normal(out[name].shape)
        drawn = base * np.exp(spread * noise) if base else spread * noise
        out[name] = jnp.asarray(drawn.astype(out[name].dtype))
    for name, factor in factors.items():
        out[name] = (out[name] * factor).astype(out[name].dtype)
    return out
```

```python
from contextlib import ExitStack

import concourse.bass as bass
from concourse import mybir

F32 = mybir.dt.float32
BF16 = mybir.dt.bfloat16
F16 = mybir.dt.float16
I32 = mybir.dt.int32
ALU = mybir.AluOpType
ACT = mybir.ActivationFunctionType
AX = mybir.AxisListType

P = 128
N_REAL = 50000
D = 128
TILES = 392
NP = TILES * P
STEPS = 2 * TILES
GT = 4
GROUPS = TILES // GT
RING = 7
SPARE = 16
HALF = 4
REGION = 8
SPT = 16
SLOTS = RING * GT
LANDING = 2
EA = 70
EF = 65
ZW = 130
EPS = 1e-5
WARM = 16
CHUNKS = [(c * P, min(P, TILES - c * P)) for c in range((TILES + P - 1) // P)]


class Signal:

    def __init__(self, handle, base=WARM):
        self.sem, self.base = handle, base

    def at(self, n):
        return n + self.base

    def advance(self, n):
        self.base += n


class Chain:

    def __init__(self, signal, eng, rounds=0, per_round=0):
        self.counter, self.eng, self.start, self.n = signal, eng, rounds * per_round, 0

    def mark(self, ins):
        ins.then_inc(self.counter.sem, 1)
        self.n += 1
        return self.counter.at(self.start + self.n)

    def wait(self, value=None):
        self.eng.wait_ge(self.counter.sem, self.counter.at(self.start + self.n) if value is None else value)


class Signals:

    def __init__(self, make):
        self.all = []

        def sig(name):
            self.all.append(make(name))
            return self.all[-1]
        self.tiles_ready = sig("tiles_ready")
        self.idx_staged = sig("idx_staged")
        self.cols_staged = sig("cols_staged")
        self.onehot_ready = sig("onehot_ready")
        self.step_done = sig("step_done")
        self.acc_done = sig("acc_done")
        self.in_t = sig("in_t")
        self.in_copied = sig("in_copied")
        self.mm_done = sig("mm_done")
        self.mm_read = sig("mm_read")
        self.mm2_done = sig("mm2_done")
        self.out_ready = sig("out_ready")
        self.x_ready = sig("x_ready")
        self.h_ready = sig("h_ready")
        self.h_t = sig("h_t")
        self.h_copied = sig("h_copied")
        self.part_ready = sig("part_ready")
        self.mask_ready = sig("mask_ready")
        self.exp_ready = sig("exp_ready")
        self.f_ready = sig("f_ready")
        self.k_ready = sig("k_ready")
        self.q_ready = sig("q_ready")
        self.prod_ready = sig("prod_ready")
        self.u_ready = sig("u_ready")
        self.um_ready = sig("um_ready")
        self.a_ready = sig("a_ready")
        self.g_ready = sig("g_ready")
        self.z_ready = sig("z_ready")
        self.first_add = sig("first_add")
        self.second_add = sig("second_add")


class Program:
    pass


def rows(ap, first, tiles):
    return ap[bass.ds(first * P, tiles * P), :].rearrange("(t p) d -> p t d", p=P)


def setup(k, ctx):
    nc = k.nc

    def sb(name, shape, dt=F32):
        return ctx.enter_context(nc.sbuf_tensor(name, shape, dt))

    def sig(name, base=WARM):
        return Signal(ctx.enter_context(nc.semaphore(name)), base)

    def dram(name, shape, dt=F32):
        return nc.dram_tensor(name, shape, dt, kind="Internal").ap()

    k.ps = ctx.enter_context(nc.psum_tensor("ps", [P, 8, 512], F32))
    k.ident = sb("ident", [P, P])
    k.iota = sb("iota", [P, P])
    k.w = {n: sb("w_" + n, [P, P]) for n in
           ("self0", "neigh0", "self1", "neigh1", "ni", "nj", "ea", "q", "k", "u", "gcn", "g0", "g1", "g2")}
    k.wf_diff = sb("wf_diff", [P, P])
    k.wa = sb("w_a", [P, 1])
    k.bf = sb("b_f", [P, 1])
    k.b = {n: sb("b_" + n, [P, GT, D]) for n in
           ("b0", "b1", "u", "gcn", "ln_g", "ln_b", "g0", "g1", "g2", "bn_a", "bn_b")}
    k.bn_rows = sb("bn_rows", [1, 2, D])
    k.eps = sb("eps", [P, 1])
    k.rel = {o: sb("rel_" + o, [P, STEPS + SPT]) for o in ("dst", "src")}
    k.keep = {o: sb("keep_" + o, [P, STEPS + SPT]) for o in ("dst", "src")}
    k.weight = sb("weight_dst", [P, STEPS + SPT])
    k.idx = {o: sb("idx_" + o, [P, TILES + SLOTS], I32) for o in ("dst", "src")}
    k.edge_src = sb("edge_src", [P, TILES], I32)
    k.edge_dst = sb("edge_dst", [P, TILES], I32)
    k.ctl_slot = {o: sb("ctl_slot_" + o, [1, STEPS], I32) for o in ("dst", "src")}
    k.ctl_out = {o: sb("ctl_out_" + o, [1, 2, STEPS // 2], I32) for o in ("dst", "src")}
    k.ctl_ready = {o: sb("ctl_ready_" + o, [1, STEPS // REGION], I32) for o in ("dst", "src")}
    k.ctl_free = {o: sb("ctl_free_" + o, [1, GROUPS], I32) for o in ("dst", "src")}
    k.mean_scale = sb("mean_scale", [P, TILES])
    k.dinv_w = sb("dinv_w", [P, TILES])
    k.dinv_c = sb("dinv_c", [P, TILES])

    k.table = [dram(f"table{n}", [NP, D]) for n in range(2)]
    k.agg = dram("agg", [NP + SPARE * P, D])
    k.agg_src = dram("agg_src", [NP + SPARE * P, ZW])
    k.z = dram("z", [NP, ZW])
    k.res = [dram(f"residual{n}", [NP, D]) for n in range(2)]
    k.elu_out = dram("elu_out", [NP, D])
    k.rec = {"dst": dram("rec_dst", [NP, 4]), "src": dram("rec_src", [NP, 2])}
    k.last_step_dram = dram("last_step", [2, 512])

    k.sp_dma = [sig(f"sp_dma{n}", 0) for n in range(8)]
    k.pool_dma = [sig(f"pool_dma{n}", 0) for n in range(8)]
    k.sp_store = [sig(f"sp_store{n}", 0) for n in range(SPT // HALF)]
    k.act_store = [sig(f"act_store{n}", 0) for n in range(SPT // HALF)]
    k.dve_chain = sig("dve_chain")
    k.pool_pass, k.dve_pass, k.sp_pass = (ctx.enter_context(nc.semaphore(n)) for n in
                                          ("pool_pass", "dve_pass", "sp_pass"))
    k.s = Signals(sig)
    k.norm_signals = [[sig(f"{name}{n}") for n in range(2)] for name in
                      ("bn_ready", "stat_ready", "root_ready", "inverse_ready", "factors_ready")]
    return k


def constants_and_loads(k, ins):
    nc, s = k.nc, k.s
    wf = ins["L1_gnn_Wf"]
    loads = [(k.w["self0"][:, :], ins["L0_gnn_W_self0"]), (k.w["neigh0"][:, :], ins["L0_gnn_W_neigh0"]),
             (k.w["self1"][:, :], ins["L0_gnn_W_self1"]), (k.w["neigh1"][:, :], ins["L0_gnn_W_neigh1"]),
             (k.w["ni"][:, :], wf[0:P, :]), (k.w["nj"][:, :], wf[P:2 * P, :]),
             (k.wf_diff[:, :], wf[2 * P:3 * P, :]), (k.w["ea"][0:EF, :], wf[3 * P:3 * P + EF, :]),
             (k.w["q"][:, :], ins["L1_gnn_Wq"]), (k.w["k"][:, :], ins["L1_gnn_Wk"]),
             (k.w["u"][:, :], ins["L1_gnn_Wu"]), (k.w["gcn"][:, :], ins["L2_gnn_W"]),
             (k.w["g0"][:, :], ins["L3_gnn_W"][0]), (k.w["g1"][:, :], ins["L3_gnn_W"][1]),
             (k.w["g2"][:, :], ins["L3_gnn_W"][2]), (k.wa[:, :], ins["L1_gnn_Wa"]),
             (k.bf[:, :], ins["L1_gnn_bf"].rearrange("(d a) -> d a", a=1)),
             (k.bn_rows[:, 0, :], ins["L2_gnn_bn_gamma"].rearrange("(a d) -> a d", a=1)),
             (k.bn_rows[:, 1, :], ins["L2_gnn_bn_beta"].rearrange("(a d) -> a d", a=1))]
    biases = {"b0": ins["L0_gnn_b0"], "b1": ins["L0_gnn_b1"], "u": ins["L1_gnn_bu"], "gcn": ins["L2_gnn_b"],
              "ln_g": ins["L2_gnn_ln_gamma"], "ln_b": ins["L2_gnn_ln_beta"],
              "g0": ins["L3_gnn_b"][0], "g1": ins["L3_gnn_b"][1], "g2": ins["L3_gnn_b"][2]}
    for name, b in biases.items():
        loads.append((k.b[name][:, 0, :], b.partition_broadcast(P)))
    sp_loads = loads[len(k.act_store):]
    sp_signals = k.sp_store + [k.sp_dma[n % 8] for n in range(len(sp_loads) - len(k.sp_store))]
    for signal in k.act_store + sp_signals:
        signal.advance(16)
    with ExitStack() as ctx:
        lane_i = ctx.enter_context(nc.sbuf_tensor("lane_i", [P, P], I32))
        diff_i = ctx.enter_context(nc.sbuf_tensor("diff_i", [P, P], I32))
        made = ctx.enter_context(nc.semaphore("consts_made"))
        block = ctx.enter_context(nc.Block())

        @block.sync
        def _(sp):
            for signal, (to, of) in zip(sp_signals, sp_loads):
                sp.dma_start(to, of).then_inc(signal.sem, 16)
            for signal in k.sp_store + k.sp_dma:
                sp.wait_ge(signal.sem, signal.base)

        @block.scalar
        def _(act):
            for signal, (to, of) in zip(k.act_store, loads):
                act.dma_start(to, of).then_inc(signal.sem, 16)
            for signal in k.act_store:
                act.wait_ge(signal.sem, signal.base)

        @block.gpsimd
        def _(pool):
            pool.iota(lane_i[:, :], pattern=[[1, P]], base=0, channel_multiplier=0).then_inc(made, 1)
            pool.iota(diff_i[:, :], pattern=[[1, P]], base=0, channel_multiplier=-1).then_inc(made, 1)
            for n in range(8):
                pool.dma_start(k.z[n * P:(n + 1) * P, 0:D], ins["x"][0:P, :]).then_inc(k.pool_dma[n].sem, 16)
                k.pool_dma[n].base = 16
            for n in range(8):
                pool.wait_ge(k.pool_dma[n].sem, 16)
            both = [signal for pair in k.norm_signals for signal in pair]
            for signal in k.s.all + both + [k.dve_chain]:
                pool.sem_inc(signal.sem, WARM)

        @block.vector
        def _(dve):
            dve.wait_ge(made, 2)
            dve.tensor_copy(k.iota[:, :], lane_i[:, :])
            dve.tensor_scalar(k.ident[:, :], diff_i[:, :], 0.0, None, ALU.is_equal)
            dve.memset(k.eps[:, :], EPS)
            for n in range(8):
                dve.wait_ge(k.sp_dma[n].sem, k.sp_dma[n].base)
            for signal in k.sp_store + k.act_store:
                dve.wait_ge(signal.sem, signal.base)
            for name in biases:
                for t in range(1, GT):
                    dve.tensor_copy(k.b[name][:, t, :], k.b[name][:, 0, :])
            dve.tensor_tensor(k.w["ni"][:, :], k.w["ni"][:, :], k.wf_diff[:, :], ALU.add)
            dve.tensor_tensor(k.w["nj"][:, :], k.w["nj"][:, :], k.wf_diff[:, :], ALU.subtract)


def prepare(k, ins):
    with ExitStack() as ctx:
        starts = {o: ctx.enter_context(k.nc.sbuf_tensor("starts_" + o, [P, TILES + 1], F32))
                  for o in ("src", "dst")}
        order_edges(k, ins, starts)
        for n, o in enumerate(("src", "dst")):
            plan_steps(k, n, o, starts[o])


def order_edges(k, ins, starts):
    nc, s = k.nc, k.s
    keys = ("src", "dst")
    with ExitStack() as ctx:
        def sb(name, shape, dt=F32):
            return ctx.enter_context(nc.sbuf_tensor(name, shape, dt))

        def sem(name):
            return ctx.enter_context(nc.semaphore(name))

        node_i = {"src": k.edge_src, "dst": k.edge_dst}
        tile_i = {o: sb(f"tile_i_{o}", [P, TILES], I32) for o in keys}
        tile_f = {o: sb(f"tile_f_{o}", [P, TILES]) for o in keys}
        lane_i = sb("lane_dst_i", [P, TILES], I32)
        lane_f = sb("lane_dst_f", [P, TILES])
        ew = sb("ew", [P, TILES])
        part_b = sb("part_b", [P, TILES], BF16)
        ew_part = [sb(f"ew_part{n}", [P, TILES]) for n in range(3)]
        rest = [sb(f"ew_rest{n}", [P, TILES]) for n in range(2)]
        bins_i = sb("bins_i", [P, TILES + 1], I32)
        edge_i = sb("edge_i", [P, TILES], I32)
        bins = sb("bins", [P, TILES + 1], F16)
        lanes = sb("lanes", [P, P], F16)
        tri_i = sb("tri_i", [P, P], I32)
        before = sb("before", [P, P], BF16)
        from_on = sb("from_on", [P, P], BF16)
        ones = sb("ones_b", [P, P], BF16)
        above = sb("above", [P, 4, TILES + 1], BF16)
        onehot = sb("onehot_tile", [P, 2, 2, TILES], BF16)
        lane_hot = sb("lane_hot", [P, 2, 4, P], BF16)
        products = sb("products", [P, 2, GT, TILES], BF16)
        rec = {"dst": sb("recs_dst", [P, TILES, 4]), "src": sb("recs_src", [P, TILES, 2])}
        pos = sb("pos", [P, 2, 2, GT])
        pos_i = sb("pos_i", [P, 2, 2, GT], I32)
        pos_t = sb("pos_t", [P, 2, 2, GT], I32)
        pos_l = sb("pos_l", [P, 2, 2, GT], I32)
        place = sb("place", [P, 2, 2, GT], I32)
        staged = {"dst": sb("staged_dst", [P, 2, GT, 4]), "src": sb("staged_src", [P, 2, GT, 2])}
        iotas, loaded, prepared = sem("iotas"), sem("loaded"), sem("prepared")
        above_ready, counted, starts_read = sem("above_ready"), sem("counted"), sem("starts_read")
        count_ps = {"src": k.ps[:, 0, 0:TILES + 1], "dst": k.ps[:, 1, 0:TILES + 1]}
        deg_ps = [k.ps[:, 2, 0:TILES], k.ps[:, 3, 0:TILES]]
        dve_per = 0
        with nc.Block() as block:
            @block.sync
            def _(sp):
                sp.dma_start(k.edge_src[:, :], ins["src"].rearrange("(p t) -> p t", p=P)).then_inc(loaded, 16)
                sp.dma_start(k.edge_dst[:, :], ins["dst"].rearrange("(p t) -> p t", p=P)).then_inc(loaded, 16)
                sp.dma_start(ew[:, :], ins["edge_weight"].rearrange("(p t) -> p t", p=P)).then_inc(loaded, 16)
                sp.wait_ge(loaded, 48)

            @block.gpsimd
            def _(pool):
                pool.iota(bins_i[:, :], pattern=[[1, TILES + 1]], base=0, channel_multiplier=0).then_inc(iotas, 1)
                pool.iota(tri_i[:, :], pattern=[[1, P]], base=0, channel_multiplier=-1).then_inc(iotas, 1)
                pool.iota(edge_i[:, :], pattern=[[1, TILES]], base=0, channel_multiplier=TILES).then_inc(iotas, 1)

            @block.vector
            def _(dve):
                c = Chain(k.dve_chain, dve)
                dve.wait_ge(iotas, 3)
                dve.tensor_copy(bins[:, :], bins_i[:, :])
                dve.tensor_copy(lanes[:, :], bins_i[:, 0:P])
                dve.tensor_scalar(before[:, :], tri_i[:, :], 0.0, None, ALU.is_gt)
                dve.tensor_scalar(from_on[:, :], tri_i[:, :], 0.0, None, ALU.is_le)
                dve.memset(ones[:, :], 1.0)
                dve.tensor_copy(rec["src"][:, :, 1], edge_i[:, :])
                dve.memset(rec["dst"][:, :, 3], 0.0)
                dve.wait_ge(loaded, 48)
                for o in keys:
                    dve.tensor_scalar(tile_i[o][:, :], node_i[o][:, :], 7, None, ALU.arith_shift_right)
                dve.tensor_scalar(lane_i[:, :], node_i["dst"][:, :], 127, None, ALU.bitwise_and)
                dve.tensor_copy(rec["src"][:, :, 0], node_i["src"][:, :])
                dve.tensor_copy(rec["dst"][:, :, 0], node_i["dst"][:, :])
                dve.tensor_copy(rec["dst"][:, :, 1], node_i["src"][:, :])
                c.mark(dve.tensor_copy(rec["dst"][:, :, 2], ew[:, :]))
                c.mark(dve.tensor_copy(part_b[:, :], ew[:, :]))
                c.wait()
                for o in keys:
                    dve.tensor_copy(tile_f[o][:, :], tile_i[o][:, :])
                dve.tensor_copy(lane_f[:, :], lane_i[:, :])
                c.mark(dve.tensor_copy(ew_part[0][:, :], part_b[:, :]))
                c.wait()
                c.mark(dve.tensor_tensor(rest[0][:, :], ew[:, :], ew_part[0][:, :], ALU.subtract))
                c.wait()
                c.mark(dve.tensor_copy(part_b[:, :], rest[0][:, :]))
                c.wait()
                c.mark(dve.tensor_copy(ew_part[1][:, :], part_b[:, :]))
                c.wait()
                c.mark(dve.tensor_tensor(rest[1][:, :], rest[0][:, :], ew_part[1][:, :], ALU.subtract))
                c.wait()
                c.mark(dve.tensor_copy(part_b[:, :], rest[1][:, :]))
                c.wait()
                ins_ = c.mark(dve.tensor_copy(ew_part[2][:, :], part_b[:, :]))
                c.wait()
                dve.sem_inc(prepared, 1)
                k.dve_chain.advance(c.n)

        with nc.Block() as block:
            @block.vector
            def _(dve):
                with dve.Fori(0, TILES // 2) as it:
                    for n in range(4):
                        o, t = keys[n % 2], it * 2 + n // 2
                        dve.wait_ge(s.step_done.sem, s.step_done.at(it * 4 + n - 3))
                        dve.tensor_scalar(above[:, n, :], bins[:, :], tile_f[o][:, bass.ds(t, 1)], None,
                                          ALU.is_gt).then_inc(s.onehot_ready.sem, 1)
                for n, o in enumerate(keys):
                    dve.wait_ge(s.step_done.sem, s.step_done.at(2 * TILES))
                    dve.tensor_copy(starts[o][:, :], count_ps[o])

            @block.tensor
            def _(pe):
                def count(it, n, first):
                    pe.wait_ge(s.onehot_ready.sem, s.onehot_ready.at(it * 4 + n + 1))
                    pe.matmul(count_ps[keys[n % 2]], ones[:, :], above[:, n, :], start=first, stop=True,
                              skip_group_check=True).then_inc(s.step_done.sem, 1)
                for n in range(4):
                    count(0, n, n < 2)
                with pe.Fori(1, TILES // 2) as it:
                    for n in range(4):
                        count(it, n, False)
            s.step_done.advance(2 * TILES)
            s.onehot_ready.advance(2 * TILES)

        hot_ready, lane_ready, ranks_ready = s.onehot_ready, s.part_ready, s.mm_done
        ranked, counted2, pos_done = s.acc_done, s.step_done, s.mm2_done
        with nc.Block() as block:
            @block.vector
            def _(dve):
                per = 6
                with dve.Fori(0, GROUPS // 2) as it:
                    for half in range(2):
                        g = it * 2 + half
                        c = Chain(k.dve_chain, dve, g, per)
                        for q in range(GT):
                            t, b = g * GT + q, q % 2
                            dve.wait_ge(counted2.sem, counted2.at(t - 1))
                            for n, o in enumerate(keys):
                                dve.tensor_scalar(onehot[:, b, n, :], bins[:, 0:TILES],
                                                  tile_f[o][:, bass.ds(t, 1)], None,
                                                  ALU.is_equal).then_inc(hot_ready.sem, 1)
                            dve.tensor_scalar(lane_hot[:, b, 0, :], lanes[:, :], lane_f[:, bass.ds(t, 1)], None,
                                              ALU.is_equal).then_inc(lane_ready.sem, 1)
                            for part in range(3):
                                dve.tensor_scalar(lane_hot[:, b, 1 + part, :], lanes[:, :],
                                                  lane_f[:, bass.ds(t, 1)], ew_part[part][:, bass.ds(t, 1)],
                                                  ALU.is_equal, ALU.mult).then_inc(lane_ready.sem, 1)
                            if q == 0:
                                dve.wait_ge(k.pool_dma[half].sem, k.pool_dma[half].at(it * 128))
                            for n, o in enumerate(keys):
                                dve.wait_ge(ranks_ready.sem, ranks_ready.at(t * 2 + n + 1))
                                ins_ = dve.tensor_tensor_reduce(
                                    products[:, n, q, :], onehot[:, b, n, :], count_ps[o][:, 0:TILES], 1.0, 0.0,
                                    ALU.mult, ALU.add, pos[:, half, n, q:q + 1])
                                ins_.then_inc(ranked.sem, 1)
                        dve.wait_ge(ranked.sem, ranked.at((g + 1) * GT * 2))
                        c.mark(dve.tensor_copy(pos_i[:, half, :, :], pos[:, half, :, :]))
                        c.wait()
                        c.mark(dve.tensor_scalar(pos_t[:, half, :, :], pos_i[:, half, :, :], 7, None,
                                                 ALU.arith_shift_right))
                        c.mark(dve.tensor_scalar(pos_l[:, half, :, :], pos_i[:, half, :, :], 127, None,
                                                 ALU.bitwise_and))
                        for o in keys:
                            c.mark(dve.tensor_copy(staged[o][:, half, :, :], rec[o][:, bass.ds(g * GT, GT), :]))
                        c.wait()
                        c.mark(dve.scalar_tensor_tensor(place[:, half, :, :], pos_l[:, half, :, :], float(TILES),
                                                        pos_t[:, half, :, :], ALU.mult, ALU.add))
                        assert c.n == per
                dve.wait_ge(counted2.sem, counted2.at(TILES))
                c = Chain(k.dve_chain, dve, GROUPS, per)
                c.mark(dve.tensor_scalar(k.mean_scale[:, :], deg_ps[0], 1.0, None, ALU.max))
                c.mark(dve.tensor_scalar(k.dinv_w[:, :], deg_ps[1], 1.0, None, ALU.add))
                c.mark(dve.tensor_scalar(k.dinv_c[:, :], deg_ps[0], 1.0, None, ALU.add))
                c.wait()
                dve.reciprocal(k.mean_scale[:, :], k.mean_scale[:, :])
                dve.reciprocal(k.dinv_w[:, :], k.dinv_w[:, :])
                c.mark(dve.reciprocal(k.dinv_c[:, :], k.dinv_c[:, :]))
                k.dve_end = k.dve_chain.at(GROUPS * per + c.n)
                k.dve_total = GROUPS * per + c.n

            @block.scalar
            def _(act):
                act.wait_ge(k.dve_chain.sem, k.dve_end)
                act.activation(k.dinv_w[:, :], k.dinv_w[:, :], ACT.Sqrt)
                act.activation(k.dinv_c[:, :], k.dinv_c[:, :], ACT.Sqrt)

            @block.tensor
            def _(pe):
                def tile(t, q, first):
                    b = q % 2
                    for n, o in enumerate(keys):
                        pe.wait_ge(hot_ready.sem, hot_ready.at(t * 2 + n + 1))
                        pe.matmul(count_ps[o][:, 0:TILES], before[:, :], onehot[:, b, n, :], start=False,
                                  stop=True, skip_group_check=True).then_inc(ranks_ready.sem, 1)
                    for part in range(4):
                        pe.wait_ge(lane_ready.sem, lane_ready.at(t * 4 + part + 1))
                        pe.matmul(deg_ps[min(part, 1)], lane_hot[:, b, part, :], onehot[:, b, 1, :],
                                  start=first and part < 2, stop=True, skip_group_check=True)
                    for n, o in enumerate(keys):
                        pe.wait_ge(ranked.sem, ranked.at(t * 2 + n + 1))
                        mm = pe.matmul(count_ps[o][:, 0:TILES], from_on[:, :], onehot[:, b, n, :], start=False,
                                       stop=True, skip_group_check=True)
                    mm.then_inc(counted2.sem, 1)
                for t in range(2):
                    tile(t, t, t == 0)
                with pe.Fori(1, TILES // 2) as it:
                    for q in range(2):
                        tile(it * 2 + q, q, False)

            @block.gpsimd
            def _(pool):
                with pool.Fori(0, GROUPS // 2) as it:
                    for half in range(2):
                        g = it * 2 + half
                        pool.wait_ge(k.dve_chain.sem, k.dve_chain.at(g * 6 + 6))
                        pool.sem_inc(k.pool_pass, 1)
                        for n, o in enumerate(keys):
                            for q in range(GT):
                                pool.indirect_dma_start(
                                    k.rec[o], bass.IndirectOffsetOnAxis(ap=place[:, half, n, q:q + 1], axis=0),
                                    staged[o][:, half, q, :], None).then_inc(k.pool_dma[half].sem, 16)
                for half in range(2):
                    pool.wait_ge(k.pool_dma[half].sem, k.pool_dma[half].at(128 * GROUPS // 2))
            for half in range(2):
                k.pool_dma[half].advance(128 * GROUPS // 2)
            k.dve_chain.advance(k.dve_total)
            hot_ready.advance(2 * TILES)
            lane_ready.advance(4 * TILES)
            ranks_ready.advance(2 * TILES)
            ranked.advance(2 * TILES)
            counted2.advance(TILES)


def plan_steps(k, number, o, starts):
    nc, s = k.nc, k.s
    with ExitStack() as ctx:
        def sb(name, shape, dt=F32):
            return ctx.enter_context(nc.sbuf_tensor(f"{name}_{o}", shape, dt))

        def sem(name):
            return ctx.enter_context(nc.semaphore(f"{name}_{o}"))

        width = 4 if o == "dst" else 2
        half = STEPS // 2
        recs = sb("sorted", [P, TILES, width])
        k_i, k_f = sb("k_i", [P, STEPS], I32), sb("k_f", [P, STEPS])
        thr_i = sb("thr_i", [P, 4], I32)
        thr = sb("thr", [P, 2, 4])
        junk = sb("junk_p", [P, TILES])
        last = sb("last", [P, 2, 4])
        index_i, index = sb("index_i", [P, 4], I32), sb("index", [P, 4])
        le = sb("le", [P, 4, STEPS])
        gt = sb("gt", [P, 4, STEPS])
        chosen = sb("chosen", [P, 4, STEPS])
        node_t = sb("node_t", [P, 4, P])
        w_t = sb("w_t", [P, 4, P])
        ones = sb("ones_f", [P, P])
        ik = sb("ik", [P, STEPS])
        jk = sb("jk", [P, STEPS])
        jk128 = sb("jk128", [P, STEPS])
        row = sb("row", [1, 6, STEPS])
        row_i = sb("row_i", [1, 3, STEPS], I32)
        ls_row = sb("ls_row", [1, 512])
        trash_i = sb("trash_i", [1, STEPS], I32)
        loaded, iotas, ready, transposed, copied = (sem(n) for n in ("recs", "iotas_p", "chosen_r", "trans", "copied"))
        summed, last_ready, last_out, last_in = (sem(n) for n in ("summed", "last_r", "last_out", "last_in"))
        cols = k.rel[o]
        values = [recs[:, :, 0]] + ([recs[:, :, 2]] if o == "dst" else [])
        with nc.Block() as block:
            @block.sync
            def _(sp):
                sp.dma_start(recs[:, :, :], k.rec[o].rearrange("(p t) c -> p t c", p=P)).then_inc(loaded, 16)
                sp.wait_ge(last_ready, 1)
                for c in range(4):
                    sp.dma_start(k.last_step_dram[number, c * P:(c + 1) * P].rearrange("(p a) -> p a", a=1),
                                 last[:, 0, c:c + 1]).then_inc(last_out, 16)
                sp.wait_ge(last_out, 64)
                sp.dma_start(ls_row[:, :], k.last_step_dram[number:number + 1, :]).then_inc(last_in, 16)
                sp.wait_ge(last_in, 16)
                sp.wait_ge(loaded, 16)

            @block.gpsimd
            def _(pool):
                pool.iota(k_i[:, :], pattern=[[1, STEPS]], base=0, channel_multiplier=0).then_inc(iotas, 1)
                pool.iota(thr_i[:, :], pattern=[[P * P, 4]], base=P - 1, channel_multiplier=P).then_inc(iotas, 1)
                pool.iota(index_i[:, :], pattern=[[P, 4]], base=0, channel_multiplier=1).then_inc(iotas, 1)
                pool.iota(trash_i[:, :], pattern=[[0, STEPS // SPARE], [1, SPARE]], base=TILES,
                          channel_multiplier=0).then_inc(iotas, 1)

            @block.vector
            def _(dve):
                c = Chain(k.dve_chain, dve)
                dve.wait_ge(iotas, 4)
                dve.tensor_copy(k_f[:, :], k_i[:, :])
                dve.tensor_copy(index[:, :], index_i[:, :])
                dve.memset(ones[:, :], 1.0)
                dve.memset(k.rel[o][:, STEPS:], -1.0)
                dve.memset(k.keep[o][:, STEPS:], 0.0)
                dve.memset(k.idx[o][:, TILES:], 0)
                if o == "dst":
                    dve.memset(k.weight[:, STEPS:], 0.0)
                c.mark(dve.tensor_copy(thr[:, 0, :], thr_i[:, :]))
                c.wait()
                c.mark(dve.tensor_scalar(thr[:, 1, :], thr[:, 0, :], -float(P), None, ALU.add))
                c.wait()
                for a in range(2):
                    for n in range(4):
                        c.mark(dve.tensor_scalar(junk[:, :], starts[:, 1:TILES + 1], thr[:, a, n:n + 1], 0.0,
                                                 ALU.is_le, ALU.add, accum_out=last[:, a, n:n + 1]))
                        c.wait()
                c.mark(dve.tensor_tensor(last[:, 0, :], last[:, 0, :], index[:, :], ALU.add))
                c.mark(dve.scalar_tensor_tensor(last[:, 1, :], last[:, 1, :], -1.0, index[:, :], ALU.add, ALU.add))
                c.wait()
                dve.sem_inc(last_ready, 1)
                for n, (_, size) in enumerate(CHUNKS):
                    dve.tensor_scalar(gt[:, n, :], k_f[:, :], last[:, 0, n:n + 1], None, ALU.is_gt)
                    c.mark(dve.tensor_scalar(le[:, n, :], k_f[:, :], last[:, 0, n:n + 1], None, ALU.is_le))
                    c.wait()
                    c.mark(dve.scalar_tensor_tensor(chosen[:, n, :], k_f[:, :], last[:, 1, n:n + 1], le[:, n, :],
                                                    ALU.is_gt, ALU.mult))
                c.wait()
                dve.sem_inc(ready, 1)
                dve.wait_ge(transposed, len(values))
                for v in range(len(values)):
                    for n, (_, size) in enumerate(CHUNKS):
                        to = (node_t, w_t)[v]
                        c.mark(dve.tensor_copy(to[0:size, n, :], k.ps[0:size, v, n * P:(n + 1) * P]))
                c.wait()
                dve.sem_inc(copied, 1)
                dve.wait_ge(summed, 1)
                for h in range(2):
                    c.mark(dve.tensor_copy(ik[:, h * half:(h + 1) * half], k.ps[:, 2 + h, 0:half]))
                c.wait()
                c.mark(dve.tensor_tensor(jk[:, :], k_f[:, :], ik[:, :], ALU.subtract))
                dve.memset(k.keep[o][:, 0:1], 0.0)
                dve.tensor_tensor(k.keep[o][:, 1:STEPS], ik[:, 1:], ik[:, 0:STEPS - 1], ALU.not_equal)
                dve.memset(row[:, 0, STEPS - 1:STEPS], 1.0)
                dve.tensor_tensor(row[:, 0, 0:STEPS - 1], ik[0:1, 1:], ik[0:1, 0:STEPS - 1], ALU.is_equal)
                dve.tensor_scalar(row[:, 1, :], ik[0:1, :], float(TILES - 1), None, ALU.min)
                c.mark(dve.tensor_copy(row[:, 2, :], trash_i[:, :]))
                c.wait()
                c.mark(dve.tensor_scalar(jk128[:, :], jk[:, :], float(P), None, ALU.mult))
                dve.tensor_tensor(row[:, 3, :], jk[0:1, :], row[:, 2, :], ALU.subtract)
                c.mark(dve.tensor_copy(row_i[:, 0, :], row[:, 1, :]))
                c.wait()
                for h in range(2):
                    cut = slice(h * half, (h + 1) * half)
                    dve.tensor_tensor(k.rel[o][:, cut], k.ps[:, 4 + h, 0:half], jk128[:, cut], ALU.subtract)
                    if o == "dst":
                        dve.tensor_copy(k.weight[:, cut], k.ps[:, 6 + h, 0:half])
                c.mark(dve.tensor_scalar(row_i[:, 2, :], row[:, 1, :], float(-(-65536 // SLOTS)), None, ALU.mult))
                c.wait()
                c.mark(dve.tensor_scalar(row_i[:, 2, :], row_i[:, 2, :], 16, None, ALU.arith_shift_right))
                c.wait()
                c.mark(dve.scalar_tensor_tensor(row_i[:, 2, :], row_i[:, 2, :], -float(SLOTS), row_i[:, 0, :],
                                                ALU.mult, ALU.add))
                c.wait()
                row_width = D if o == "dst" else ZW
                dve.tensor_scalar(k.ctl_slot[o][:, :], row_i[:, 2, :], float(row_width), None, ALU.mult)
                c.mark(dve.tensor_tensor(row[:, 4, :], row[:, 3, :], row[:, 0, :], ALU.mult))
                c.mark(dve.tensor_scalar(row_i[:, 1, :], row_i[:, 0, :], 2, None, ALU.arith_shift_right))
                c.wait()
                c.mark(dve.tensor_tensor(row[:, 5, :], row[:, 4, :], row[:, 2, :], ALU.add))
                dve.tensor_scalar(k.ctl_ready[o][:, :], row_i[:, 1, REGION - 1::REGION], 1.0 + LANDING, None,
                                  ALU.add)
                c.wait()
                for parity in range(2):
                    dve.tensor_scalar(k.ctl_out[o][:, parity, :], row[:, 5, parity::2], float(P), None, ALU.mult)
                dve.wait_ge(last_in, 16)
                lag = SLOTS // GT
                dve.memset(k.ctl_free[o][:, 0:lag], 0)
                dve.tensor_scalar(k.ctl_free[o][:, lag:], ls_row[:, GT - 1:(GROUPS - lag) * GT:GT], 1.0, None,
                                  ALU.add)
                dve.wait_ge(loaded, 16)
                dve.tensor_copy(k.idx[o][:, 0:TILES], recs[:, :, 1])
                k.dve_chain.advance(c.n)

            @block.tensor
            def _(pe):
                pe.wait_ge(loaded, 16)
                for v, value in enumerate(values):
                    for n, (first, size) in enumerate(CHUNKS):
                        mm = pe.transpose(k.ps[0:size, v, n * P:(n + 1) * P], value[:, first:first + size],
                                          k.ident[:, :])
                    mm.then_inc(transposed, 1)
                pe.wait_ge(ready, 1)
                pe.wait_ge(copied, 1)
                for h in range(2):
                    cut = slice(h * half, (h + 1) * half)
                    jobs = [(2, ones, gt), (4, node_t, chosen)] + ([(6, w_t, chosen)] if o == "dst" else [])
                    for bank, lhs, rhs in jobs:
                        for n, (_, size) in enumerate(CHUNKS):
                            l = ones[0:size, :] if lhs is ones else lhs[0:size, n, :]
                            mm = pe.matmul(k.ps[:, bank + h, 0:half], l, rhs[0:size, n, cut],
                                           start=(n == 0), stop=(n == len(CHUNKS) - 1))
                mm.then_inc(summed, 1)


def level(k, pool, signals):
    top = max(signal.base for signal in signals)
    for signal in signals:
        if signal.base < top:
            pool.sem_inc(signal.sem, top - signal.base)
            signal.base = top
    return top


def sum_over_nodes(k, o, table, width, out, weighted=False):
    nc, s = k.nc, k.s
    cols = D if width == D else D + 1
    turns = STEPS // SPT
    counted = (s.onehot_ready, s.step_done, s.acc_done)
    top = max(signal.base for signal in counted)
    with ExitStack() as ctx:
        def sb(name, shape, dt=F32):
            return ctx.enter_context(nc.sbuf_tensor(k.name(name), shape, dt))

        ring = sb("ring", [P, SLOTS * width])
        acc = sb("acc", [P, SPT, width])
        hot = sb("hot", [P, 2 * HALF, P])
        staged = sb("staged", [P, 2, SLOTS], I32)
        rel, keep = sb("rel_now", [P, SPT]), sb("keep_now", [P, SPT])
        weight = sb("weight_now", [P, SPT])
        block = ctx.enter_context(nc.Block())

        @block.gpsimd
        def _(pool):
            level(k, pool, counted)

            def stage(turn, b):
                pool.tensor_copy(staged[:, b, :], k.idx[o][:, bass.ds(turn * SLOTS, SLOTS)]
                                 ).then_inc(s.idx_staged.sem, 1)

            def announce(rounds, r):
                pool.wait_ge(k.pool_dma[r].sem, k.pool_dma[r].at(rounds * (GT * 16)))
                pool.sem_inc(s.tiles_ready.sem, 1)

            stage(0, 0)
            with pool.Fori(0, GROUPS // RING // 2) as pair:
                for b in range(2):
                    it = pair * 2 + b
                    for r in range(RING):
                        g = it * RING + r
                        free = pool.value_load(k.ctl_free[o][0:1, bass.ds(g, 1)], min_val=0, max_val=STEPS)
                        announce(it + (1 if r >= LANDING else 0), (r - LANDING) % RING)
                        if r == LANDING:
                            stage(it + 1, 1 - b)
                        if r == 0:
                            pool.wait_ge(s.idx_staged.sem, s.idx_staged.at(it + 1))
                            pool.sem_inc(k.pool_pass, 1)
                        pool.wait_ge(s.step_done.sem, s.step_done.at(free))
                        pool.sem_inc(k.pool_pass, 1)
                        for q in range(r * GT, (r + 1) * GT):
                            pool.indirect_dma_start(
                                ring[:, q * width:(q + 1) * width], None, table,
                                bass.IndirectOffsetOnAxis(ap=staged[:, b, q:q + 1], axis=0)
                            ).then_inc(k.pool_dma[r].sem, 16)
            for r in range(RING - LANDING, RING):
                announce(GROUPS // RING, r)

        @block.vector
        def _(dve):
            def onehots(half, staged_count, done):
                if staged_count is not None:
                    dve.wait_ge(s.cols_staged.sem, staged_count)
                dve.wait_ge(s.step_done.sem, done)
                for n in range(HALF):
                    q = (half * HALF + n) % SPT
                    scale = (weight[:, q:q + 1], ALU.mult) if weighted else (None, ALU.bypass)
                    dve.tensor_scalar(hot[:, q % (2 * HALF), :], k.iota[:, :], rel[:, q:q + 1], scale[0],
                                      ALU.is_equal, scale[1]).then_inc(s.onehot_ready.sem, 1)

            dve.memset(acc[:, SPT - 1, :], 0.0)
            onehots(0, s.cols_staged.at(1), top)
            with dve.Fori(0, turns) as it:
                now = dve.snap(it * SPT + top)
                count = [dve.snap(now + q) if q else now for q in range(SPT + 1)]
                regions = dve.snap(it * 2 + s.cols_staged.base)
                stored = dve.snap(it * (HALF // 2 * 16) + k.sp_store[0].base)
                for half in range(SPT // HALF):
                    region = {1: 2, 3: 3}.get(half)
                    onehots(half + 1, regions + region if region else None, count[half * HALF])
                    dve.wait_ge(k.sp_store[half].sem, stored)
                    dve.wait_ge(k.act_store[half].sem, stored)
                    for n in range(HALF):
                        q = half * HALF + n
                        dve.wait_ge(s.step_done.sem, count[q + 1])
                        dve.wait_ge(s.acc_done.sem, count[q])
                        dve.scalar_tensor_tensor(acc[:, q, 0:cols], acc[:, (q - 1) % SPT, 0:cols],
                                                 keep[:, q:q + 1], k.ps[:, q % 8, 0:cols],
                                                 ALU.mult, ALU.add).then_inc(s.acc_done.sem, 1)

        @block.tensor
        def _(pe):
            with pe.Fori(0, turns * 2) as m:
                now = pe.snap(m * REGION + top)
                need = pe.value_load(k.ctl_ready[o][0:1, bass.ds(m, 1)], min_val=1, max_val=GROUPS + LANDING)
                places = nc.values_load_multi_w_load_instructions(
                    k.ctl_slot[o][0:1, bass.ds(m * REGION, REGION)], engines=[pe.engine], min_val=0,
                    max_val=(SLOTS - 1) * width, skip_runtime_bounds_check_because="worked out by plan_steps")[1]
                pe.wait_ge(s.tiles_ready.sem, s.tiles_ready.at(need))
                for q in range(REGION):
                    if q % HALF == 0:
                        pe.wait_ge(s.onehot_ready.sem, now + (q + HALF))
                        pe.wait_ge(s.acc_done.sem, now + (q - HALF))
                    pe.matmul(k.ps[:, q, 0:cols], hot[:, q, :], ring[:, bass.ds(places[q], cols)],
                              start=True, stop=True).then_inc(s.step_done.sem, 1)

        @block.sync
        def _(sp):
            with sp.Fori(0, turns) as it:
                now = sp.snap(it * SPT + top)
                for region in range(2):
                    rows_to = nc.values_load_multi_w_load_instructions(
                        k.ctl_out[o][0:1, 0, bass.ds((it * 2 + region) * HALF, HALF)], engines=[sp.engine],
                        min_val=0, max_val=NP + SPARE * P - P, skip_runtime_bounds_check_because="worked out by plan_steps")[1]
                    for n, to in enumerate(rows_to):
                        q = region * REGION + 2 * n
                        sp.wait_ge(s.acc_done.sem, now + (q + 1))
                        sp.sem_inc(k.sp_pass, 1)
                        sp.dma_start(out[bass.ds(to, P), 0:cols], acc[:, q, 0:cols]
                                     ).then_inc(k.sp_store[q // HALF].sem, 16)
            for half in range(SPT // HALF):
                sp.wait_ge(k.sp_store[half].sem, k.sp_store[half].at(turns * (HALF // 2 * 16)))

        @block.scalar
        def _(act):
            def stage_columns(step, region):
                cut = slice(region * REGION, (region + 1) * REGION)
                act.copy(rel[:, cut], k.rel[o][:, bass.ds(step, REGION)])
                if weighted:
                    act.copy(weight[:, cut], k.weight[:, bass.ds(step, REGION)])
                act.copy(keep[:, cut], k.keep[o][:, bass.ds(step, REGION)]).then_inc(s.cols_staged.sem, 1)

            for region in range(2):
                stage_columns(region * REGION, region)
            with act.Fori(0, turns) as it:
                now = act.snap(it * SPT + top)
                for region in range(2):
                    rows_to = nc.values_load_multi_w_load_instructions(
                        k.ctl_out[o][0:1, 1, bass.ds((it * 2 + region) * HALF, HALF)], engines=[act.engine],
                        min_val=0, max_val=NP + SPARE * P - P, skip_runtime_bounds_check_because="worked out by plan_steps")[1]
                    for n, to in enumerate(rows_to):
                        q = region * REGION + 2 * n + 1
                        act.wait_ge(s.acc_done.sem, now + (q + 1))
                        act.dma_start(out[bass.ds(to, P), 0:cols], acc[:, q, 0:cols]
                                      ).then_inc(k.act_store[q // HALF].sem, 16)
                    stage_columns((it + 1) * SPT + region * REGION, region)
            for half in range(SPT // HALF):
                act.wait_ge(k.act_store[half].sem, k.act_store[half].at(turns * (HALF // 2 * 16)))

        for r in range(RING):
            k.pool_dma[r].advance(GT * 16 * (GROUPS // RING))
        for half in range(SPT // HALF):
            k.sp_store[half].advance(turns * (HALF // 2 * 16))
            k.act_store[half].advance(turns * (HALF // 2 * 16))
        s.idx_staged.advance(GROUPS // RING + 1)
        s.cols_staged.advance(2 * turns + 2)
        s.tiles_ready.advance(GROUPS + LANDING)
        s.onehot_ready.advance(STEPS + HALF)
        s.step_done.advance(STEPS)
        s.acc_done.advance(STEPS)


def by_groups(eng, *parts):
    def turn(it, r, groups=None):
        for p, part in enumerate(parts):
            g, slot, rnd = it * RING + (r - p), (r - p) % RING, it - (1 if r < p else 0)
            if groups is None or 0 <= g < groups:
                part(g, slot, rnd)
    for r in range(RING):
        turn(0, r, GROUPS)
    with eng.Fori(1, GROUPS // RING) as it:
        for r in range(RING):
            turn(it, r)
    for r in range(len(parts) - 1):
        turn(GROUPS // RING, r, GROUPS)


def node_pass(k, loads, stores, engines, tallies):
    nc, s = k.nc, k.s
    with nc.Block() as block:
        @block.sync
        def _(sp):
            def body(g, r, it):
                sp.wait_ge(k.pool_dma[r].sem, k.pool_dma[r].at(it * (16 * len(stores))))
                sp.sem_inc(k.sp_pass, 1)
                for buf, table, *cols in loads:
                    c = cols[0] if cols else D
                    sp.dma_start(buf[:, r, :, 0:c], rows(table, g * GT, GT)[:, :, 0:c]
                                 ).then_inc(k.sp_dma[r].sem, 16)
            by_groups(sp, body)

        @block.gpsimd
        def _(pool):
            def body(g, r, it):
                pool.wait_ge(s.out_ready.sem, s.out_ready.at(g + 1))
                pool.sem_inc(k.pool_pass, 1)
                for buf, table in stores:
                    pool.dma_start(rows(table, g * GT, GT), buf[:, r]).then_inc(k.pool_dma[r].sem, 16)
            by_groups(pool, body)
            for r in range(RING):
                pool.wait_ge(k.pool_dma[r].sem, k.pool_dma[r].at(16 * len(stores) * (GROUPS // RING)))

        if "tensor" in engines:
            block.tensor(engines["tensor"])
        block.vector(engines["vector"])
        block.scalar(engines["scalar"])
    for r in range(RING):
        k.sp_dma[r].advance(16 * len(loads) * (GROUPS // RING))
        k.pool_dma[r].advance(16 * len(stores) * (GROUPS // RING))
    for signal, n in tallies:
        signal.advance(n * GROUPS)


def bank_free(g, r):
    return g if r == 0 else g - 1


class Norm:

    def __init__(self, k, ctx, number=0):
        self.k = k
        self.bn, self.stat, self.root_sig, self.inverse, self.factor = (x[number] for x in k.norm_signals)

        def sb(name, shape):
            return ctx.enter_context(k.nc.sbuf_tensor(k.name(name), shape, F32))
        self.stats, self.mv = sb("bn_stats", [P, RING, GT, 6]), sb("mean_var", [P, RING, GT, 2])
        self.root, self.scale = sb("root", [P, RING, GT]), sb("rstd", [P, RING, GT])
        self.shift = sb("shift", [P, RING, GT])

    def statistics(self, dve, x, g, r):
        for q in range(GT):
            dve.bn_stats(self.stats[:, r, q, :], x[:, r, q, :]).then_inc(self.bn.sem, 1)
        dve.wait_ge(self.bn.sem, self.bn.at((g + 1) * GT))
        dve.sem_inc(self.k.dve_pass, 1)
        for q in range(GT):
            ins = dve.bn_aggr(self.mv[:, r, q, :], self.stats[:, r, q, :])
        ins.then_inc(self.stat.sem, 1)

    def square_root(self, act, g, r):
        act.wait_ge(self.stat.sem, self.stat.at(g + 1))
        act.activation(self.root[:, r, :], self.mv[:, r, :, 1], ACT.Sqrt,
                       bias=self.k.eps[:, 0:1]).then_inc(self.root_sig.sem, 1)

    def factors(self, dve, g, r, extra=None):
        n = 2 if extra is not None else 1
        dve.wait_ge(self.root_sig.sem, self.root_sig.at(g + 1))
        dve.reciprocal(self.scale[:, r, :], self.root[:, r, :]).then_inc(self.inverse.sem, 1)
        dve.wait_ge(self.inverse.sem, self.inverse.at(g * n + 1))
        if extra is not None:
            dve.tensor_tensor(self.scale[:, r, :], self.scale[:, r, :], extra, ALU.mult
                              ).then_inc(self.inverse.sem, 1)
            dve.wait_ge(self.inverse.sem, self.inverse.at(g * n + 2))
        dve.scalar_tensor_tensor(self.shift[:, r, :], self.mv[:, r, :, 0], -1.0, self.scale[:, r, :],
                                 ALU.mult, ALU.mult).then_inc(self.factor.sem, 1)

    def apply(self, act, g, r, out, x, func):
        act.wait_ge(self.factor.sem, self.factor.at(g + 1))
        for q in range(GT):
            ins = act.activation(out[:, r, q, :], x[:, r, q, :], func, bias=self.shift[:, r, q:q + 1],
                                 scale=self.scale[:, r, q:q + 1])
        return ins

    def tallies(self, extra=False):
        return [(self.bn, GT), (self.stat, 1), (self.root_sig, 1), (self.inverse, 2 if extra else 1),
                (self.factor, 1)]


def ring_buffer(k, ctx, name, width=D):
    return ctx.enter_context(k.nc.sbuf_tensor(k.name(name), [P, RING, GT, width], F32))


def pair_buffer(k, ctx, name):
    return ctx.enter_context(k.nc.sbuf_tensor(k.name(name), [P, 2, GT, D], F32))


def bank(k, n):
    return k.ps[:, n, :].rearrange("p (t d) -> p t d", t=GT)


def norm_pass(k, x, out):
    s = k.s
    with ExitStack() as ctx:
        xb, hb = ring_buffer(k, ctx, "x"), ring_buffer(k, ctx, "h")
        norm = Norm(k, ctx)

        def vector(dve):
            def stats(g, r, it):
                dve.wait_ge(k.sp_dma[r].sem, k.sp_dma[r].at((it + 1) * 16))
                norm.statistics(dve, xb, g, r)

            def factors(g, r, it):
                norm.factors(dve, g, r)
            by_groups(dve, stats, factors)

        def scalar(act):
            def body(g, r, it):
                norm.square_root(act, g, r)
                norm.apply(act, g, r, hb, xb, ACT.Relu).then_inc(s.out_ready.sem, 1)
            by_groups(act, lambda g, r, it: None, body)

        node_pass(k, [(xb, x)], [(hb, out)], {"vector": vector, "scalar": scalar},
                  [(s.out_ready, 1)] + norm.tallies())


def sage_pass(k, h, w_self, w_neigh, bias, out, x=None, x_out=None):
    s = k.s
    with ExitStack() as ctx:
        hb, ab = ring_buffer(k, ctx, "h"), ring_buffer(k, ctx, "agg")
        yb, ob = ring_buffer(k, ctx, "y"), ring_buffer(k, ctx, "out")
        xb = ring_buffer(k, ctx, "x") if x is not None else None
        mean = pair_buffer(k, ctx, "mean")
        h_t, a_t = pair_buffer(k, ctx, "h_t"), pair_buffer(k, ctx, "mean_t")
        norm = Norm(k, ctx)
        loads = [(hb, h), (ab, k.agg)] + ([(xb, x)] if x is not None else [])
        stores = [(ob, out)] + ([(yb, x_out)] if x is not None else [])

        def landed(eng, r, it):
            eng.wait_ge(k.sp_dma[r].sem, k.sp_dma[r].at((it + 1) * (16 * len(loads))))

        def scalar(act):
            def copy(g, r, it):
                b = r % 2
                landed(act, r, it)
                act.wait_ge(s.h_t.sem, s.h_t.at(bank_free(g, r)))
                for q in range(GT):
                    ins = act.activation(mean[:, b, q, :], ab[:, r, q, :], ACT.Copy,
                                         scale=k.mean_scale[:, bass.ds(g * GT + q, 1)])
                ins.then_inc(s.part_ready.sem, 1)
                act.wait_ge(s.in_t.sem, s.in_t.at(g + 1))
                act.wait_ge(s.mm_done.sem, s.mm_done.at(bank_free(g, r)))
                act.copy(h_t[:, b], bank(k, b)).then_inc(s.in_copied.sem, 1)

            def relu(g, r, it):
                act.wait_ge(s.mm_read.sem, s.mm_read.at(g + 1))
                act.activation(ob[:, r], yb[:, r], ACT.Relu).then_inc(s.out_ready.sem, 1)

            def normed(g, r, it):
                norm.square_root(act, g, r)
                norm.apply(act, g, r, ob, yb, ACT.Relu).then_inc(s.out_ready.sem, 1)
            if x is None:
                by_groups(act, copy, relu)
            else:
                by_groups(act, copy, lambda g, r, it: None, normed)

        def tensor(pe):
            def turn(g, r, it):
                b = r % 2
                landed(pe, r, it)
                pe.wait_ge(s.in_copied.sem, s.in_copied.at(bank_free(g, r)))
                for q in range(GT):
                    mm = pe.transpose(bank(k, b)[:, q, :], hb[:, r, q, :], k.ident[:, :])
                mm.then_inc(s.in_t.sem, 1)
                pe.wait_ge(s.part_ready.sem, s.part_ready.at(g + 1))
                pe.wait_ge(s.h_copied.sem, s.h_copied.at(bank_free(g, r)))
                for q in range(GT):
                    mm = pe.transpose(bank(k, 2 + b)[:, q, :], mean[:, b, q, :], k.ident[:, :])
                mm.then_inc(s.h_t.sem, 1)

            def multiply(g, r, it):
                b = r % 2
                pe.wait_ge(s.in_copied.sem, s.in_copied.at(g + 1))
                pe.wait_ge(s.h_copied.sem, s.h_copied.at(g + 1))
                pe.wait_ge(s.mm_read.sem, s.mm_read.at(bank_free(g, r)))
                for q in range(GT):
                    pe.matmul(bank(k, 4 + b)[:, q, :], h_t[:, b, q, :], w_self[:, :], start=True, stop=False)
                    mm = pe.matmul(bank(k, 4 + b)[:, q, :], a_t[:, b, q, :], w_neigh[:, :],
                                   start=False, stop=True)
                mm.then_inc(s.mm_done.sem, 1)
            by_groups(pe, turn, multiply)

        def vector(dve):
            def copy(g, r, it):
                b = r % 2
                dve.wait_ge(s.h_t.sem, s.h_t.at(g + 1))
                dve.wait_ge(s.mm_done.sem, s.mm_done.at(bank_free(g, r)))
                dve.tensor_copy(a_t[:, b], bank(k, 2 + b)).then_inc(s.h_copied.sem, 1)

            def add(g, r, it):
                b = r % 2
                dve.wait_ge(s.mm_done.sem, s.mm_done.at(g + 1))
                dve.tensor_tensor(yb[:, r], bank(k, 4 + b), bias[:, :, :], ALU.add).then_inc(s.mm_read.sem, 1)
                if x is not None:
                    landed(dve, r, it)
                    dve.wait_ge(s.mm_read.sem, s.mm_read.at(g + 1))
                    dve.tensor_tensor(yb[:, r], yb[:, r], xb[:, r], ALU.add).then_inc(s.x_ready.sem, 1)
                    dve.wait_ge(s.x_ready.sem, s.x_ready.at(g + 1))
                    norm.statistics(dve, yb, g, r)

            def factors(g, r, it):
                norm.factors(dve, g, r)
            if x is None:
                by_groups(dve, copy, add)
            else:
                by_groups(dve, copy, add, factors)

        node_pass(k, loads, stores, {"vector": vector, "scalar": scalar, "tensor": tensor},
                  [(s.out_ready, 1), (s.h_t, 1), (s.part_ready, 1), (s.in_t, 1),
                   (s.mm_done, 1), (s.in_copied, 1), (s.h_copied, 1), (s.mm_read, 1)]
                  + (norm.tallies() + [(s.x_ready, 1)] if x is not None else []))


def attention_pass(k, h, x, x_out, out):
    s = k.s
    with ExitStack() as ctx:
        hb, ab = ring_buffer(k, ctx, "h"), ring_buffer(k, ctx, "agg", ZW)
        xb, yb, ob = (ring_buffer(k, ctx, n) for n in ("x", "y", "out"))
        h_t, n_t = pair_buffer(k, ctx, "h_t"), pair_buffer(k, ctx, "n_t")
        den = ctx.enter_context(k.nc.sbuf_tensor(k.name("den"), [P, RING, GT], F32))
        nb = hb
        norm = Norm(k, ctx)
        loads = [(hb, h), (ab, k.agg_src, D + 1), (xb, x)]

        def landed(eng, r, it):
            eng.wait_ge(k.sp_dma[r].sem, k.sp_dma[r].at((it + 1) * (16 * len(loads))))

        def scalar(act):
            def first(g, r, it):
                b = r % 2
                landed(act, r, it)
                act.activation(den[:, r, :], ab[:, r, :, D], ACT.Exp).then_inc(s.exp_ready.sem, 1)
                act.wait_ge(s.in_t.sem, s.in_t.at(g + 1))
                act.wait_ge(s.mm_done.sem, s.mm_done.at(bank_free(g, r)))
                act.copy(h_t[:, b], bank(k, b)).then_inc(s.in_copied.sem, 1)

            def normed(g, r, it):
                norm.square_root(act, g, r)
                norm.apply(act, g, r, nb, yb, ACT.Relu).then_inc(s.h_ready.sem, 1)

            def scaled(g, r, it):
                act.wait_ge(s.mm2_done.sem, s.mm2_done.at(g + 1))
                for q in range(GT):
                    ins = act.activation(ob[:, r, q, :], bank(k, 6 + r % 2)[:, q, :], ACT.Copy,
                                         scale=k.dinv_w[:, bass.ds(g * GT + q, 1)])
                ins.then_inc(s.out_ready.sem, 1)
            by_groups(act, first, lambda g, r, it: None, normed, lambda g, r, it: None, scaled)

        def tensor(pe):
            def turn(g, r, it):
                b = r % 2
                landed(pe, r, it)
                pe.wait_ge(s.in_copied.sem, s.in_copied.at(bank_free(g, r)))
                for q in range(GT):
                    mm = pe.transpose(bank(k, b)[:, q, :], hb[:, r, q, :], k.ident[:, :])
                mm.then_inc(s.in_t.sem, 1)

            def multiply(g, r, it):
                b = r % 2
                pe.wait_ge(s.in_copied.sem, s.in_copied.at(g + 1))
                pe.wait_ge(s.mm_read.sem, s.mm_read.at(bank_free(g, r)))
                for q in range(GT):
                    mm = pe.matmul(bank(k, 4 + b)[:, q, :], h_t[:, b, q, :], k.w["u"][:, :],
                                   start=True, stop=True)
                mm.then_inc(s.mm_done.sem, 1)

            def turn_normed(g, r, it):
                b = r % 2
                pe.wait_ge(s.h_ready.sem, s.h_ready.at(g + 1))
                pe.wait_ge(s.h_copied.sem, s.h_copied.at(bank_free(g, r)))
                for q in range(GT):
                    mm = pe.transpose(bank(k, 2 + b)[:, q, :], nb[:, r, q, :], k.ident[:, :])
                mm.then_inc(s.h_t.sem, 1)

            def multiply_normed(g, r, it):
                b = r % 2
                pe.wait_ge(s.h_copied.sem, s.h_copied.at(g + 1))
                pe.wait_ge(s.out_ready.sem, s.out_ready.at(bank_free(g, r)))
                for q in range(GT):
                    mm = pe.matmul(bank(k, 6 + b)[:, q, :], n_t[:, b, q, :], k.w["gcn"][:, :],
                                   start=True, stop=True)
                mm.then_inc(s.mm2_done.sem, 1)
            by_groups(pe, turn, multiply, lambda g, r, it: None, turn_normed, multiply_normed)

        def vector(dve):
            def add(g, r, it):
                b = r % 2
                dve.wait_ge(s.exp_ready.sem, s.exp_ready.at(g + 1))
                dve.reciprocal(den[:, r, :], den[:, r, :]).then_inc(s.first_add.sem, 1)
                dve.wait_ge(s.mm_done.sem, s.mm_done.at(g + 1))
                dve.tensor_tensor(yb[:, r], bank(k, 4 + b), k.b["u"][:, :, :], ALU.add
                                  ).then_inc(s.mm_read.sem, 1)
                landed(dve, r, it)
                dve.wait_ge(s.first_add.sem, s.first_add.at(g + 1))
                for q in range(GT):
                    dve.scalar_tensor_tensor(xb[:, r, q, :], ab[:, r, q, 0:D], den[:, r, q:q + 1],
                                             xb[:, r, q, :], ALU.mult, ALU.add).then_inc(s.second_add.sem, 1)
                dve.wait_ge(s.mm_read.sem, s.mm_read.at(g + 1))
                dve.wait_ge(s.second_add.sem, s.second_add.at((g + 1) * GT))
                dve.tensor_tensor(yb[:, r], yb[:, r], xb[:, r], ALU.add).then_inc(s.x_ready.sem, 1)
                dve.wait_ge(s.x_ready.sem, s.x_ready.at(g + 1))
                norm.statistics(dve, yb, g, r)

            def factors(g, r, it):
                norm.factors(dve, g, r)

            def copy(g, r, it):
                b = r % 2
                dve.wait_ge(s.h_t.sem, s.h_t.at(g + 1))
                dve.wait_ge(s.mm2_done.sem, s.mm2_done.at(bank_free(g, r)))
                dve.tensor_copy(n_t[:, b], bank(k, 2 + b)).then_inc(s.h_copied.sem, 1)
            by_groups(dve, lambda g, r, it: None, add, factors, copy)

        node_pass(k, loads, [(ob, out), (yb, x_out)], {"vector": vector, "scalar": scalar, "tensor": tensor},
                  [(s.out_ready, 1), (s.h_t, 1), (s.in_t, 1), (s.mm_done, 1), (s.in_copied, 1),
                   (s.h_copied, 1), (s.mm_read, 1), (s.x_ready, 1), (s.exp_ready, 1), (s.h_ready, 1),
                   (s.mm2_done, 1), (s.first_add, 1), (s.second_add, GT)] + norm.tallies())


def elu_pass(k, table, out):
    s, nc = k.s, k.nc
    with ExitStack() as ctx:
        ab, tb = ring_buffer(k, ctx, "agg"), ring_buffer(k, ctx, "own")
        eb, qb = ring_buffer(k, ctx, "exp"), ring_buffer(k, ctx, "square")
        ones = ctx.enter_context(nc.sbuf_tensor("ones_col", [P, 1], F32))
        ones_ready = ctx.enter_context(nc.semaphore("ones_col_ready"))

        def vector(dve):
            dve.memset(ones[:, :], 1.0).then_inc(ones_ready, 1)

            def first(g, r, it):
                dve.wait_ge(k.sp_dma[r].sem, k.sp_dma[r].at((it + 1) * 32))
                dve.tensor_tensor(ab[:, r], ab[:, r], tb[:, r], ALU.add).then_inc(s.first_add.sem, 1)
                dve.wait_ge(s.first_add.sem, s.first_add.at(g + 1))
                for q in range(GT):
                    ins = dve.scalar_tensor_tensor(tb[:, r, q, :], ab[:, r, q, :],
                                                   k.dinv_w[:, bass.ds(g * GT + q, 1)], k.b["gcn"][:, q, :],
                                                   ALU.mult, ALU.add)
                ins.then_inc(s.x_ready.sem, 1)

            def second(g, r, it):
                dve.wait_ge(s.exp_ready.sem, s.exp_ready.at(g + 1))
                dve.tensor_scalar(eb[:, r], eb[:, r], 1.0, -1.0, ALU.min, ALU.add).then_inc(s.second_add.sem, 1)
                dve.wait_ge(s.second_add.sem, s.second_add.at(g + 1))
                dve.tensor_tensor(eb[:, r], eb[:, r], tb[:, r], ALU.max).then_inc(s.h_ready.sem, 1)
            by_groups(dve, first, second)

        def scalar(act):
            def exponential(g, r, it):
                act.wait_ge(s.x_ready.sem, s.x_ready.at(g + 1))
                act.activation(eb[:, r], tb[:, r], ACT.Exp).then_inc(s.exp_ready.sem, 1)

            def square(g, r, it):
                act.wait_ge(s.h_ready.sem, s.h_ready.at(g + 1))
                act.activation(qb[:, r], eb[:, r], ACT.Square).then_inc(s.part_ready.sem, 1)
            by_groups(act, exponential, square)

        def tensor(pe):
            pe.wait_ge(ones_ready, 1)

            def total(g, r, it):
                pe.wait_ge(s.part_ready.sem, s.part_ready.at(g + 1))
                first = isinstance(g, int) and g == 0
                for n, buf in enumerate((eb, qb)):
                    mm = pe.matmul(k.ps[0:1, n, :], ones[:, :], buf[:, r].rearrange("p t d -> p (t d)"),
                                   start=first, stop=True, skip_group_check=True)
                mm.then_inc(s.out_ready.sem, 1)

            def tail(g, r, it):
                pe.wait_ge(s.part_ready.sem, s.part_ready.at(g + 1))
                for n, buf in enumerate((eb, qb)):
                    for q in range(GT):
                        real = min(P, N_REAL - (g * GT + q) * P)
                        if real > 0:
                            mm = pe.matmul(k.ps[0:1, n, q * P:(q + 1) * P], ones[0:real, :], buf[0:real, r, q, :],
                                           start=False, stop=True, skip_group_check=True)
                mm.then_inc(s.out_ready.sem, 1)

            for r in range(RING):
                total(r, r, 0)
            with pe.Fori(1, GROUPS // RING - 1) as it:
                for r in range(RING):
                    total(it * RING + r, r, it)
            for r in range(RING):
                g = GROUPS - RING + r
                (tail if g == GROUPS - 1 else total)(g, r, GROUPS // RING - 1)

        node_pass(k, [(ab, k.agg), (tb, table)], [(eb, out)],
                  {"vector": vector, "scalar": scalar, "tensor": tensor},
                  [(s.out_ready, 1), (s.first_add, 1), (s.second_add, 1), (s.x_ready, 1), (s.exp_ready, 1),
                   (s.h_ready, 1), (s.part_ready, 1)])


def batch_factors(k):
    nc = k.nc
    with ExitStack() as ctx:
        def sb(name, shape):
            return ctx.enter_context(nc.sbuf_tensor(name, shape, F32))

        means, sq = sb("bn_means", [1, 2, D]), sb("bn_sq", [1, D])
        factor = sb("bn_factor", [1, 2, D])
        ones = sb("ones_row", [1, P])
        var_ready, root_ready, rows_ready, spread = (ctx.enter_context(nc.semaphore(n)) for n in (
            "var_ready", "root_ready_bn", "rows_ready", "spread"))
        with nc.Block() as block:
            @block.vector
            def _(dve):
                c = Chain(k.dve_chain, dve)
                dve.memset(ones[:, :], 1.0)
                for n in range(2):
                    c.mark(dve.tensor_reduce(means[:, n, :], k.ps[0:1, n, :].rearrange("p (t d) -> p d t", t=GT),
                                             AX.X, ALU.add))
                c.wait()
                c.mark(dve.tensor_scalar(means[:, :, :], means[:, :, :], 1.0 / N_REAL, None, ALU.mult))
                c.wait()
                c.mark(dve.tensor_tensor(sq[:, :], means[:, 0, :], means[:, 0, :], ALU.mult))
                c.wait()
                c.mark(dve.tensor_tensor(sq[:, :], means[:, 1, :], sq[:, :], ALU.subtract))
                c.wait()
                dve.tensor_scalar(sq[:, :], sq[:, :], 0.0, None, ALU.max).then_inc(var_ready, 1)
                dve.wait_ge(root_ready, 1)
                c.mark(dve.reciprocal(sq[:, :], sq[:, :]))
                c.wait()
                c.mark(dve.tensor_tensor(factor[:, 0, :], sq[:, :], k.bn_rows[:, 0, :], ALU.mult))
                c.wait()
                c.mark(dve.tensor_tensor(sq[:, :], means[:, 0, :], factor[:, 0, :], ALU.mult))
                c.wait()
                dve.tensor_tensor(factor[:, 1, :], k.bn_rows[:, 1, :], sq[:, :], ALU.subtract
                                  ).then_inc(rows_ready, 1)
                dve.wait_ge(spread, 1)
                for n, name in enumerate(("bn_a", "bn_b")):
                    for t in range(GT):
                        dve.tensor_copy(k.b[name][:, t, :], k.ps[:, 2, n * D:(n + 1) * D])
                k.dve_chain.advance(c.n)

            @block.scalar
            def _(act):
                act.wait_ge(var_ready, 1)
                act.activation(sq[:, :], sq[:, :], ACT.Sqrt, bias=k.eps[0:1, 0:1]).then_inc(root_ready, 1)

            @block.tensor
            def _(pe):
                pe.wait_ge(rows_ready, 1)
                pe.matmul(k.ps[:, 2, 0:2 * D], ones[:, :], factor[:, :, :].rearrange("p n d -> p (n d)"),
                          start=True, stop=True).then_inc(spread, 1)


def batch_pass(k, o, x, x_out, out):
    s = k.s
    with ExitStack() as ctx:
        eb, xb, yb, ob = (ring_buffer(k, ctx, n) for n in ("o", "x", "y", "out"))
        inner, outer = Norm(k, ctx, 0), Norm(k, ctx, 1)

        def vector(dve):
            def batch(g, r, it):
                dve.wait_ge(k.sp_dma[r].sem, k.sp_dma[r].at((it + 1) * 32))
                dve.tensor_tensor(eb[:, r], eb[:, r], k.b["bn_a"][:, :, :], ALU.mult).then_inc(s.first_add.sem, 1)
                dve.wait_ge(s.first_add.sem, s.first_add.at(g + 1))
                dve.tensor_tensor(eb[:, r], eb[:, r], k.b["bn_b"][:, :, :], ALU.add).then_inc(s.second_add.sem, 1)
                dve.wait_ge(s.second_add.sem, s.second_add.at(g + 1))
                inner.statistics(dve, eb, g, r)

            def inner_factors(g, r, it):
                inner.factors(dve, g, r)

            def add(g, r, it):
                dve.wait_ge(s.h_ready.sem, s.h_ready.at(g + 1))
                for n, (other, op) in enumerate(((k.b["ln_g"][:, :, :], ALU.mult), (k.b["ln_b"][:, :, :], ALU.add),
                                                 (xb[:, r], ALU.add))):
                    dve.tensor_tensor(yb[:, r], yb[:, r], other, op).then_inc(s.x_ready.sem, 1)
                    dve.wait_ge(s.x_ready.sem, s.x_ready.at(g * 3 + n + 1))
                outer.statistics(dve, yb, g, r)

            def outer_factors(g, r, it):
                outer.factors(dve, g, r, k.dinv_c[:, bass.ds(g * GT, GT)])
            by_groups(dve, batch, inner_factors, add, outer_factors)

        def scalar(act):
            def inner_norm(g, r, it):
                inner.square_root(act, g, r)
                inner.apply(act, g, r, yb, eb, ACT.Identity).then_inc(s.h_ready.sem, 1)

            def outer_norm(g, r, it):
                outer.square_root(act, g, r)
                outer.apply(act, g, r, ob, yb, ACT.Relu).then_inc(s.out_ready.sem, 1)
            by_groups(act, lambda g, r, it: None, inner_norm, lambda g, r, it: None, outer_norm)

        node_pass(k, [(eb, o), (xb, x)], [(ob, out), (yb, x_out)], {"vector": vector, "scalar": scalar},
                  [(s.out_ready, 1), (s.first_add, 1), (s.second_add, 1), (s.x_ready, 3), (s.h_ready, 1)]
                  + inner.tallies() + outer.tallies(extra=True))


def gcn_pass(k, table, w, bias, out, x=None):
    s = k.s
    with ExitStack() as ctx:
        ab, tb, ob = (ring_buffer(k, ctx, n) for n in ("agg", "own", "out"))
        xb = ring_buffer(k, ctx, "x") if x is not None else None
        sum_t = pair_buffer(k, ctx, "sum_t")
        loads = [(ab, k.agg), (tb, table)] + ([(xb, x)] if x is not None else [])

        def landed(eng, r, it):
            eng.wait_ge(k.sp_dma[r].sem, k.sp_dma[r].at((it + 1) * (16 * len(loads))))

        def vector(dve):
            def add(g, r, it):
                landed(dve, r, it)
                dve.tensor_tensor(ab[:, r], ab[:, r], tb[:, r], ALU.add).then_inc(s.first_add.sem, 1)

            def finish(g, r, it):
                dve.wait_ge(s.mm_done.sem, s.mm_done.at(g + 1))
                for q in range(GT):
                    ins = dve.scalar_tensor_tensor(tb[:, r, q, :], bank(k, 4 + r % 2)[:, q, :],
                                                   k.dinv_c[:, bass.ds(g * GT + q, 1)], bias[:, q, :],
                                                   ALU.mult, ALU.add)
                ins.then_inc(s.mm_read.sem, 1)
                if x is not None:
                    dve.wait_ge(s.mm_read.sem, s.mm_read.at(g + 1))
                    dve.tensor_tensor(ob[:, r], tb[:, r], xb[:, r], ALU.add).then_inc(s.out_ready.sem, 1)
            by_groups(dve, add, finish)

        def scalar(act):
            def copy(g, r, it):
                act.wait_ge(s.in_t.sem, s.in_t.at(g + 1))
                act.wait_ge(s.mm_done.sem, s.mm_done.at(bank_free(g, r)))
                act.copy(sum_t[:, r % 2], bank(k, r % 2)).then_inc(s.in_copied.sem, 1)

            def scale(g, r, it):
                act.wait_ge(s.mm_read.sem, s.mm_read.at(g + 1))
                for q in range(GT):
                    ins = act.activation(ob[:, r, q, :], tb[:, r, q, :], ACT.Copy,
                                         scale=k.dinv_c[:, bass.ds(g * GT + q, 1)])
                ins.then_inc(s.out_ready.sem, 1)
            if x is None:
                by_groups(act, copy, lambda g, r, it: None, scale)
            else:
                by_groups(act, copy)

        def tensor(pe):
            def turn(g, r, it):
                pe.wait_ge(s.first_add.sem, s.first_add.at(g + 1))
                pe.wait_ge(s.in_copied.sem, s.in_copied.at(bank_free(g, r)))
                for q in range(GT):
                    mm = pe.transpose(bank(k, r % 2)[:, q, :], ab[:, r, q, :], k.ident[:, :])
                mm.then_inc(s.in_t.sem, 1)

            def multiply(g, r, it):
                pe.wait_ge(s.in_copied.sem, s.in_copied.at(g + 1))
                pe.wait_ge(s.mm_read.sem, s.mm_read.at(bank_free(g, r)))
                for q in range(GT):
                    mm = pe.matmul(bank(k, 4 + r % 2)[:, q, :], sum_t[:, r % 2, q, :], w[:, :],
                                   start=True, stop=True)
                mm.then_inc(s.mm_done.sem, 1)
            by_groups(pe, turn, multiply)

        node_pass(k, loads, [(ob, out)], {"vector": vector, "scalar": scalar, "tensor": tensor},
                  [(s.out_ready, 1), (s.first_add, 1), (s.mm_done, 1), (s.mm_read, 1), (s.in_t, 1),
                   (s.in_copied, 1)])


def edge_pass(k, h, ins):
    nc, s = k.nc, k.s
    scale = float(D) ** -0.5
    with ExitStack() as ctx:
        def sb(name, shape, dt=F32):
            return ctx.enter_context(nc.sbuf_tensor(name, shape, dt))

        ni, nj = sb("ni", [P, 2, GT, D]), sb("nj", [P, 2, GT, D])
        ea = sb("ea", [P, 2, GT, EA])
        zb = sb("zb", [P, 2, GT, ZW])
        staged = sb("staged_ij", [P, 2, 2, GT], I32)
        ni_t, nj_t = sb("ni_t", [P, 2, GT * P]), sb("nj_t", [P, 2, GT * P])
        ea_t = sb("ea_t", [P, 2, GT * P])
        ex, f_t = sb("ex", [P, GT * P]), sb("f_t", [P, GT * P])
        m1 = sb("m1", [P, GT * P])
        q_t, prod = sb("q_t", [P, GT * P]), sb("prod", [P, GT * P])
        mask = sb("mask", [P, 2, GT])
        um, a, ea_x, wz = (sb(n, [P, GT]) for n in ("um", "a", "exp_a", "wz"))
        ea_in = ins["edge_attr_70"].rearrange("(p t) c -> p t c", p=P)
        z_out = k.z.rearrange("(p t) c -> p t c", p=P)
        B_NI, B_NJ, B_EA, B_PRE, B_Q, B_K, B_U, B_G = range(8)
        ps = k.ps

        with nc.Block() as block:
            def pairs(eng, body, peel=False):
                with eng.Fori(0, GROUPS // 2 - (1 if peel else 0)) as it:
                    for b in range(2):
                        body(it * 2 + b, b, it)
                if peel:
                    for b in range(2):
                        body(GROUPS - 2 + b, b, GROUPS // 2 - 1)

            @block.sync
            def _(sp):
                def load(g, b):
                    sp.wait_ge(s.in_t.sem, s.in_t.at(g - 1))
                    sp.sem_inc(k.sp_pass, 1)
                    sp.wait_ge(s.mask_ready.sem, s.mask_ready.at(g - 1))
                    sp.sem_inc(k.sp_pass, 1)
                    sp.dma_start(ea[:, b, :, :], ea_in[:, bass.ds(g * GT, GT), :]).then_inc(k.sp_dma[b].sem, 16)

                def body(g, b, it):
                    if not (isinstance(g, int) and g == GROUPS - 1):
                        load(g + 1, 1 - b)
                    sp.wait_ge(s.z_ready.sem, s.z_ready.at(g + 1))
                    sp.sem_inc(k.sp_pass, 1)
                    sp.dma_start(z_out[:, bass.ds(g * GT, GT), :], zb[:, b, :, :]
                                 ).then_inc(k.sp_dma[2 + b].sem, 16)
                load(0, 0)
                pairs(sp, body, peel=True)
                for b in range(2):
                    sp.wait_ge(k.sp_dma[2 + b].sem, k.sp_dma[2 + b].at(16 * GROUPS // 2))

            @block.gpsimd
            def _(pool):
                def body(g, b, it):
                    pool.wait_ge(s.in_t.sem, s.in_t.at(g - 1))
                    pool.sem_inc(k.pool_pass, 1)
                    pool.wait_ge(s.idx_staged.sem, s.idx_staged.at(g + 1))
                    pool.sem_inc(k.pool_pass, 1)
                    for n, buf in enumerate((ni, nj)):
                        for q in range(GT):
                            pool.indirect_dma_start(
                                buf[:, b, q, :], None, h,
                                bass.IndirectOffsetOnAxis(ap=staged[:, b, n, q:q + 1], axis=0)
                            ).then_inc(k.pool_dma[b].sem, 16)
                pairs(pool, body)

            @block.tensor
            def _(pe):
                def turn(g, b, it):
                    pe.wait_ge(k.pool_dma[b].sem, k.pool_dma[b].at((it + 1) * (16 * 2 * GT)))
                    pe.wait_ge(k.sp_dma[b].sem, k.sp_dma[b].at((it + 1) * 16))
                    pe.wait_ge(s.in_copied.sem, s.in_copied.at(g * 3))
                    for q in range(GT):
                        cut = slice(q * P, (q + 1) * P)
                        pe.transpose(ps[:, B_NI, cut], ni[:, b, q, :], k.ident[:, :])
                        pe.transpose(ps[:, B_NJ, cut], nj[:, b, q, :], k.ident[:, :])
                        mm = pe.transpose(ps[0:EF, B_EA, cut], ea[:, b, q, 0:EF], k.ident[:, :])
                    mm.then_inc(s.in_t.sem, 1)

                def project(g, b, it):
                    pe.wait_ge(s.in_copied.sem, s.in_copied.at(g * 3 + 3))
                    pe.wait_ge(s.q_ready.sem, s.q_ready.at(g))
                    pe.matmul(ps[:, B_Q, :], k.w["q"][:, :], ni_t[:, b, :], start=True,
                              stop=True).then_inc(s.h_t.sem, 1)
                    pe.wait_ge(s.f_ready.sem, s.f_ready.at(g))
                    pe.matmul(ps[:, B_PRE, :], k.w["ni"][:, :], ni_t[:, b, :], start=True, stop=False)
                    pe.matmul(ps[:, B_PRE, :], k.w["nj"][:, :], nj_t[:, b, :], start=False, stop=False)
                    pe.matmul(ps[:, B_PRE, :], k.w["ea"][0:EF, :], ea_t[0:EF, b, :], start=False,
                              stop=True).then_inc(s.mm_done.sem, 1)

                def score(g, b, it):
                    more = not (isinstance(g, int) and g == GROUPS - 1)
                    if more:
                        turn(g + 1, 1 - b, it + b)
                    pe.wait_ge(s.f_ready.sem, s.f_ready.at(g + 1))
                    pe.matmul(ps[:, B_K, :], k.w["k"][:, :], f_t[:, :], start=True,
                              stop=True).then_inc(s.k_ready.sem, 1)
                    pe.wait_ge(s.z_ready.sem, s.z_ready.at(g))
                    for q in range(GT):
                        mm = pe.matmul(ps[:, B_G, q * P:(q + 1) * P], f_t[:, q * P:(q + 1) * P], k.w["u"][:, :],
                                       start=True, stop=True)
                    mm.then_inc(s.g_ready.sem, 1)
                    if more:
                        project(g + 1, 1 - b, it + b)
                    pe.wait_ge(s.prod_ready.sem, s.prod_ready.at(g + 1))
                    for q in range(GT):
                        mm = pe.matmul(ps[:, B_U, q:q + 1], prod[:, q * P:(q + 1) * P], k.wa[:, :],
                                       start=True, stop=True)
                    mm.then_inc(s.u_ready.sem, 1)
                turn(0, 0, 0)
                project(0, 0, 0)
                pairs(pe, score, peel=True)

            @block.scalar
            def _(act):
                def stage(g, b, it):
                    act.wait_ge(k.pool_dma[b].sem, k.pool_dma[b].at(it * (16 * 2 * GT)))
                    act.copy(staged[:, b, 0, :], k.edge_src[:, bass.ds(g * GT, GT)])
                    act.copy(staged[:, b, 1, :], k.edge_dst[:, bass.ds(g * GT, GT)]
                             ).then_inc(s.idx_staged.sem, 1)

                def copy(g, b, it):
                    act.wait_ge(s.in_t.sem, s.in_t.at(g + 1))
                    act.copy(ni_t[:, b, :], ps[:, B_NI, :]).then_inc(s.in_copied.sem, 1)
                    act.copy(ea_t[0:EF, b, :], ps[0:EF, B_EA, :]).then_inc(s.in_copied.sem, 1)

                def body(g, b, it):
                    act.wait_ge(s.h_t.sem, s.h_t.at(g + 1))
                    act.wait_ge(s.prod_ready.sem, s.prod_ready.at(g))
                    act.activation(q_t[:, :], ps[:, B_Q, :], ACT.Copy, scale=scale).then_inc(s.q_ready.sem, 1)
                    act.wait_ge(s.mm_done.sem, s.mm_done.at(g + 1))
                    act.activation(ex[:, :], ps[:, B_PRE, :], ACT.Exp, bias=k.bf[:, 0:1]
                                   ).then_inc(s.exp_ready.sem, 1)
                    if not (isinstance(g, int) and g == GROUPS - 1):
                        copy(g + 1, 1 - b, it + b)
                    if not (isinstance(g, int) and g >= GROUPS - 2):
                        stage(g + 2, b, it + 1)
                    act.wait_ge(s.um_ready.sem, s.um_ready.at(g + 1))
                    act.activation(a[:, :], um[:, :], ACT.Tanh).then_inc(s.a_ready.sem, 1)
                    act.wait_ge(s.a_ready.sem, s.a_ready.at(2 * g + 1))
                    act.activation(ea_x[:, :], a[:, :], ACT.Exp).then_inc(s.a_ready.sem, 1)
                for b in range(2):
                    stage(b, b, 0)
                copy(0, 0, 0)
                pairs(act, body, peel=True)

            @block.vector
            def _(dve):
                def copy(g, b, it):
                    dve.wait_ge(s.in_t.sem, s.in_t.at(g + 1))
                    dve.tensor_copy(nj_t[:, b, :], ps[:, B_NJ, :]).then_inc(s.in_copied.sem, 1)
                    dve.wait_ge(k.sp_dma[b].sem, k.sp_dma[b].at((it + 1) * 16))
                    dve.tensor_scalar(mask[:, b, :], ea[:, b, :, 0], 8.0, None, ALU.is_lt
                                      ).then_inc(s.mask_ready.sem, 1)

                def body(g, b, it):
                    c = Chain(k.dve_chain, dve, g, 2)
                    dve.wait_ge(s.exp_ready.sem, s.exp_ready.at(g + 1))
                    c.mark(dve.tensor_scalar(m1[:, :], ex[:, :], 1.0, -1.0, ALU.min, ALU.add))
                    c.wait()
                    dve.wait_ge(s.g_ready.sem, s.g_ready.at(g))
                    dve.scalar_tensor_tensor(f_t[:, :], ps[:, B_PRE, :], k.bf[:, 0:1], m1[:, :], ALU.add,
                                             ALU.max).then_inc(s.f_ready.sem, 1)
                    if not (isinstance(g, int) and g == GROUPS - 1):
                        copy(g + 1, 1 - b, it + b)
                    dve.wait_ge(s.k_ready.sem, s.k_ready.at(g + 1))
                    dve.wait_ge(s.q_ready.sem, s.q_ready.at(g + 1))
                    dve.wait_ge(s.u_ready.sem, s.u_ready.at(g))
                    dve.tensor_tensor(prod[:, :], q_t[:, :], ps[:, B_K, :], ALU.mult
                                      ).then_inc(s.prod_ready.sem, 1)
                    dve.wait_ge(s.u_ready.sem, s.u_ready.at(g + 1))
                    dve.wait_ge(s.mask_ready.sem, s.mask_ready.at(g + 1))
                    dve.tensor_tensor(um[:, :], ps[:, B_U, 0:GT], mask[:, b, :], ALU.mult
                                      ).then_inc(s.um_ready.sem, 1)
                    dve.wait_ge(s.a_ready.sem, s.a_ready.at(2 * g + 2))
                    c.mark(dve.tensor_tensor(wz[:, :], ea_x[:, :], mask[:, b, :], ALU.mult))
                    c.wait()
                    dve.wait_ge(s.g_ready.sem, s.g_ready.at(g + 1))
                    dve.wait_ge(k.sp_dma[2 + b].sem, k.sp_dma[2 + b].at(it * 16))
                    dve.tensor_copy(zb[:, b, :, D], a[:, :])
                    for q in range(GT):
                        z = dve.tensor_scalar(zb[:, b, q, 0:D], ps[:, B_G, q * P:(q + 1) * P], wz[:, q:q + 1],
                                              None, ALU.mult)
                    z.then_inc(s.z_ready.sem, 1)
                dve.memset(zb[:, :, :, D + 1:], 0.0)
                copy(0, 0, 0)
                pairs(dve, body, peel=True)

        for b in range(2):
            k.pool_dma[b].advance(16 * 2 * GT * GROUPS // 2)
            k.sp_dma[b].advance(16 * GROUPS // 2)
            k.sp_dma[2 + b].advance(16 * GROUPS // 2)
        for signal, n in ((s.in_t, 1), (s.in_copied, 3), (s.h_t, 1), (s.mm_done, 1), (s.k_ready, 1),
                          (s.g_ready, 1), (s.u_ready, 1), (s.idx_staged, 1), (s.q_ready, 1),
                          (s.exp_ready, 1), (s.a_ready, 2), (s.mask_ready, 1), (s.f_ready, 1),
                          (s.prod_ready, 1), (s.um_ready, 1), (s.z_ready, 1), (k.dve_chain, 2)):
            signal.advance(n * GROUPS)


def build(nc, ins, out, stop=None):
    k = Program()
    k.nc, k.names = nc, 0

    def name(text):
        k.names += 1
        return f"{text}_{k.names}"
    k.name = name
    with ExitStack() as ctx:
        setup(k, ctx)
        t0, t1 = k.table
        r0, r1 = k.res
        w, b = k.w, k.b
        steps = [
            lambda: constants_and_loads(k, ins),
            lambda: prepare(k, ins),
            lambda: norm_pass(k, ins["x"], t0),
            lambda: sum_over_nodes(k, "dst", t0, D, k.agg),
            lambda: sage_pass(k, t0, w["self0"], w["neigh0"], b["b0"], t1),
            lambda: sum_over_nodes(k, "dst", t1, D, k.agg),
            lambda: sage_pass(k, t1, w["self1"], w["neigh1"], b["b1"], t0, ins["x"], r0),
            lambda: edge_pass(k, t0, ins),
            lambda: sum_over_nodes(k, "src", k.z, ZW, k.agg_src),
            lambda: attention_pass(k, t0, r0, r1, t1),
            lambda: sum_over_nodes(k, "dst", t1, D, k.agg, weighted=True),
            lambda: elu_pass(k, t1, k.elu_out),
            lambda: batch_factors(k),
            lambda: batch_pass(k, k.elu_out, r1, r0, t0),
            lambda: sum_over_nodes(k, "dst", t0, D, k.agg),
            lambda: gcn_pass(k, t0, w["g0"], b["g0"], t1),
            lambda: sum_over_nodes(k, "dst", t1, D, k.agg),
            lambda: gcn_pass(k, t1, w["g1"], b["g1"], t0),
            lambda: sum_over_nodes(k, "dst", t0, D, k.agg),
            lambda: gcn_pass(k, t0, w["g2"], b["g2"], out, x=r0),
        ]
        for n, step in enumerate(steps[:stop]):
            step()


NAMES = ["x", "src", "dst", "edge_attr_70", "edge_weight",
         "L0_gnn_W_self0", "L0_gnn_W_neigh0", "L0_gnn_b0", "L0_gnn_W_self1", "L0_gnn_W_neigh1", "L0_gnn_b1",
         "L1_gnn_Wf", "L1_gnn_bf", "L1_gnn_Wq", "L1_gnn_Wk", "L1_gnn_Wa", "L1_gnn_Wu", "L1_gnn_bu",
         "L2_gnn_W", "L2_gnn_b", "L2_gnn_bn_gamma", "L2_gnn_bn_beta", "L2_gnn_ln_gamma", "L2_gnn_ln_beta",
         "L3_gnn_W", "L3_gnn_b"]
STOP = None


def kernel(**inputs):
    import numpy as np
    import concourse.bacc as bacc
    from concourse.bass_utils import run_bass_kernel_spmd

    nc = bacc.Bacc("TRN2", target_bir_lowering=False, num_devices=1)
    arrays, ins = {}, {}
    for name in NAMES:
        a = np.ascontiguousarray(inputs[name])
        if a.shape[0] == N_REAL:
            padded = np.full((NP,) + a.shape[1:], NP - 1 if name in ("src", "dst") else 0, a.dtype)
            padded[:N_REAL] = a
            a = padded
        arrays[name] = a
        ins[name] = nc.dram_tensor(name, a.shape, mybir.dt.from_np(a.dtype), kind="ExternalInput").ap()
    out = nc.dram_tensor("out", (NP, D), F32, kind="ExternalOutput").ap()
    build(nc, ins, out, STOP)
    r = run_bass_kernel_spmd(nc, [arrays], core_ids=[0])
    return r.results[0]["out"][:N_REAL]
```

```python
from contextlib import ExitStack

import concourse.bass as bass
from concourse import mybir

F32 = mybir.dt.float32
BF16 = mybir.dt.bfloat16
F16 = mybir.dt.float16
I32 = mybir.dt.int32
ALU = mybir.AluOpType
ACT = mybir.ActivationFunctionType
AX = mybir.AxisListType

P = 128
N_REAL = 50000
D = 128
TILES = 392
NP = TILES * P
STEPS = 2 * TILES
GT = 4
GROUPS = TILES // GT
RING = 7
SPARE = 16
HALF = 4
REGION = 8
SPT = 16
SLOTS = RING * GT
LANDING = 2
EA = 70
EF = 65
ZW = 130
EPS = 1e-5
WARM = 16
CHUNKS = [(c * P, min(P, TILES - c * P)) for c in range((TILES + P - 1) // P)]


class Signal:

    def __init__(self, handle, base=WARM):
        self.sem, self.base = handle, base

    def at(self, n):
        return n + self.base

    def advance(self, n):
        self.base += n


class Chain:

    def __init__(self, signal, eng, rounds=0, per_round=0):
        self.counter, self.eng, self.start, self.n = signal, eng, rounds * per_round, 0

    def mark(self, ins):
        ins.then_inc(self.counter.sem, 1)
        self.n += 1
        return self.counter.at(self.start + self.n)

    def wait(self, value=None):
        self.eng.wait_ge(self.counter.sem, self.counter.at(self.start + self.n) if value is None else value)


class Signals:

    def __init__(self, make):
        self.all = []

        def sig(name):
            self.all.append(make(name))
            return self.all[-1]
        self.tiles_ready = sig("tiles_ready")
        self.idx_staged = sig("idx_staged")
        self.cols_staged = sig("cols_staged")
        self.onehot_ready = sig("onehot_ready")
        self.step_done = sig("step_done")
        self.acc_done = sig("acc_done")
        self.in_t = sig("in_t")
        self.in_copied = sig("in_copied")
        self.mm_done = sig("mm_done")
        self.mm_read = sig("mm_read")
        self.mm2_done = sig("mm2_done")
        self.out_ready = sig("out_ready")
        self.x_ready = sig("x_ready")
        self.h_ready = sig("h_ready")
        self.h_t = sig("h_t")
        self.h_copied = sig("h_copied")
        self.part_ready = sig("part_ready")
        self.mask_ready = sig("mask_ready")
        self.exp_ready = sig("exp_ready")
        self.f_ready = sig("f_ready")
        self.nj_copied, self.ea_copied = sig("nj_copied"), sig("ea_copied")
        self.m1_ready, self.w_ready, self.wz_ready = sig("m1_ready"), sig("w_ready"), sig("wz_ready")
        self.k_ready = sig("k_ready")
        self.q_ready = sig("q_ready")
        self.prod_ready = sig("prod_ready")
        self.u_ready = sig("u_ready")
        self.um_ready = sig("um_ready")
        self.a_ready = sig("a_ready")
        self.g_ready = sig("g_ready")
        self.z_ready = sig("z_ready")
        self.first_add = sig("first_add")
        self.second_add = sig("second_add")


class Program:
    pass


def rows(ap, first, tiles):
    return ap[bass.ds(first * P, tiles * P), :].rearrange("(t p) d -> p t d", p=P)


def setup(k, ctx):
    nc = k.nc

    def sb(name, shape, dt=F32):
        return ctx.enter_context(nc.sbuf_tensor(name, shape, dt))

    def sig(name, base=WARM):
        return Signal(ctx.enter_context(nc.semaphore(name)), base)

    def dram(name, shape, dt=F32):
        return nc.dram_tensor(name, shape, dt, kind="Internal").ap()

    k.ps = ctx.enter_context(nc.psum_tensor("ps", [P, 8, 512], F32))
    k.ident = sb("ident", [P, P])
    k.iota = sb("iota", [P, P])
    k.w = {n: sb("w_" + n, [P, P]) for n in
           ("self0", "neigh0", "self1", "neigh1", "ni", "nj", "ea", "q", "k", "u", "gcn", "g0", "g1", "g2")}
    k.wf_diff = sb("wf_diff", [P, P])
    k.wa = sb("w_a", [P, 1])
    k.bf = sb("b_f", [P, 1])
    k.b = {n: sb("b_" + n, [P, GT, D]) for n in
           ("b0", "b1", "u", "gcn", "ln_g", "ln_b", "g0", "g1", "g2", "bn_a", "bn_b")}
    k.bn_rows = sb("bn_rows", [1, 2, D])
    k.eps = sb("eps", [P, 1])
    k.rel = {o: sb("rel_" + o, [P, STEPS + SPT]) for o in ("dst", "src")}
    k.keep = {o: sb("keep_" + o, [P, STEPS + SPT]) for o in ("dst", "src")}
    k.weight = sb("weight_dst", [P, STEPS + SPT])
    k.idx = {o: sb("idx_" + o, [P, TILES + SLOTS], I32) for o in ("dst", "src")}
    k.edge_src = sb("edge_src", [P, TILES + SLOTS], I32)
    k.edge_dst = sb("edge_dst", [P, TILES + SLOTS], I32)
    k.ctl_slot = {o: sb("ctl_slot_" + o, [1, STEPS], I32) for o in ("dst", "src")}
    k.ctl_out = {o: sb("ctl_out_" + o, [1, 2, STEPS // 2], I32) for o in ("dst", "src")}
    k.ctl_ready = {o: sb("ctl_ready_" + o, [1, STEPS // REGION], I32) for o in ("dst", "src")}
    k.ctl_free = {o: sb("ctl_free_" + o, [1, GROUPS], I32) for o in ("dst", "src")}
    k.mean_scale = sb("mean_scale", [P, TILES])
    k.dinv_w = sb("dinv_w", [P, TILES])
    k.dinv_c = sb("dinv_c", [P, TILES])

    k.table = [dram(f"table{n}", [NP, D]) for n in range(2)]
    k.agg = dram("agg", [NP + SPARE * P, D])
    k.agg_src = dram("agg_src", [NP + SPARE * P, ZW])
    k.z = dram("z", [NP, ZW])
    k.res = [dram(f"residual{n}", [NP, D]) for n in range(2)]
    k.elu_out = dram("elu_out", [NP, D])
    k.rec = {"dst": dram("rec_dst", [NP, 4]), "src": dram("rec_src", [NP, 2])}
    k.last_step_dram = dram("last_step", [2, 512])

    k.sp_dma = [sig(f"sp_dma{n}", 0) for n in range(RING)]
    k.pool_dma = [sig(f"pool_dma{n}", 0) for n in range(RING)]
    k.pool_pair = [sig(f"pool_pair{n}", 0) for n in range(2)]
    k.sp_second = [sig(f"sp_second{n}", 0) for n in range(RING)]
    k.sp_store = [sig(f"sp_store{n}", 0) for n in range(SPT // HALF)]
    k.act_store = [sig(f"act_store{n}", 0) for n in range(SPT // HALF)]
    k.dve_chain = sig("dve_chain")
    k.pool_pass, k.dve_pass, k.sp_pass = (ctx.enter_context(nc.semaphore(n)) for n in
                                          ("pool_pass", "dve_pass", "sp_pass"))
    k.s = Signals(sig)
    k.norm_signals = [[sig(f"{name}{n}") for n in range(2)] for name in
                      ("bn_ready", "stat_ready", "root_ready", "inverse_ready", "scaled_ready", "factors_ready")]
    return k


def constants_and_loads(k, ins):
    nc, s = k.nc, k.s
    wf = ins["L1_gnn_Wf"]
    loads = [(k.w["self0"][:, :], ins["L0_gnn_W_self0"]), (k.w["neigh0"][:, :], ins["L0_gnn_W_neigh0"]),
             (k.w["self1"][:, :], ins["L0_gnn_W_self1"]), (k.w["neigh1"][:, :], ins["L0_gnn_W_neigh1"]),
             (k.w["ni"][:, :], wf[0:P, :]), (k.w["nj"][:, :], wf[P:2 * P, :]),
             (k.wf_diff[:, :], wf[2 * P:3 * P, :]), (k.w["ea"][0:EF, :], wf[3 * P:3 * P + EF, :]),
             (k.w["q"][:, :], ins["L1_gnn_Wq"]), (k.w["k"][:, :], ins["L1_gnn_Wk"]),
             (k.w["u"][:, :], ins["L1_gnn_Wu"]), (k.w["gcn"][:, :], ins["L2_gnn_W"]),
             (k.w["g0"][:, :], ins["L3_gnn_W"][0]), (k.w["g1"][:, :], ins["L3_gnn_W"][1]),
             (k.w["g2"][:, :], ins["L3_gnn_W"][2]), (k.wa[:, :], ins["L1_gnn_Wa"]),
             (k.bf[:, :], ins["L1_gnn_bf"].rearrange("(d a) -> d a", a=1)),
             (k.bn_rows[:, 0, :], ins["L2_gnn_bn_gamma"].rearrange("(a d) -> a d", a=1)),
             (k.bn_rows[:, 1, :], ins["L2_gnn_bn_beta"].rearrange("(a d) -> a d", a=1))]
    biases = {"b0": ins["L0_gnn_b0"], "b1": ins["L0_gnn_b1"], "u": ins["L1_gnn_bu"], "gcn": ins["L2_gnn_b"],
              "ln_g": ins["L2_gnn_ln_gamma"], "ln_b": ins["L2_gnn_ln_beta"],
              "g0": ins["L3_gnn_b"][0], "g1": ins["L3_gnn_b"][1], "g2": ins["L3_gnn_b"][2]}
    for name, b in biases.items():
        loads.append((k.b[name][:, 0, :], b.partition_broadcast(P)))
    sp_loads = loads[len(k.act_store):]
    first = k.sp_store + k.sp_dma + k.sp_second
    sp_signals = first + [k.sp_second[n % RING] for n in range(len(sp_loads) - len(first))]
    for signal in k.act_store + sp_signals:
        signal.advance(16)
    with ExitStack() as ctx:
        lane_i = ctx.enter_context(nc.sbuf_tensor("lane_i", [P, P], I32))
        diff_i = ctx.enter_context(nc.sbuf_tensor("diff_i", [P, P], I32))
        made = ctx.enter_context(nc.semaphore("consts_made"))
        block = ctx.enter_context(nc.Block())

        @block.sync
        def _(sp):
            for signal, (to, of) in zip(sp_signals, sp_loads):
                sp.dma_start(to, of).then_inc(signal.sem, 16)
            for signal in first:
                sp.wait_ge(signal.sem, signal.base)

        @block.scalar
        def _(act):
            for signal, (to, of) in zip(k.act_store, loads):
                act.dma_start(to, of).then_inc(signal.sem, 16)
            for signal in k.act_store:
                act.wait_ge(signal.sem, signal.base)

        @block.gpsimd
        def _(pool):
            pool.iota(lane_i[:, :], pattern=[[1, P]], base=0, channel_multiplier=0).then_inc(made, 1)
            pool.iota(diff_i[:, :], pattern=[[1, P]], base=0, channel_multiplier=-1).then_inc(made, 1)
            for n, signal in enumerate(k.pool_dma + k.pool_pair):
                pool.dma_start(k.z[n * P:(n + 1) * P, 0:D], ins["x"][0:P, :]).then_inc(signal.sem, 16)
                signal.base = 16
            for signal in k.pool_dma + k.pool_pair:
                pool.wait_ge(signal.sem, 16)
            both = [signal for pair in k.norm_signals for signal in pair]
            for signal in k.s.all + both + [k.dve_chain]:
                pool.sem_inc(signal.sem, WARM)

        @block.vector
        def _(dve):
            dve.wait_ge(made, 2)
            dve.tensor_copy(k.iota[:, :], lane_i[:, :])
            dve.tensor_scalar(k.ident[:, :], diff_i[:, :], 0.0, None, ALU.is_equal)
            dve.memset(k.eps[:, :], EPS)
            for signal in first + k.act_store:
                dve.wait_ge(signal.sem, signal.base)
            for name in biases:
                for t in range(1, GT):
                    dve.tensor_copy(k.b[name][:, t, :], k.b[name][:, 0, :])
            dve.tensor_tensor(k.w["ni"][:, :], k.w["ni"][:, :], k.wf_diff[:, :], ALU.add)
            dve.tensor_tensor(k.w["nj"][:, :], k.w["nj"][:, :], k.wf_diff[:, :], ALU.subtract)


def prepare(k, ins):
    with ExitStack() as ctx:
        starts = {o: ctx.enter_context(k.nc.sbuf_tensor("starts_" + o, [P, TILES + 1], F32))
                  for o in ("src", "dst")}
        order_edges(k, ins, starts)
        for n, o in enumerate(("src", "dst")):
            plan_steps(k, n, o, starts[o])


def order_edges(k, ins, starts):
    nc, s = k.nc, k.s
    keys = ("src", "dst")
    with ExitStack() as ctx:
        def sb(name, shape, dt=F32):
            return ctx.enter_context(nc.sbuf_tensor(name, shape, dt))

        def sem(name):
            return ctx.enter_context(nc.semaphore(name))

        node_i = {"src": k.edge_src, "dst": k.edge_dst}
        tile_i = {o: sb(f"tile_i_{o}", [P, TILES], I32) for o in keys}
        tile_f = {o: sb(f"tile_f_{o}", [P, TILES]) for o in keys}
        lane_i = sb("lane_dst_i", [P, TILES], I32)
        lane_f = sb("lane_dst_f", [P, TILES])
        ew = sb("ew", [P, TILES])
        part_b = sb("part_b", [P, TILES], BF16)
        ew_part = [sb(f"ew_part{n}", [P, TILES]) for n in range(3)]
        rest = [sb(f"ew_rest{n}", [P, TILES]) for n in range(2)]
        bins_i = sb("bins_i", [P, TILES + 1], I32)
        edge_i = sb("edge_i", [P, TILES], I32)
        bins = sb("bins", [P, TILES + 1], F16)
        lanes = sb("lanes", [P, P], F16)
        tri_i = sb("tri_i", [P, P], I32)
        before = sb("before", [P, P], BF16)
        from_on = sb("from_on", [P, P], BF16)
        ones = sb("ones_b", [P, P], BF16)
        above = sb("above", [P, 4, TILES + 1], BF16)
        onehot = sb("onehot_tile", [P, 2, 2, TILES], BF16)
        lane_hot = sb("lane_hot", [P, 2, 4, P], BF16)
        products = sb("products", [P, 2, GT, TILES], BF16)
        rec = {"dst": sb("recs_dst", [P, TILES, 4]), "src": sb("recs_src", [P, TILES, 2])}
        pos = sb("pos", [P, 2, 2, GT])
        pos_i = sb("pos_i", [P, 2, 2, GT], I32)
        pos_t = sb("pos_t", [P, 2, 2, GT], I32)
        pos_l = sb("pos_l", [P, 2, 2, GT], I32)
        place = sb("place", [P, 2, 2, GT], I32)
        staged = {"dst": sb("staged_dst", [P, 2, GT, 4]), "src": sb("staged_src", [P, 2, GT, 2])}
        iotas, loaded, prepared = sem("iotas"), sem("loaded"), sem("prepared")
        above_ready, counted, starts_read = sem("above_ready"), sem("counted"), sem("starts_read")
        count_ps = {"src": k.ps[:, 0, 0:TILES + 1], "dst": k.ps[:, 1, 0:TILES + 1]}
        deg_ps = [k.ps[:, 2, 0:TILES], k.ps[:, 3, 0:TILES]]
        dve_per = 0
        with nc.Block() as block:
            @block.sync
            def _(sp):
                sp.dma_start(k.edge_src[:, 0:TILES], ins["src"].rearrange("(p t) -> p t", p=P)).then_inc(loaded, 16)
                sp.dma_start(k.edge_dst[:, 0:TILES], ins["dst"].rearrange("(p t) -> p t", p=P)).then_inc(loaded, 16)
                sp.dma_start(ew[:, :], ins["edge_weight"].rearrange("(p t) -> p t", p=P)).then_inc(loaded, 16)
                sp.wait_ge(loaded, 48)

            @block.gpsimd
            def _(pool):
                pool.iota(bins_i[:, :], pattern=[[1, TILES + 1]], base=0, channel_multiplier=0).then_inc(iotas, 1)
                pool.iota(tri_i[:, :], pattern=[[1, P]], base=0, channel_multiplier=-1).then_inc(iotas, 1)
                pool.iota(edge_i[:, :], pattern=[[1, TILES]], base=0, channel_multiplier=TILES).then_inc(iotas, 1)

            @block.vector
            def _(dve):
                c = Chain(k.dve_chain, dve)
                dve.wait_ge(iotas, 3)
                dve.tensor_copy(bins[:, :], bins_i[:, :])
                dve.tensor_copy(lanes[:, :], bins_i[:, 0:P])
                dve.tensor_scalar(before[:, :], tri_i[:, :], 0.0, None, ALU.is_gt)
                dve.tensor_scalar(from_on[:, :], tri_i[:, :], 0.0, None, ALU.is_le)
                dve.memset(ones[:, :], 1.0)
                dve.tensor_copy(rec["src"][:, :, 1], edge_i[:, :])
                dve.memset(rec["dst"][:, :, 3], 0.0)
                for o in keys:
                    dve.memset(node_i[o][:, TILES:], 0)
                dve.wait_ge(loaded, 48)
                for o in keys:
                    dve.tensor_scalar(tile_i[o][:, :], node_i[o][:, 0:TILES], 7, None, ALU.arith_shift_right)
                dve.tensor_scalar(lane_i[:, :], node_i["dst"][:, 0:TILES], 127, None, ALU.bitwise_and)
                dve.tensor_copy(rec["src"][:, :, 0], node_i["src"][:, 0:TILES])
                dve.tensor_copy(rec["dst"][:, :, 0], node_i["dst"][:, 0:TILES])
                dve.tensor_copy(rec["dst"][:, :, 1], node_i["src"][:, 0:TILES])
                c.mark(dve.tensor_copy(rec["dst"][:, :, 2], ew[:, :]))
                c.mark(dve.tensor_copy(part_b[:, :], ew[:, :]))
                c.wait()
                for o in keys:
                    dve.tensor_copy(tile_f[o][:, :], tile_i[o][:, :])
                dve.tensor_copy(lane_f[:, :], lane_i[:, :])
                c.mark(dve.tensor_copy(ew_part[0][:, :], part_b[:, :]))
                c.wait()
                c.mark(dve.tensor_tensor(rest[0][:, :], ew[:, :], ew_part[0][:, :], ALU.subtract))
                c.wait()
                c.mark(dve.tensor_copy(part_b[:, :], rest[0][:, :]))
                c.wait()
                c.mark(dve.tensor_copy(ew_part[1][:, :], part_b[:, :]))
                c.wait()
                c.mark(dve.tensor_tensor(rest[1][:, :], rest[0][:, :], ew_part[1][:, :], ALU.subtract))
                c.wait()
                c.mark(dve.tensor_copy(part_b[:, :], rest[1][:, :]))
                c.wait()
                ins_ = c.mark(dve.tensor_copy(ew_part[2][:, :], part_b[:, :]))
                c.wait()
                dve.sem_inc(prepared, 1)
                k.dve_chain.advance(c.n)

        with nc.Block() as block:
            @block.vector
            def _(dve):
                with dve.Fori(0, TILES // 2) as it:
                    for n in range(4):
                        o, t = keys[n % 2], it * 2 + n // 2
                        dve.wait_ge(s.step_done.sem, s.step_done.at(it * 4 + n - 3))
                        dve.tensor_scalar(above[:, n, :], bins[:, :], tile_f[o][:, bass.ds(t, 1)], None,
                                          ALU.is_gt).then_inc(s.onehot_ready.sem, 1)
                for n, o in enumerate(keys):
                    dve.wait_ge(s.step_done.sem, s.step_done.at(2 * TILES))
                    dve.tensor_copy(starts[o][:, :], count_ps[o])

            @block.tensor
            def _(pe):
                def count(it, n, first):
                    pe.wait_ge(s.onehot_ready.sem, s.onehot_ready.at(it * 4 + n + 1))
                    pe.matmul(count_ps[keys[n % 2]], ones[:, :], above[:, n, :], start=first, stop=True,
                              skip_group_check=True).then_inc(s.step_done.sem, 1)
                for n in range(4):
                    count(0, n, n < 2)
                with pe.Fori(1, TILES // 2) as it:
                    for n in range(4):
                        count(it, n, False)
            s.step_done.advance(2 * TILES)
            s.onehot_ready.advance(2 * TILES)

        hot_ready, lane_ready, ranks_ready = s.onehot_ready, s.part_ready, s.mm_done
        ranked, counted2, pos_done = s.acc_done, s.step_done, s.mm2_done
        with nc.Block() as block:
            @block.vector
            def _(dve):
                per = 6
                with dve.Fori(0, GROUPS // 2) as it:
                    for half in range(2):
                        g = it * 2 + half
                        c = Chain(k.dve_chain, dve, g, per)
                        for q in range(GT):
                            t, b = g * GT + q, q % 2
                            dve.wait_ge(counted2.sem, counted2.at(t - 1))
                            for n, o in enumerate(keys):
                                dve.tensor_scalar(onehot[:, b, n, :], bins[:, 0:TILES],
                                                  tile_f[o][:, bass.ds(t, 1)], None,
                                                  ALU.is_equal).then_inc(hot_ready.sem, 1)
                            dve.tensor_scalar(lane_hot[:, b, 0, :], lanes[:, :], lane_f[:, bass.ds(t, 1)], None,
                                              ALU.is_equal).then_inc(lane_ready.sem, 1)
                            for part in range(3):
                                dve.tensor_scalar(lane_hot[:, b, 1 + part, :], lanes[:, :],
                                                  lane_f[:, bass.ds(t, 1)], ew_part[part][:, bass.ds(t, 1)],
                                                  ALU.is_equal, ALU.mult).then_inc(lane_ready.sem, 1)
                            if q == 0:
                                dve.wait_ge(k.pool_pair[half].sem, k.pool_pair[half].at(it * 128))
                            for n, o in enumerate(keys):
                                dve.wait_ge(ranks_ready.sem, ranks_ready.at(t * 2 + n + 1))
                                ins_ = dve.tensor_tensor_reduce(
                                    products[:, n, q, :], onehot[:, b, n, :], count_ps[o][:, 0:TILES], 1.0, 0.0,
                                    ALU.mult, ALU.add, pos[:, half, n, q:q + 1])
                                ins_.then_inc(ranked.sem, 1)
                        dve.wait_ge(ranked.sem, ranked.at((g + 1) * GT * 2))
                        c.mark(dve.tensor_copy(pos_i[:, half, :, :], pos[:, half, :, :]))
                        c.wait()
                        c.mark(dve.tensor_scalar(pos_t[:, half, :, :], pos_i[:, half, :, :], 7, None,
                                                 ALU.arith_shift_right))
                        c.mark(dve.tensor_scalar(pos_l[:, half, :, :], pos_i[:, half, :, :], 127, None,
                                                 ALU.bitwise_and))
                        for o in keys:
                            c.mark(dve.tensor_copy(staged[o][:, half, :, :], rec[o][:, bass.ds(g * GT, GT), :]))
                        c.wait()
                        c.mark(dve.scalar_tensor_tensor(place[:, half, :, :], pos_l[:, half, :, :], float(TILES),
                                                        pos_t[:, half, :, :], ALU.mult, ALU.add))
                        assert c.n == per
                dve.wait_ge(counted2.sem, counted2.at(TILES))
                c = Chain(k.dve_chain, dve, GROUPS, per)
                c.mark(dve.tensor_scalar(k.mean_scale[:, :], deg_ps[0], 1.0, None, ALU.max))
                c.mark(dve.tensor_scalar(k.dinv_w[:, :], deg_ps[1], 1.0, None, ALU.add))
                c.mark(dve.tensor_scalar(k.dinv_c[:, :], deg_ps[0], 1.0, None, ALU.add))
                c.wait()
                dve.reciprocal(k.mean_scale[:, :], k.mean_scale[:, :])
                dve.reciprocal(k.dinv_w[:, :], k.dinv_w[:, :])
                c.mark(dve.reciprocal(k.dinv_c[:, :], k.dinv_c[:, :]))
                k.dve_end = k.dve_chain.at(GROUPS * per + c.n)
                k.dve_total = GROUPS * per + c.n

            @block.scalar
            def _(act):
                act.wait_ge(k.dve_chain.sem, k.dve_end)
                act.activation(k.dinv_w[:, :], k.dinv_w[:, :], ACT.Sqrt)
                act.activation(k.dinv_c[:, :], k.dinv_c[:, :], ACT.Sqrt)

            @block.tensor
            def _(pe):
                def tile(t, q, first):
                    b = q % 2
                    for n, o in enumerate(keys):
                        pe.wait_ge(hot_ready.sem, hot_ready.at(t * 2 + n + 1))
                        pe.matmul(count_ps[o][:, 0:TILES], before[:, :], onehot[:, b, n, :], start=False,
                                  stop=True, skip_group_check=True).then_inc(ranks_ready.sem, 1)
                    for part in range(4):
                        pe.wait_ge(lane_ready.sem, lane_ready.at(t * 4 + part + 1))
                        pe.matmul(deg_ps[min(part, 1)], lane_hot[:, b, part, :], onehot[:, b, 1, :],
                                  start=first and part < 2, stop=True, skip_group_check=True)
                    for n, o in enumerate(keys):
                        pe.wait_ge(ranked.sem, ranked.at(t * 2 + n + 1))
                        mm = pe.matmul(count_ps[o][:, 0:TILES], from_on[:, :], onehot[:, b, n, :], start=False,
                                       stop=True, skip_group_check=True)
                    mm.then_inc(counted2.sem, 1)
                for t in range(2):
                    tile(t, t, t == 0)
                with pe.Fori(1, TILES // 2) as it:
                    for q in range(2):
                        tile(it * 2 + q, q, False)

            @block.gpsimd
            def _(pool):
                with pool.Fori(0, GROUPS // 2) as it:
                    for half in range(2):
                        g = it * 2 + half
                        pool.wait_ge(k.dve_chain.sem, k.dve_chain.at(g * 6 + 6))
                        pool.sem_inc(k.pool_pass, 1)
                        for n, o in enumerate(keys):
                            for q in range(GT):
                                pool.indirect_dma_start(
                                    k.rec[o], bass.IndirectOffsetOnAxis(ap=place[:, half, n, q:q + 1], axis=0),
                                    staged[o][:, half, q, :], None).then_inc(k.pool_pair[half].sem, 16)
                for half in range(2):
                    pool.wait_ge(k.pool_pair[half].sem, k.pool_pair[half].at(128 * GROUPS // 2))
            for half in range(2):
                k.pool_pair[half].advance(128 * GROUPS // 2)
            k.dve_chain.advance(k.dve_total)
            hot_ready.advance(2 * TILES)
            lane_ready.advance(4 * TILES)
            ranks_ready.advance(2 * TILES)
            ranked.advance(2 * TILES)
            counted2.advance(TILES)


def plan_steps(k, number, o, starts):
    nc, s = k.nc, k.s
    with ExitStack() as ctx:
        def sb(name, shape, dt=F32):
            return ctx.enter_context(nc.sbuf_tensor(f"{name}_{o}", shape, dt))

        def sem(name):
            return ctx.enter_context(nc.semaphore(f"{name}_{o}"))

        width = 4 if o == "dst" else 2
        half = STEPS // 2
        recs = sb("sorted", [P, TILES, width])
        k_i, k_f = sb("k_i", [P, STEPS], I32), sb("k_f", [P, STEPS])
        thr_i = sb("thr_i", [P, 4], I32)
        thr = sb("thr", [P, 2, 4])
        junk = sb("junk_p", [P, TILES])
        last = sb("last", [P, 2, 4])
        index_i, index = sb("index_i", [P, 4], I32), sb("index", [P, 4])
        le = sb("le", [P, 4, STEPS])
        gt = sb("gt", [P, 4, STEPS])
        chosen = sb("chosen", [P, 4, STEPS])
        node_t = sb("node_t", [P, 4, P])
        w_t = sb("w_t", [P, 4, P])
        ones = sb("ones_f", [P, P])
        ik = sb("ik", [P, STEPS])
        jk = sb("jk", [P, STEPS])
        jk128 = sb("jk128", [P, STEPS])
        row = sb("row", [1, 6, STEPS])
        row_i = sb("row_i", [1, 3, STEPS], I32)
        ls_row = sb("ls_row", [1, 512])
        trash_i = sb("trash_i", [1, STEPS], I32)
        loaded, iotas, ready, transposed, copied = (sem(n) for n in ("recs", "iotas_p", "chosen_r", "trans", "copied"))
        summed, last_ready, last_out, last_in = (sem(n) for n in ("summed", "last_r", "last_out", "last_in"))
        cols = k.rel[o]
        values = [recs[:, :, 0]] + ([recs[:, :, 2]] if o == "dst" else [])
        with nc.Block() as block:
            @block.sync
            def _(sp):
                sp.dma_start(recs[:, :, :], k.rec[o].rearrange("(p t) c -> p t c", p=P)).then_inc(loaded, 16)
                sp.wait_ge(last_ready, 1)
                for c in range(4):
                    sp.dma_start(k.last_step_dram[number, c * P:(c + 1) * P].rearrange("(p a) -> p a", a=1),
                                 last[:, 0, c:c + 1]).then_inc(last_out, 16)
                sp.wait_ge(last_out, 64)
                sp.dma_start(ls_row[:, :], k.last_step_dram[number:number + 1, :]).then_inc(last_in, 16)
                sp.wait_ge(last_in, 16)
                sp.wait_ge(loaded, 16)

            @block.gpsimd
            def _(pool):
                pool.iota(k_i[:, :], pattern=[[1, STEPS]], base=0, channel_multiplier=0).then_inc(iotas, 1)
                pool.iota(thr_i[:, :], pattern=[[P * P, 4]], base=P - 1, channel_multiplier=P).then_inc(iotas, 1)
                pool.iota(index_i[:, :], pattern=[[P, 4]], base=0, channel_multiplier=1).then_inc(iotas, 1)
                pool.iota(trash_i[:, :], pattern=[[0, STEPS // SPARE], [1, SPARE]], base=TILES,
                          channel_multiplier=0).then_inc(iotas, 1)

            @block.vector
            def _(dve):
                c = Chain(k.dve_chain, dve)
                dve.wait_ge(iotas, 4)
                dve.tensor_copy(k_f[:, :], k_i[:, :])
                dve.tensor_copy(index[:, :], index_i[:, :])
                dve.memset(ones[:, :], 1.0)
                dve.memset(k.rel[o][:, STEPS:], -1.0)
                dve.memset(k.keep[o][:, STEPS:], 0.0)
                dve.memset(k.idx[o][:, TILES:], 0)
                if o == "dst":
                    dve.memset(k.weight[:, STEPS:], 0.0)
                c.mark(dve.tensor_copy(thr[:, 0, :], thr_i[:, :]))
                c.wait()
                c.mark(dve.tensor_scalar(thr[:, 1, :], thr[:, 0, :], -float(P), None, ALU.add))
                c.wait()
                for a in range(2):
                    for n in range(4):
                        c.mark(dve.tensor_scalar(junk[:, :], starts[:, 1:TILES + 1], thr[:, a, n:n + 1], 0.0,
                                                 ALU.is_le, ALU.add, accum_out=last[:, a, n:n + 1]))
                        c.wait()
                c.mark(dve.tensor_tensor(last[:, 0, :], last[:, 0, :], index[:, :], ALU.add))
                c.mark(dve.scalar_tensor_tensor(last[:, 1, :], last[:, 1, :], -1.0, index[:, :], ALU.add, ALU.add))
                c.wait()
                dve.sem_inc(last_ready, 1)
                for n, (_, size) in enumerate(CHUNKS):
                    dve.tensor_scalar(gt[:, n, :], k_f[:, :], last[:, 0, n:n + 1], None, ALU.is_gt)
                    c.mark(dve.tensor_scalar(le[:, n, :], k_f[:, :], last[:, 0, n:n + 1], None, ALU.is_le))
                    c.wait()
                    c.mark(dve.scalar_tensor_tensor(chosen[:, n, :], k_f[:, :], last[:, 1, n:n + 1], le[:, n, :],
                                                    ALU.is_gt, ALU.mult))
                c.wait()
                dve.sem_inc(ready, 1)
                dve.wait_ge(transposed, len(values))
                for v in range(len(values)):
                    for n, (_, size) in enumerate(CHUNKS):
                        to = (node_t, w_t)[v]
                        c.mark(dve.tensor_copy(to[0:size, n, :], k.ps[0:size, v, n * P:(n + 1) * P]))
                c.wait()
                dve.sem_inc(copied, 1)
                dve.wait_ge(summed, 1)
                for h in range(2):
                    c.mark(dve.tensor_copy(ik[:, h * half:(h + 1) * half], k.ps[:, 2 + h, 0:half]))
                c.wait()
                c.mark(dve.tensor_tensor(jk[:, :], k_f[:, :], ik[:, :], ALU.subtract))
                dve.memset(k.keep[o][:, 0:1], 0.0)
                dve.tensor_tensor(k.keep[o][:, 1:STEPS], ik[:, 1:], ik[:, 0:STEPS - 1], ALU.not_equal)
                dve.memset(row[:, 0, STEPS - 1:STEPS], 1.0)
                dve.tensor_tensor(row[:, 0, 0:STEPS - 1], ik[0:1, 1:], ik[0:1, 0:STEPS - 1], ALU.is_equal)
                dve.tensor_scalar(row[:, 1, :], ik[0:1, :], float(TILES - 1), None, ALU.min)
                c.mark(dve.tensor_copy(row[:, 2, :], trash_i[:, :]))
                c.wait()
                c.mark(dve.tensor_scalar(jk128[:, :], jk[:, :], float(P), None, ALU.mult))
                dve.tensor_tensor(row[:, 3, :], jk[0:1, :], row[:, 2, :], ALU.subtract)
                c.mark(dve.tensor_copy(row_i[:, 0, :], row[:, 1, :]))
                c.wait()
                for h in range(2):
                    cut = slice(h * half, (h + 1) * half)
                    dve.tensor_tensor(k.rel[o][:, cut], k.ps[:, 4 + h, 0:half], jk128[:, cut], ALU.subtract)
                    if o == "dst":
                        dve.tensor_copy(k.weight[:, cut], k.ps[:, 6 + h, 0:half])
                c.mark(dve.tensor_scalar(row_i[:, 2, :], row[:, 1, :], float(-(-65536 // SLOTS)), None, ALU.mult))
                c.wait()
                c.mark(dve.tensor_scalar(row_i[:, 2, :], row_i[:, 2, :], 16, None, ALU.arith_shift_right))
                c.wait()
                c.mark(dve.scalar_tensor_tensor(row_i[:, 2, :], row_i[:, 2, :], -float(SLOTS), row_i[:, 0, :],
                                                ALU.mult, ALU.add))
                c.wait()
                row_width = D if o == "dst" else ZW
                dve.tensor_scalar(k.ctl_slot[o][:, :], row_i[:, 2, :], float(row_width), None, ALU.mult)
                c.mark(dve.tensor_tensor(row[:, 4, :], row[:, 3, :], row[:, 0, :], ALU.mult))
                c.mark(dve.tensor_scalar(row_i[:, 1, :], row_i[:, 0, :], 2, None, ALU.arith_shift_right))
                c.wait()
                c.mark(dve.tensor_tensor(row[:, 5, :], row[:, 4, :], row[:, 2, :], ALU.add))
                dve.tensor_scalar(k.ctl_ready[o][:, :], row_i[:, 1, REGION - 1::REGION], 1.0 + LANDING, None,
                                  ALU.add)
                c.wait()
                for parity in range(2):
                    dve.tensor_scalar(k.ctl_out[o][:, parity, :], row[:, 5, parity::2], float(P), None, ALU.mult)
                dve.wait_ge(last_in, 16)
                lag = SLOTS // GT
                dve.memset(k.ctl_free[o][:, 0:lag], 0)
                dve.tensor_scalar(k.ctl_free[o][:, lag:], ls_row[:, GT - 1:(GROUPS - lag) * GT:GT], 1.0, None,
                                  ALU.add)
                dve.wait_ge(loaded, 16)
                dve.tensor_copy(k.idx[o][:, 0:TILES], recs[:, :, 1])
                k.dve_chain.advance(c.n)

            @block.tensor
            def _(pe):
                pe.wait_ge(loaded, 16)
                for v, value in enumerate(values):
                    for n, (first, size) in enumerate(CHUNKS):
                        mm = pe.transpose(k.ps[0:size, v, n * P:(n + 1) * P], value[:, first:first + size],
                                          k.ident[:, :])
                    mm.then_inc(transposed, 1)
                pe.wait_ge(ready, 1)
                pe.wait_ge(copied, 1)
                for h in range(2):
                    cut = slice(h * half, (h + 1) * half)
                    jobs = [(2, ones, gt), (4, node_t, chosen)] + ([(6, w_t, chosen)] if o == "dst" else [])
                    for bank, lhs, rhs in jobs:
                        for n, (_, size) in enumerate(CHUNKS):
                            l = ones[0:size, :] if lhs is ones else lhs[0:size, n, :]
                            mm = pe.matmul(k.ps[:, bank + h, 0:half], l, rhs[0:size, n, cut],
                                           start=(n == 0), stop=(n == len(CHUNKS) - 1))
                mm.then_inc(summed, 1)


def level(k, pool, signals):
    top = max(signal.base for signal in signals)
    for signal in signals:
        if signal.base < top:
            pool.sem_inc(signal.sem, top - signal.base)
            signal.base = top
    return top


def sum_over_nodes(k, o, table, width, out, weighted=False):
    nc, s = k.nc, k.s
    cols = D if width == D else D + 1
    turns = STEPS // SPT
    counted = (s.onehot_ready, s.step_done, s.acc_done)
    top = max(signal.base for signal in counted)
    with ExitStack() as ctx:
        def sb(name, shape, dt=F32):
            return ctx.enter_context(nc.sbuf_tensor(k.name(name), shape, dt))

        ring = sb("ring", [P, SLOTS * width])
        acc = sb("acc", [P, SPT, width])
        hot = sb("hot", [P, 2 * HALF, P])
        staged = sb("staged", [P, 2, SLOTS], I32)
        rel, keep = sb("rel_now", [P, SPT]), sb("keep_now", [P, SPT])
        weight = sb("weight_now", [P, SPT])
        block = ctx.enter_context(nc.Block())

        @block.gpsimd
        def _(pool):
            level(k, pool, counted)

            def stage(turn, b):
                pool.tensor_copy(staged[:, b, :], k.idx[o][:, bass.ds(turn * SLOTS, SLOTS)]
                                 ).then_inc(s.idx_staged.sem, 1)

            def announce(rounds, r):
                pool.wait_ge(k.pool_dma[r].sem, k.pool_dma[r].at(rounds * (GT * 16)))
                pool.sem_inc(s.tiles_ready.sem, 1)

            stage(0, 0)
            with pool.Fori(0, GROUPS // RING // 2) as pair:
                for b in range(2):
                    it = pair * 2 + b
                    for r in range(RING):
                        g = it * RING + r
                        free = pool.value_load(k.ctl_free[o][0:1, bass.ds(g, 1)], min_val=0, max_val=STEPS)
                        announce(it + (1 if r >= LANDING else 0), (r - LANDING) % RING)
                        if r == LANDING:
                            stage(it + 1, 1 - b)
                        if r == 0:
                            pool.wait_ge(s.idx_staged.sem, s.idx_staged.at(it + 1))
                            pool.sem_inc(k.pool_pass, 1)
                        pool.wait_ge(s.step_done.sem, s.step_done.at(free))
                        pool.sem_inc(k.pool_pass, 1)
                        for q in range(r * GT, (r + 1) * GT):
                            pool.indirect_dma_start(
                                ring[:, q * width:(q + 1) * width], None, table,
                                bass.IndirectOffsetOnAxis(ap=staged[:, b, q:q + 1], axis=0)
                            ).then_inc(k.pool_dma[r].sem, 16)
            for r in range(RING - LANDING, RING):
                announce(GROUPS // RING, r)

        @block.vector
        def _(dve):
            def onehots(half, staged_count, done):
                if staged_count is not None:
                    dve.wait_ge(s.cols_staged.sem, staged_count)
                dve.wait_ge(s.step_done.sem, done)
                for n in range(HALF):
                    q = (half * HALF + n) % SPT
                    scale = (weight[:, q:q + 1], ALU.mult) if weighted else (None, ALU.bypass)
                    dve.tensor_scalar(hot[:, q % (2 * HALF), :], k.iota[:, :], rel[:, q:q + 1], scale[0],
                                      ALU.is_equal, scale[1]).then_inc(s.onehot_ready.sem, 1)

            dve.memset(acc[:, SPT - 1, :], 0.0)
            onehots(0, s.cols_staged.at(1), top)
            with dve.Fori(0, turns) as it:
                now = dve.snap(it * SPT + top)
                count = [dve.snap(now + q) if q else now for q in range(SPT + 1)]
                regions = dve.snap(it * 2 + s.cols_staged.base)
                stored = dve.snap(it * (HALF // 2 * 16) + k.sp_store[0].base)
                for half in range(SPT // HALF):
                    region = {1: 2, 3: 3}.get(half)
                    onehots(half + 1, regions + region if region else None, count[half * HALF])
                    dve.wait_ge(k.sp_store[half].sem, stored)
                    dve.wait_ge(k.act_store[half].sem, stored)
                    for n in range(HALF):
                        q = half * HALF + n
                        dve.wait_ge(s.step_done.sem, count[q + 1])
                        dve.wait_ge(s.acc_done.sem, count[q])
                        dve.scalar_tensor_tensor(acc[:, q, 0:cols], acc[:, (q - 1) % SPT, 0:cols],
                                                 keep[:, q:q + 1], k.ps[:, q % 8, 0:cols],
                                                 ALU.mult, ALU.add).then_inc(s.acc_done.sem, 1)

        @block.tensor
        def _(pe):
            with pe.Fori(0, turns * 2) as m:
                now = pe.snap(m * REGION + top)
                need = pe.value_load(k.ctl_ready[o][0:1, bass.ds(m, 1)], min_val=1, max_val=GROUPS + LANDING)
                places = nc.values_load_multi_w_load_instructions(
                    k.ctl_slot[o][0:1, bass.ds(m * REGION, REGION)], engines=[pe.engine], min_val=0,
                    max_val=(SLOTS - 1) * width, skip_runtime_bounds_check_because="worked out by plan_steps")[1]
                pe.wait_ge(s.tiles_ready.sem, s.tiles_ready.at(need))
                for q in range(REGION):
                    if q % HALF == 0:
                        pe.wait_ge(s.onehot_ready.sem, now + (q + HALF))
                        pe.wait_ge(s.acc_done.sem, now + (q - HALF))
                    pe.matmul(k.ps[:, q, 0:cols], hot[:, q, :], ring[:, bass.ds(places[q], cols)],
                              start=True, stop=True).then_inc(s.step_done.sem, 1)

        @block.sync
        def _(sp):
            with sp.Fori(0, turns) as it:
                now = sp.snap(it * SPT + top)
                for region in range(2):
                    rows_to = nc.values_load_multi_w_load_instructions(
                        k.ctl_out[o][0:1, 0, bass.ds((it * 2 + region) * HALF, HALF)], engines=[sp.engine],
                        min_val=0, max_val=NP + SPARE * P - P, skip_runtime_bounds_check_because="worked out by plan_steps")[1]
                    for n, to in enumerate(rows_to):
                        q = region * REGION + 2 * n
                        sp.wait_ge(s.acc_done.sem, now + (q + 1))
                        sp.sem_inc(k.sp_pass, 1)
                        sp.dma_start(out[bass.ds(to, P), 0:cols], acc[:, q, 0:cols]
                                     ).then_inc(k.sp_store[q // HALF].sem, 16)
            for half in range(SPT // HALF):
                sp.wait_ge(k.sp_store[half].sem, k.sp_store[half].at(turns * (HALF // 2 * 16)))

        @block.scalar
        def _(act):
            def stage_columns(step, region):
                cut = slice(region * REGION, (region + 1) * REGION)
                act.copy(rel[:, cut], k.rel[o][:, bass.ds(step, REGION)])
                if weighted:
                    act.copy(weight[:, cut], k.weight[:, bass.ds(step, REGION)])
                act.copy(keep[:, cut], k.keep[o][:, bass.ds(step, REGION)]).then_inc(s.cols_staged.sem, 1)

            for region in range(2):
                stage_columns(region * REGION, region)
            with act.Fori(0, turns) as it:
                now = act.snap(it * SPT + top)
                for region in range(2):
                    rows_to = nc.values_load_multi_w_load_instructions(
                        k.ctl_out[o][0:1, 1, bass.ds((it * 2 + region) * HALF, HALF)], engines=[act.engine],
                        min_val=0, max_val=NP + SPARE * P - P, skip_runtime_bounds_check_because="worked out by plan_steps")[1]
                    for n, to in enumerate(rows_to):
                        q = region * REGION + 2 * n + 1
                        act.wait_ge(s.acc_done.sem, now + (q + 1))
                        act.dma_start(out[bass.ds(to, P), 0:cols], acc[:, q, 0:cols]
                                      ).then_inc(k.act_store[q // HALF].sem, 16)
                    stage_columns((it + 1) * SPT + region * REGION, region)
            for half in range(SPT // HALF):
                act.wait_ge(k.act_store[half].sem, k.act_store[half].at(turns * (HALF // 2 * 16)))

        for r in range(RING):
            k.pool_dma[r].advance(GT * 16 * (GROUPS // RING))
        for half in range(SPT // HALF):
            k.sp_store[half].advance(turns * (HALF // 2 * 16))
            k.act_store[half].advance(turns * (HALF // 2 * 16))
        s.idx_staged.advance(GROUPS // RING + 1)
        s.cols_staged.advance(2 * turns + 2)
        s.tiles_ready.advance(GROUPS + LANDING)
        s.onehot_ready.advance(STEPS + HALF)
        s.step_done.advance(STEPS)
        s.acc_done.advance(STEPS)


class Turn:

    def __init__(self, loop, g, r, it, n):
        self.loop, self.g, self.r, self.it, self.n = loop, g, r, it, n

    @property
    def b(self):
        return self.r % 2

    @property
    def done(self):
        return self.loop.count(self.n + 1)

    @property
    def prior(self):
        return self.loop.count(self.n)

    @property
    def free(self):
        return self.loop.count(self.n if self.r == 0 else self.n - 1)

    def landed(self, dmas):
        return self.loop.rounds(self.loop.k.sp_dma[self.r].base, dmas, (self.n - self.r) // RING + 1)

    def gathered(self, dmas):
        return self.loop.rounds(self.loop.k.pool_dma[self.r].base, dmas, (self.n - self.r) // RING + 1)

    def rounds_of(self, signals, dmas):
        return self.loop.rounds(signals[self.r].base, dmas, (self.n - self.r) // RING)

    def stored(self, dmas):
        return self.loop.rounds(self.loop.k.pool_dma[self.r].base, dmas, (self.n - self.r) // RING)


class Round:

    def __init__(self, k, eng, it):
        self.k, self.eng, self.it, self.known = k, eng, it, {}

    def value(self, key, make):
        if isinstance(self.it, int):
            return make()
        if key not in self.known:
            self.known[key] = self.eng.snap(make())
        return self.known[key]

    def count(self, n):
        first = self.value("first", lambda: self.it * RING + self.k.top)
        return first if n == 0 else self.value(n, lambda: first + n)

    def rounds(self, base, dmas, more):
        return self.value((base, dmas, more), lambda: (self.it + more) * (16 * dmas) + base)


def by_groups(k, eng, *parts):
    def turn(loop, r, ends):
        for lag, part in parts:
            n = r - lag
            if not ends or 0 <= loop.it * RING + n < GROUPS:
                part(Turn(loop, loop.it * RING + n, n % RING, loop.it + n // RING, n))
    first = Round(k, eng, 0)
    for r in range(RING):
        turn(first, r, True)
    with eng.Fori(1, GROUPS // RING) as it:
        loop = Round(k, eng, it)
        for r in range(RING):
            turn(loop, r, False)
    end = Round(k, eng, GROUPS // RING)
    for r in range(max(lag for lag, _ in parts)):
        turn(end, r, True)


def node_pass(k, loads, stores, engines, tallies):
    nc, s = k.nc, k.s
    counted = k.s.all + [signal for pair in k.norm_signals for signal in pair]
    k.top = max(signal.base for signal in counted)
    with nc.Block() as block:
        @block.sync
        def _(sp):
            def body(t):
                sp.wait_ge(k.pool_dma[t.r].sem, t.stored(len(stores)))
                sp.sem_inc(k.sp_pass, 1)
                for buf, table, *cols in loads:
                    c = cols[0] if cols else D
                    sp.dma_start(buf[:, t.r, :, 0:c], rows(table, t.g * GT, GT)[:, :, 0:c]
                                 ).then_inc(k.sp_dma[t.r].sem, 16)
            by_groups(k, sp, (0, body))

        @block.gpsimd
        def _(pool):
            level(k, pool, counted)

            def body(t):
                pool.wait_ge(s.out_ready.sem, t.done)
                pool.sem_inc(k.pool_pass, 1)
                for buf, table in stores:
                    pool.dma_start(rows(table, t.g * GT, GT), buf[:, t.r]).then_inc(k.pool_dma[t.r].sem, 16)
            by_groups(k, pool, (0, body))
            for r in range(RING):
                pool.wait_ge(k.pool_dma[r].sem, k.pool_dma[r].at(16 * len(stores) * (GROUPS // RING)))

        if "tensor" in engines:
            block.tensor(engines["tensor"])
        block.vector(engines["vector"])
        block.scalar(engines["scalar"])
    for r in range(RING):
        k.sp_dma[r].advance(16 * len(loads) * (GROUPS // RING))
        k.pool_dma[r].advance(16 * len(stores) * (GROUPS // RING))
    for signal, n in tallies:
        signal.advance(n * GROUPS)


class Norm:

    def __init__(self, k, ctx, number=0):
        self.k = k
        self.bn, self.stat, self.root_sig, self.inverse, self.scaled, self.factor = (x[number] for x in k.norm_signals)

        def sb(name, shape):
            return ctx.enter_context(k.nc.sbuf_tensor(k.name(name), shape, F32))
        self.stats, self.mv = sb("bn_stats", [P, RING, GT, 6]), sb("mean_var", [P, RING, GT, 2])
        self.root, self.scale = sb("root", [P, RING, GT]), sb("rstd", [P, RING, GT])
        self.shift = sb("shift", [P, RING, GT])

    def statistics(self, dve, x, t):
        for q in range(GT):
            ins = dve.bn_stats(self.stats[:, t.r, q, :], x[:, t.r, q, :])
        ins.then_inc(self.bn.sem, 1)
        dve.wait_ge(self.bn.sem, t.done)
        dve.sem_inc(self.k.dve_pass, 1)
        for q in range(GT):
            ins = dve.bn_aggr(self.mv[:, t.r, q, :], self.stats[:, t.r, q, :])
        ins.then_inc(self.stat.sem, 1)

    def square_root(self, act, t):
        act.wait_ge(self.stat.sem, t.done)
        act.activation(self.root[:, t.r, :], self.mv[:, t.r, :, 1], ACT.Sqrt,
                       bias=self.k.eps[:, 0:1]).then_inc(self.root_sig.sem, 1)

    def factors(self, dve, t, extra=None):
        dve.wait_ge(self.root_sig.sem, t.done)
        dve.reciprocal(self.scale[:, t.r, :], self.root[:, t.r, :]).then_inc(self.inverse.sem, 1)
        dve.wait_ge(self.inverse.sem, t.done)
        if extra is not None:
            dve.tensor_tensor(self.scale[:, t.r, :], self.scale[:, t.r, :], extra, ALU.mult
                              ).then_inc(self.scaled.sem, 1)
            dve.wait_ge(self.scaled.sem, t.done)
        dve.scalar_tensor_tensor(self.shift[:, t.r, :], self.mv[:, t.r, :, 0], -1.0, self.scale[:, t.r, :],
                                 ALU.mult, ALU.mult).then_inc(self.factor.sem, 1)

    def apply(self, act, t, out, x, func):
        act.wait_ge(self.factor.sem, t.done)
        for q in range(GT):
            ins = act.activation(out[:, t.r, q, :], x[:, t.r, q, :], func, bias=self.shift[:, t.r, q:q + 1],
                                 scale=self.scale[:, t.r, q:q + 1])
        return ins

    def tallies(self, extra=False):
        return [(x, 1) for x in (self.bn, self.stat, self.root_sig, self.inverse, self.factor)
                + ((self.scaled,) if extra else ())]


def ring_buffer(k, ctx, name, width=D):
    return ctx.enter_context(k.nc.sbuf_tensor(k.name(name), [P, RING, GT, width], F32))


def pair_buffer(k, ctx, name):
    return ctx.enter_context(k.nc.sbuf_tensor(k.name(name), [P, 2, GT, D], F32))


def bank(k, n):
    return k.ps[:, n, :].rearrange("p (t d) -> p t d", t=GT)


def norm_pass(k, x, out):
    s = k.s
    with ExitStack() as ctx:
        xb, hb = ring_buffer(k, ctx, "x"), ring_buffer(k, ctx, "h")
        norm = Norm(k, ctx)

        def vector(dve):
            def stats(t):
                dve.wait_ge(k.sp_dma[t.r].sem, t.landed(1))
                norm.statistics(dve, xb, t)

            def factors(t):
                norm.factors(dve, t)
            by_groups(k, dve, (1, factors), (0, stats))

        def scalar(act):
            def apply(t):
                norm.apply(act, t, hb, xb, ACT.Relu).then_inc(s.out_ready.sem, 1)
            by_groups(k, act, (1, lambda t: norm.square_root(act, t)), (2, apply))

        node_pass(k, [(xb, x)], [(hb, out)], {"vector": vector, "scalar": scalar},
                  [(s.out_ready, 1)] + norm.tallies())


def sage_pass(k, h, w_self, w_neigh, bias, out, x=None, x_out=None):
    s = k.s
    with ExitStack() as ctx:
        hb, ab = ring_buffer(k, ctx, "h"), ring_buffer(k, ctx, "agg")
        yb, ob = ring_buffer(k, ctx, "y"), ring_buffer(k, ctx, "out")
        xb = ring_buffer(k, ctx, "x") if x is not None else None
        mean = pair_buffer(k, ctx, "mean")
        h_t, a_t = pair_buffer(k, ctx, "h_t"), pair_buffer(k, ctx, "mean_t")
        norm = Norm(k, ctx)
        loads = [(hb, h), (ab, k.agg)] + ([(xb, x)] if x is not None else [])
        stores = [(ob, out)] + ([(yb, x_out)] if x is not None else [])

        def landed(eng, t):
            eng.wait_ge(k.sp_dma[t.r].sem, t.landed(len(loads)))

        def scalar(act):
            def means(t):
                b = t.b
                landed(act, t)
                act.wait_ge(s.h_t.sem, t.free)
                for q in range(GT):
                    ins = act.activation(mean[:, b, q, :], ab[:, t.r, q, :], ACT.Copy,
                                         scale=k.mean_scale[:, bass.ds(t.g * GT + q, 1)])
                ins.then_inc(s.part_ready.sem, 1)

            def copy(t):
                b = t.b
                act.wait_ge(s.in_t.sem, t.done)
                act.wait_ge(s.mm_done.sem, t.free)
                act.copy(h_t[:, b], bank(k, b)).then_inc(s.in_copied.sem, 1)

            def relu(t):
                act.wait_ge(s.mm_read.sem, t.done)
                act.activation(ob[:, t.r], yb[:, t.r], ACT.Relu).then_inc(s.out_ready.sem, 1)

            def normed(t):
                norm.apply(act, t, ob, yb, ACT.Relu).then_inc(s.out_ready.sem, 1)
            if x is None:
                by_groups(k, act, (0, means), (1, copy), (3, relu))
            else:
                by_groups(k, act, (3, lambda t: norm.square_root(act, t)), (0, means), (1, copy), (3, normed))

        def tensor(pe):
            def turn(t):
                b = t.b
                landed(pe, t)
                pe.wait_ge(s.in_copied.sem, t.free)
                for q in range(GT):
                    mm = pe.transpose(bank(k, b)[:, q, :], hb[:, t.r, q, :], k.ident[:, :])
                mm.then_inc(s.in_t.sem, 1)
                pe.wait_ge(s.part_ready.sem, t.done)
                pe.wait_ge(s.h_copied.sem, t.free)
                for q in range(GT):
                    mm = pe.transpose(bank(k, 2 + b)[:, q, :], mean[:, b, q, :], k.ident[:, :])
                mm.then_inc(s.h_t.sem, 1)

            def multiply(t):
                b = t.b
                pe.wait_ge(s.in_copied.sem, t.done)
                pe.wait_ge(s.h_copied.sem, t.done)
                pe.wait_ge(s.mm_read.sem, t.free)
                for q in range(GT):
                    pe.matmul(bank(k, 4 + b)[:, q, :], h_t[:, b, q, :], w_self[:, :], start=True, stop=False)
                    mm = pe.matmul(bank(k, 4 + b)[:, q, :], a_t[:, b, q, :], w_neigh[:, :],
                                   start=False, stop=True)
                mm.then_inc(s.mm_done.sem, 1)
            by_groups(k, pe, (1, turn), (2, multiply))

        def vector(dve):
            def copy(t):
                b = t.b
                dve.wait_ge(s.h_t.sem, t.done)
                dve.wait_ge(s.mm_done.sem, t.free)
                dve.tensor_copy(a_t[:, b], bank(k, 2 + b)).then_inc(s.h_copied.sem, 1)

            def add(t):
                b = t.b
                dve.wait_ge(s.mm_done.sem, t.done)
                dve.tensor_tensor(yb[:, t.r], bank(k, 4 + b), bias[:, :, :], ALU.add).then_inc(s.mm_read.sem, 1)
                if x is not None:
                    landed(dve, t)
                    dve.wait_ge(s.mm_read.sem, t.done)
                    dve.tensor_tensor(yb[:, t.r], yb[:, t.r], xb[:, t.r], ALU.add).then_inc(s.x_ready.sem, 1)
                    dve.wait_ge(s.x_ready.sem, t.done)
                    norm.statistics(dve, yb, t)

            def factors(t):
                norm.factors(dve, t)
            if x is None:
                by_groups(k, dve, (1, copy), (2, add))
            else:
                by_groups(k, dve, (3, factors), (1, copy), (2, add))

        node_pass(k, loads, stores, {"vector": vector, "scalar": scalar, "tensor": tensor},
                  [(s.out_ready, 1), (s.h_t, 1), (s.part_ready, 1), (s.in_t, 1),
                   (s.mm_done, 1), (s.in_copied, 1), (s.h_copied, 1), (s.mm_read, 1)]
                  + (norm.tallies() + [(s.x_ready, 1)] if x is not None else []))


def attention_pass(k, h, x, x_out, out):
    s = k.s
    with ExitStack() as ctx:
        hb, ab = ring_buffer(k, ctx, "h"), ring_buffer(k, ctx, "agg", ZW)
        xb, yb, ob = (ring_buffer(k, ctx, n) for n in ("x", "y", "out"))
        h_t, n_t = pair_buffer(k, ctx, "h_t"), pair_buffer(k, ctx, "n_t")
        den = ctx.enter_context(k.nc.sbuf_tensor(k.name("den"), [P, RING, GT], F32))
        nb = hb
        norm = Norm(k, ctx)
        loads = [(hb, h), (ab, k.agg_src, D + 1), (xb, x)]

        def landed(eng, t):
            eng.wait_ge(k.sp_dma[t.r].sem, t.landed(len(loads)))

        def scalar(act):
            def first(t):
                b = t.b
                landed(act, t)
                act.activation(den[:, t.r, :], ab[:, t.r, :, D], ACT.Exp).then_inc(s.exp_ready.sem, 1)
                act.wait_ge(s.in_t.sem, t.done)
                act.wait_ge(s.mm_done.sem, t.free)
                act.copy(h_t[:, b], bank(k, b)).then_inc(s.in_copied.sem, 1)

            def normed(t):
                norm.apply(act, t, nb, yb, ACT.Relu).then_inc(s.h_ready.sem, 1)

            def stored(t):
                act.wait_ge(s.mm2_done.sem, t.done)
                act.copy(ob[:, t.r], bank(k, 6 + t.b)).then_inc(s.out_ready.sem, 1)
            by_groups(k, act, (2, lambda t: norm.square_root(act, t)), (5, stored), (2, normed), (0, first))

        def tensor(pe):
            def turn(t):
                b = t.b
                landed(pe, t)
                pe.wait_ge(s.in_copied.sem, t.free)
                for q in range(GT):
                    mm = pe.transpose(bank(k, b)[:, q, :], hb[:, t.r, q, :], k.ident[:, :])
                mm.then_inc(s.in_t.sem, 1)

            def multiply(t):
                b = t.b
                pe.wait_ge(s.in_copied.sem, t.done)
                pe.wait_ge(s.mm_read.sem, t.free)
                for q in range(GT):
                    mm = pe.matmul(bank(k, 4 + b)[:, q, :], h_t[:, b, q, :], k.w["u"][:, :],
                                   start=True, stop=True)
                mm.then_inc(s.mm_done.sem, 1)

            def turn_normed(t):
                b = t.b
                pe.wait_ge(s.h_ready.sem, t.done)
                pe.wait_ge(s.h_copied.sem, t.free)
                for q in range(GT):
                    mm = pe.transpose(bank(k, 2 + b)[:, q, :], nb[:, t.r, q, :], k.ident[:, :])
                mm.then_inc(s.h_t.sem, 1)

            def multiply_normed(t):
                b = t.b
                pe.wait_ge(s.h_copied.sem, t.done)
                pe.wait_ge(s.out_ready.sem, t.free)
                for q in range(GT):
                    mm = pe.matmul(bank(k, 6 + b)[:, q, :], n_t[:, b, q, :], k.w["gcn"][:, :],
                                   start=True, stop=True)
                mm.then_inc(s.mm2_done.sem, 1)
            by_groups(k, pe, (0, turn), (1, multiply), (3, turn_normed), (4, multiply_normed))

        def vector(dve):
            def add(t):
                b = t.b
                dve.wait_ge(s.exp_ready.sem, t.done)
                dve.reciprocal(den[:, t.r, :], den[:, t.r, :]).then_inc(s.first_add.sem, 1)
                dve.wait_ge(s.mm_done.sem, t.done)
                dve.tensor_tensor(yb[:, t.r], bank(k, 4 + b), k.b["u"][:, :, :], ALU.add
                                  ).then_inc(s.mm_read.sem, 1)
                landed(dve, t)
                dve.wait_ge(s.first_add.sem, t.done)
                for q in range(GT):
                    ins = dve.scalar_tensor_tensor(xb[:, t.r, q, :], ab[:, t.r, q, 0:D], den[:, t.r, q:q + 1],
                                                   xb[:, t.r, q, :], ALU.mult, ALU.add)
                ins.then_inc(s.second_add.sem, 1)
                dve.wait_ge(s.mm_read.sem, t.done)
                dve.wait_ge(s.second_add.sem, t.done)
                dve.tensor_tensor(yb[:, t.r], yb[:, t.r], xb[:, t.r], ALU.add).then_inc(s.x_ready.sem, 1)
                dve.wait_ge(s.x_ready.sem, t.done)
                norm.statistics(dve, yb, t)

            def factors(t):
                norm.factors(dve, t, k.dinv_w[:, bass.ds(t.g * GT, GT)])

            def copy(t):
                b = t.b
                dve.wait_ge(s.h_t.sem, t.done)
                dve.wait_ge(s.mm2_done.sem, t.free)
                dve.tensor_copy(n_t[:, b], bank(k, 2 + b)).then_inc(s.h_copied.sem, 1)
            by_groups(k, dve, (2, factors), (1, add), (3, copy))

        node_pass(k, loads, [(ob, out), (yb, x_out)], {"vector": vector, "scalar": scalar, "tensor": tensor},
                  [(s.out_ready, 1), (s.h_t, 1), (s.in_t, 1), (s.mm_done, 1), (s.in_copied, 1),
                   (s.h_copied, 1), (s.mm_read, 1), (s.x_ready, 1), (s.exp_ready, 1), (s.h_ready, 1),
                   (s.mm2_done, 1), (s.first_add, 1), (s.second_add, 1)] + norm.tallies(extra=True))


def elu_pass(k, table, out):
    s, nc = k.s, k.nc
    with ExitStack() as ctx:
        ab, tb = ring_buffer(k, ctx, "agg"), ring_buffer(k, ctx, "own")
        eb, qb = ring_buffer(k, ctx, "exp"), ring_buffer(k, ctx, "square")
        ones = ctx.enter_context(nc.sbuf_tensor("ones_col", [P, 1], F32))
        ones_ready = ctx.enter_context(nc.semaphore("ones_col_ready"))

        def vector(dve):
            dve.memset(ones[:, :], 1.0).then_inc(ones_ready, 1)

            def first(t):
                dve.wait_ge(k.sp_dma[t.r].sem, t.landed(2))
                dve.tensor_tensor(ab[:, t.r], ab[:, t.r], tb[:, t.r], ALU.add).then_inc(s.first_add.sem, 1)
                dve.wait_ge(s.first_add.sem, t.done)
                for q in range(GT):
                    ins = dve.scalar_tensor_tensor(tb[:, t.r, q, :], ab[:, t.r, q, :],
                                                   k.dinv_w[:, bass.ds(t.g * GT + q, 1)], k.b["gcn"][:, q, :],
                                                   ALU.mult, ALU.add)
                ins.then_inc(s.x_ready.sem, 1)

            def second(t):
                dve.wait_ge(s.exp_ready.sem, t.done)
                dve.tensor_scalar(eb[:, t.r], eb[:, t.r], 1.0, -1.0, ALU.min, ALU.add).then_inc(s.second_add.sem, 1)
                dve.wait_ge(s.second_add.sem, t.done)
                dve.tensor_tensor(eb[:, t.r], eb[:, t.r], tb[:, t.r], ALU.max).then_inc(s.h_ready.sem, 1)
            by_groups(k, dve, (2, second), (0, first))

        def scalar(act):
            def exponential(t):
                act.wait_ge(s.x_ready.sem, t.done)
                act.activation(eb[:, t.r], tb[:, t.r], ACT.Exp).then_inc(s.exp_ready.sem, 1)

            def square(t):
                act.wait_ge(s.h_ready.sem, t.done)
                act.activation(qb[:, t.r], eb[:, t.r], ACT.Square).then_inc(s.part_ready.sem, 1)
            by_groups(k, act, (1, exponential), (3, square))

        def tensor(pe):
            pe.wait_ge(ones_ready, 1)

            def total(t):
                pe.wait_ge(s.part_ready.sem, t.done)
                first = isinstance(t.g, int) and t.g == 0
                for n, buf in enumerate((eb, qb)):
                    mm = pe.matmul(k.ps[0:1, n, :], ones[:, :], buf[:, t.r].rearrange("p t d -> p (t d)"),
                                   start=first, stop=True, skip_group_check=True)
                mm.then_inc(s.out_ready.sem, 1)

            def tail(t):
                pe.wait_ge(s.part_ready.sem, t.done)
                for n, buf in enumerate((eb, qb)):
                    for q in range(GT):
                        real = min(P, N_REAL - (t.g * GT + q) * P)
                        if real > 0:
                            mm = pe.matmul(k.ps[0:1, n, q * P:(q + 1) * P], ones[0:real, :], buf[0:real, t.r, q, :],
                                           start=False, stop=True, skip_group_check=True)
                mm.then_inc(s.out_ready.sem, 1)

            for r in range(RING):
                total(Turn(Round(k, pe, 0), r, r, 0, r))
            with pe.Fori(1, GROUPS // RING - 1) as it:
                loop = Round(k, pe, it)
                for r in range(RING):
                    total(Turn(loop, it * RING + r, r, it, r))
            for r in range(RING):
                last = Turn(Round(k, pe, GROUPS // RING - 1), GROUPS - RING + r, r, GROUPS // RING - 1, r)
                (tail if r == RING - 1 else total)(last)

        node_pass(k, [(ab, k.agg), (tb, table)], [(eb, out)],
                  {"vector": vector, "scalar": scalar, "tensor": tensor},
                  [(s.out_ready, 1), (s.first_add, 1), (s.second_add, 1), (s.x_ready, 1), (s.exp_ready, 1),
                   (s.h_ready, 1), (s.part_ready, 1)])


def batch_factors(k):
    nc = k.nc
    with ExitStack() as ctx:
        def sb(name, shape):
            return ctx.enter_context(nc.sbuf_tensor(name, shape, F32))

        means, sq = sb("bn_means", [1, 2, D]), sb("bn_sq", [1, D])
        factor = sb("bn_factor", [1, 2, D])
        ones = sb("ones_row", [1, P])
        var_ready, root_ready, rows_ready, spread = (ctx.enter_context(nc.semaphore(n)) for n in (
            "var_ready", "root_ready_bn", "rows_ready", "spread"))
        with nc.Block() as block:
            @block.vector
            def _(dve):
                c = Chain(k.dve_chain, dve)
                dve.memset(ones[:, :], 1.0)
                for n in range(2):
                    c.mark(dve.tensor_reduce(means[:, n, :], k.ps[0:1, n, :].rearrange("p (t d) -> p d t", t=GT),
                                             AX.X, ALU.add))
                c.wait()
                c.mark(dve.tensor_scalar(means[:, :, :], means[:, :, :], 1.0 / N_REAL, None, ALU.mult))
                c.wait()
                c.mark(dve.tensor_tensor(sq[:, :], means[:, 0, :], means[:, 0, :], ALU.mult))
                c.wait()
                c.mark(dve.tensor_tensor(sq[:, :], means[:, 1, :], sq[:, :], ALU.subtract))
                c.wait()
                dve.tensor_scalar(sq[:, :], sq[:, :], 0.0, None, ALU.max).then_inc(var_ready, 1)
                dve.wait_ge(root_ready, 1)
                c.mark(dve.reciprocal(sq[:, :], sq[:, :]))
                c.wait()
                c.mark(dve.tensor_tensor(factor[:, 0, :], sq[:, :], k.bn_rows[:, 0, :], ALU.mult))
                c.wait()
                c.mark(dve.tensor_tensor(sq[:, :], means[:, 0, :], factor[:, 0, :], ALU.mult))
                c.wait()
                dve.tensor_tensor(factor[:, 1, :], k.bn_rows[:, 1, :], sq[:, :], ALU.subtract
                                  ).then_inc(rows_ready, 1)
                dve.wait_ge(spread, 1)
                for n, name in enumerate(("bn_a", "bn_b")):
                    for t in range(GT):
                        dve.tensor_copy(k.b[name][:, t, :], k.ps[:, 2, n * D:(n + 1) * D])
                k.dve_chain.advance(c.n)

            @block.scalar
            def _(act):
                act.wait_ge(var_ready, 1)
                act.activation(sq[:, :], sq[:, :], ACT.Sqrt, bias=k.eps[0:1, 0:1]).then_inc(root_ready, 1)

            @block.tensor
            def _(pe):
                pe.wait_ge(rows_ready, 1)
                pe.matmul(k.ps[:, 2, 0:2 * D], ones[:, :], factor[:, :, :].rearrange("p n d -> p (n d)"),
                          start=True, stop=True).then_inc(spread, 1)


def batch_pass(k, o, x, x_out, out):
    s = k.s
    with ExitStack() as ctx:
        eb, xb, yb, ob = (ring_buffer(k, ctx, n) for n in ("o", "x", "y", "out"))
        inner, outer = Norm(k, ctx, 0), Norm(k, ctx, 1)

        def vector(dve):
            def batch(t):
                dve.wait_ge(k.sp_dma[t.r].sem, t.landed(2))
                dve.tensor_tensor(eb[:, t.r], eb[:, t.r], k.b["bn_a"][:, :, :], ALU.mult).then_inc(s.first_add.sem, 1)
                dve.wait_ge(s.first_add.sem, t.done)
                dve.tensor_tensor(eb[:, t.r], eb[:, t.r], k.b["bn_b"][:, :, :], ALU.add).then_inc(s.second_add.sem, 1)
                dve.wait_ge(s.second_add.sem, t.done)
                inner.statistics(dve, eb, t)

            def inner_factors(t):
                inner.factors(dve, t)

            def add(t):
                dve.wait_ge(s.h_ready.sem, t.done)
                for other, op, done in ((k.b["ln_g"][:, :, :], ALU.mult, s.f_ready),
                                        (k.b["ln_b"][:, :, :], ALU.add, s.g_ready), (xb[:, t.r], ALU.add, s.x_ready)):
                    dve.tensor_tensor(yb[:, t.r], yb[:, t.r], other, op).then_inc(done.sem, 1)
                    dve.wait_ge(done.sem, t.done)
                outer.statistics(dve, yb, t)

            def outer_factors(t):
                outer.factors(dve, t, k.dinv_c[:, bass.ds(t.g * GT, GT)])
            by_groups(k, dve, (1, inner_factors), (3, outer_factors), (0, batch), (2, add))

        def scalar(act):
            def inner_norm(t):
                inner.apply(act, t, yb, eb, ACT.Identity).then_inc(s.h_ready.sem, 1)

            def roots(t):
                inner.square_root(act, t)

            def outer_roots(t):
                outer.square_root(act, t)

            def outer_norm(t):
                outer.apply(act, t, ob, yb, ACT.Relu).then_inc(s.out_ready.sem, 1)
            by_groups(k, act, (1, roots), (3, outer_roots), (1, inner_norm), (3, outer_norm))

        node_pass(k, [(eb, o), (xb, x)], [(ob, out), (yb, x_out)], {"vector": vector, "scalar": scalar},
                  [(s.out_ready, 1), (s.first_add, 1), (s.second_add, 1), (s.x_ready, 1), (s.h_ready, 1),
                   (s.f_ready, 1), (s.g_ready, 1)]
                  + inner.tallies() + outer.tallies(extra=True))


def gcn_pass(k, table, w, bias, out, x=None):
    s = k.s
    with ExitStack() as ctx:
        ab, tb, ob = (ring_buffer(k, ctx, n) for n in ("agg", "own", "out"))
        xb = ring_buffer(k, ctx, "x") if x is not None else None
        sum_t = pair_buffer(k, ctx, "sum_t")
        loads = [(ab, k.agg), (tb, table)] + ([(xb, x)] if x is not None else [])

        def landed(eng, t):
            eng.wait_ge(k.sp_dma[t.r].sem, t.landed(len(loads)))

        def vector(dve):
            def add(t):
                landed(dve, t)
                dve.tensor_tensor(ab[:, t.r], ab[:, t.r], tb[:, t.r], ALU.add).then_inc(s.first_add.sem, 1)

            def finish(t):
                dve.wait_ge(s.mm_done.sem, t.done)
                for q in range(GT):
                    ins = dve.scalar_tensor_tensor(tb[:, t.r, q, :], bank(k, 4 + t.b)[:, q, :],
                                                   k.dinv_c[:, bass.ds(t.g * GT + q, 1)], bias[:, q, :],
                                                   ALU.mult, ALU.add)
                ins.then_inc(s.mm_read.sem, 1)
                if x is not None:
                    dve.wait_ge(s.mm_read.sem, t.done)
                    dve.tensor_tensor(ob[:, t.r], tb[:, t.r], xb[:, t.r], ALU.add).then_inc(s.out_ready.sem, 1)
            by_groups(k, dve, (0, add), (2, finish))

        def scalar(act):
            def copy(t):
                act.wait_ge(s.in_t.sem, t.done)
                act.wait_ge(s.mm_done.sem, t.free)
                act.copy(sum_t[:, t.b], bank(k, t.b)).then_inc(s.in_copied.sem, 1)

            def scale(t):
                act.wait_ge(s.mm_read.sem, t.done)
                for q in range(GT):
                    ins = act.activation(ob[:, t.r, q, :], tb[:, t.r, q, :], ACT.Copy,
                                         scale=k.dinv_c[:, bass.ds(t.g * GT + q, 1)])
                ins.then_inc(s.out_ready.sem, 1)
            if x is None:
                by_groups(k, act, (1, copy), (3, scale))
            else:
                by_groups(k, act, (1, copy))

        def tensor(pe):
            def turn(t):
                pe.wait_ge(s.first_add.sem, t.done)
                pe.wait_ge(s.in_copied.sem, t.free)
                for q in range(GT):
                    mm = pe.transpose(bank(k, t.b)[:, q, :], ab[:, t.r, q, :], k.ident[:, :])
                mm.then_inc(s.in_t.sem, 1)

            def multiply(t):
                pe.wait_ge(s.in_copied.sem, t.done)
                pe.wait_ge(s.mm_read.sem, t.free)
                for q in range(GT):
                    mm = pe.matmul(bank(k, 4 + t.b)[:, q, :], sum_t[:, t.b, q, :], w[:, :],
                                   start=True, stop=True)
                mm.then_inc(s.mm_done.sem, 1)
            by_groups(k, pe, (1, turn), (2, multiply))

        node_pass(k, loads, [(ob, out)], {"vector": vector, "scalar": scalar, "tensor": tensor},
                  [(s.out_ready, 1), (s.first_add, 1), (s.mm_done, 1), (s.mm_read, 1), (s.in_t, 1),
                   (s.in_copied, 1)])


def edge_pass(k, h, ins):
    nc, s = k.nc, k.s
    scale = float(D) ** -0.5
    turns = GROUPS // RING
    used = (s.in_t, s.in_copied, s.nj_copied, s.ea_copied, s.h_t, s.mm_done, s.k_ready, s.g_ready, s.u_ready,
            s.q_ready, s.exp_ready, s.a_ready, s.w_ready, s.wz_ready, s.mask_ready, s.m1_ready, s.f_ready,
            s.prod_ready, s.um_ready, s.z_ready)
    k.top = max(signal.base for signal in used)
    with ExitStack() as ctx:
        def sb(name, shape, dt=F32):
            return ctx.enter_context(nc.sbuf_tensor(name, shape, dt))

        ni, nj = sb("ni", [P, RING, GT * D]), sb("nj", [P, RING, GT * D])
        ea = sb("ea", [P, RING, GT, EA])
        zb = sb("zb", [P, RING, GT, ZW])
        staged = sb("staged_ij", [P, 2, 2, SLOTS], I32)
        ni_t, nj_t, ea_t, f_t = (sb(n, [P, RING, GT * P]) for n in ("ni_t", "nj_t", "ea_t", "f_t"))
        ex, m1, q_t, prod = (sb(n, [P, 2, GT * P]) for n in ("ex", "m1", "q_t", "prod"))
        mask, um, a, exp_a, wz = (sb(n, [P, RING, GT]) for n in ("mask", "um", "score", "exp_a", "wz"))
        ea_in = ins["edge_attr_70"].rearrange("(p t) c -> p t c", p=P)
        z_out = k.z.rearrange("(p t) c -> p t c", p=P)
        B_NI, B_NJ, B_EA, B_PRE, B_Q, B_K, B_U, B_G = range(8)
        ps = k.ps

        with nc.Block() as block:
            @block.gpsimd
            def _(pool):
                level(k, pool, used)

                def stage(turn, b):
                    for n, table in enumerate((k.edge_src, k.edge_dst)):
                        ins_ = pool.tensor_copy(staged[:, b, n, :], table[:, bass.ds(turn * SLOTS, SLOTS)])
                    ins_.then_inc(s.idx_staged.sem, 1)

                stage(0, 0)
                with pool.Fori(0, turns // 2) as pair:
                    for b in range(2):
                        it = pair * 2 + b
                        for r in range(RING):
                            if r == 0:
                                pool.wait_ge(s.idx_staged.sem, s.idx_staged.at(it + 1))
                                pool.sem_inc(k.pool_pass, 1)
                            if r == 1:
                                pool.wait_ge(s.in_t.sem, k.top + it * RING)
                                pool.sem_inc(k.pool_pass, 1)
                                stage(it + 1, 1 - b)
                            pool.wait_ge(s.in_t.sem, it * RING + (k.top + r + 1 - RING))
                            pool.sem_inc(k.pool_pass, 1)
                            for n, buf in enumerate((ni, nj)):
                                for q in range(GT):
                                    pool.indirect_dma_start(
                                        buf[:, r, q * D:(q + 1) * D], None, h, bass.IndirectOffsetOnAxis(
                                            ap=staged[:, b, n, r * GT + q:r * GT + q + 1], axis=0)
                                    ).then_inc(k.pool_dma[r].sem, 16)

            @block.sync
            def _(sp):
                def load(t):
                    sp.wait_ge(k.sp_second[t.r].sem, t.rounds_of(k.sp_second, 1))
                    sp.sem_inc(k.sp_pass, 1)
                    sp.dma_start(ea[:, t.r], ea_in[:, bass.ds(t.g * GT, GT), :]).then_inc(k.sp_dma[t.r].sem, 16)

                def store(t):
                    sp.wait_ge(s.z_ready.sem, t.done)
                    sp.sem_inc(k.sp_pass, 1)
                    sp.dma_start(z_out[:, bass.ds(t.g * GT, GT), :], zb[:, t.r]
                                 ).then_inc(k.sp_second[t.r].sem, 16)
                by_groups(k, sp, (0, load), (5, store))
                for r in range(RING):
                    sp.wait_ge(k.sp_second[r].sem, k.sp_second[r].at(16 * turns))

            @block.tensor
            def _(pe):
                def turn(t):
                    pe.wait_ge(k.pool_dma[t.r].sem, t.gathered(2 * GT))
                    pe.wait_ge(k.sp_dma[t.r].sem, t.landed(1))
                    pe.wait_ge(s.in_copied.sem, t.prior)
                    pe.wait_ge(s.nj_copied.sem, t.prior)
                    pe.wait_ge(s.ea_copied.sem, t.prior)
                    for q in range(GT):
                        cut = slice(q * P, (q + 1) * P)
                        pe.transpose(ps[:, B_NI, cut], ni[:, t.r, cut], k.ident[:, :])
                        pe.transpose(ps[:, B_NJ, cut], nj[:, t.r, cut], k.ident[:, :])
                        mm = pe.transpose(ps[0:EF, B_EA, cut], ea[:, t.r, q, 0:EF], k.ident[:, :])
                    mm.then_inc(s.in_t.sem, 1)

                def project(t):
                    pe.wait_ge(s.in_copied.sem, t.done)
                    pe.wait_ge(s.q_ready.sem, t.prior)
                    pe.matmul(ps[:, B_Q, :], k.w["q"][:, :], ni_t[:, t.r, :], start=True,
                              stop=True).then_inc(s.h_t.sem, 1)
                    pe.wait_ge(s.nj_copied.sem, t.done)
                    pe.wait_ge(s.ea_copied.sem, t.done)
                    pe.wait_ge(s.f_ready.sem, t.prior)
                    pe.matmul(ps[:, B_PRE, :], k.w["ni"][:, :], ni_t[:, t.r, :], start=True, stop=False)
                    pe.matmul(ps[:, B_PRE, :], k.w["nj"][:, :], nj_t[:, t.r, :], start=False, stop=False)
                    pe.matmul(ps[:, B_PRE, :], k.w["ea"][0:EF, :], ea_t[0:EF, t.r, :], start=False,
                              stop=True).then_inc(s.mm_done.sem, 1)

                def key(t):
                    pe.wait_ge(s.f_ready.sem, t.done)
                    pe.wait_ge(s.prod_ready.sem, t.prior)
                    pe.matmul(ps[:, B_K, :], k.w["k"][:, :], f_t[:, t.r, :], start=True,
                              stop=True).then_inc(s.k_ready.sem, 1)

                def score(t):
                    pe.wait_ge(s.prod_ready.sem, t.done)
                    pe.wait_ge(s.um_ready.sem, t.prior)
                    for q in range(GT):
                        mm = pe.matmul(ps[:, B_U, q:q + 1], prod[:, t.b, q * P:(q + 1) * P], k.wa[:, :],
                                       start=True, stop=True)
                    mm.then_inc(s.u_ready.sem, 1)
                    pe.wait_ge(s.z_ready.sem, t.prior)
                    for q in range(GT):
                        cut = slice(q * P, (q + 1) * P)
                        mm = pe.matmul(ps[:, B_G, cut], f_t[:, t.r, cut], k.w["u"][:, :], start=True, stop=True)
                    mm.then_inc(s.g_ready.sem, 1)
                by_groups(k, pe, (3, score), (2, key), (1, project), (0, turn))

            @block.scalar
            def _(act):
                def scores(t):
                    act.wait_ge(s.um_ready.sem, t.done)
                    act.activation(a[:, t.r, :], um[:, t.r, :], ACT.Tanh).then_inc(s.a_ready.sem, 1)
                    act.wait_ge(s.a_ready.sem, t.done)
                    act.activation(exp_a[:, t.r, :], a[:, t.r, :], ACT.Exp).then_inc(s.w_ready.sem, 1)

                def exponentials(t):
                    act.wait_ge(s.h_t.sem, t.done)
                    act.wait_ge(s.prod_ready.sem, t.free)
                    act.activation(q_t[:, t.b, :], ps[:, B_Q, :], ACT.Copy, scale=scale
                                   ).then_inc(s.q_ready.sem, 1)
                    act.wait_ge(s.mm_done.sem, t.done)
                    act.wait_ge(s.m1_ready.sem, t.free)
                    act.activation(ex[:, t.b, :], ps[:, B_PRE, :], ACT.Exp, bias=k.bf[:, 0:1]
                                   ).then_inc(s.exp_ready.sem, 1)

                def copy(t):
                    act.wait_ge(s.in_t.sem, t.done)
                    act.copy(ni_t[:, t.r, :], ps[:, B_NI, :]).then_inc(s.in_copied.sem, 1)
                    act.copy(ea_t[0:EF, t.r, :], ps[0:EF, B_EA, :]).then_inc(s.ea_copied.sem, 1)
                by_groups(k, act, (3, scores), (1, exponentials), (0, copy))

            @block.vector
            def _(dve):
                dve.memset(zb[:, :, :, D + 1:], 0.0)

                def product(t):
                    dve.wait_ge(s.k_ready.sem, t.done)
                    dve.wait_ge(s.q_ready.sem, t.done)
                    dve.wait_ge(s.u_ready.sem, t.free)
                    dve.tensor_tensor(prod[:, t.b, :], q_t[:, t.b, :], ps[:, B_K, :], ALU.mult
                                      ).then_inc(s.prod_ready.sem, 1)

                def masked(t):
                    dve.wait_ge(s.u_ready.sem, t.done)
                    dve.tensor_tensor(um[:, t.r, :], ps[:, B_U, 0:GT], mask[:, t.r, :], ALU.mult
                                      ).then_inc(s.um_ready.sem, 1)

                def features(t):
                    dve.wait_ge(s.exp_ready.sem, t.done)
                    dve.tensor_scalar(m1[:, t.b, :], ex[:, t.b, :], 1.0, -1.0, ALU.min, ALU.add
                                      ).then_inc(s.m1_ready.sem, 1)
                    dve.wait_ge(s.m1_ready.sem, t.done)
                    dve.scalar_tensor_tensor(f_t[:, t.r, :], ps[:, B_PRE, :], k.bf[:, 0:1], m1[:, t.b, :], ALU.add,
                                             ALU.max).then_inc(s.f_ready.sem, 1)

                def results(t):
                    dve.wait_ge(s.w_ready.sem, t.done)
                    dve.tensor_tensor(wz[:, t.r, :], exp_a[:, t.r, :], mask[:, t.r, :], ALU.mult
                                      ).then_inc(s.wz_ready.sem, 1)
                    dve.tensor_copy(zb[:, t.r, :, D], a[:, t.r, :])
                    dve.wait_ge(s.wz_ready.sem, t.done)
                    dve.wait_ge(s.g_ready.sem, t.done)
                    for q in range(GT):
                        z = dve.tensor_scalar(zb[:, t.r, q, 0:D], ps[:, B_G, q * P:(q + 1) * P],
                                              wz[:, t.r, q:q + 1], None, ALU.mult)
                    z.then_inc(s.z_ready.sem, 1)

                def copy(t):
                    dve.wait_ge(s.in_t.sem, t.done)
                    dve.tensor_copy(nj_t[:, t.r, :], ps[:, B_NJ, :]).then_inc(s.nj_copied.sem, 1)
                    dve.wait_ge(k.sp_dma[t.r].sem, t.landed(1))
                    dve.tensor_scalar(mask[:, t.r, :], ea[:, t.r, :, 0], 8.0, None, ALU.is_lt
                                      ).then_inc(s.mask_ready.sem, 1)
                by_groups(k, dve, (3, masked), (2, product), (3, results), (1, features), (0, copy))

        for r in range(RING):
            k.pool_dma[r].advance(16 * 2 * GT * turns)
            k.sp_dma[r].advance(16 * turns)
            k.sp_second[r].advance(16 * turns)
        s.idx_staged.advance(turns + 1)
        for signal in used:
            signal.advance(GROUPS)


def build(nc, ins, out, stop=None):
    k = Program()
    k.nc, k.names = nc, 0

    def name(text):
        k.names += 1
        return f"{text}_{k.names}"
    k.name = name
    with ExitStack() as ctx:
        setup(k, ctx)
        t0, t1 = k.table
        r0, r1 = k.res
        w, b = k.w, k.b
        steps = [
            lambda: constants_and_loads(k, ins),
            lambda: prepare(k, ins),
            lambda: norm_pass(k, ins["x"], t0),
            lambda: sum_over_nodes(k, "dst", t0, D, k.agg),
            lambda: sage_pass(k, t0, w["self0"], w["neigh0"], b["b0"], t1),
            lambda: sum_over_nodes(k, "dst", t1, D, k.agg),
            lambda: sage_pass(k, t1, w["self1"], w["neigh1"], b["b1"], t0, ins["x"], r0),
            lambda: edge_pass(k, t0, ins),
            lambda: sum_over_nodes(k, "src", k.z, ZW, k.agg_src),
            lambda: attention_pass(k, t0, r0, r1, t1),
            lambda: sum_over_nodes(k, "dst", t1, D, k.agg, weighted=True),
            lambda: elu_pass(k, t1, k.elu_out),
            lambda: batch_factors(k),
            lambda: batch_pass(k, k.elu_out, r1, r0, t0),
            lambda: sum_over_nodes(k, "dst", t0, D, k.agg),
            lambda: gcn_pass(k, t0, w["g0"], b["g0"], t1),
            lambda: sum_over_nodes(k, "dst", t1, D, k.agg),
            lambda: gcn_pass(k, t1, w["g1"], b["g1"], t0),
            lambda: sum_over_nodes(k, "dst", t0, D, k.agg),
            lambda: gcn_pass(k, t0, w["g2"], b["g2"], out, x=r0),
        ]
        for n, step in enumerate(steps[:stop]):
            step()


NAMES = ["x", "src", "dst", "edge_attr_70", "edge_weight",
         "L0_gnn_W_self0", "L0_gnn_W_neigh0", "L0_gnn_b0", "L0_gnn_W_self1", "L0_gnn_W_neigh1", "L0_gnn_b1",
         "L1_gnn_Wf", "L1_gnn_bf", "L1_gnn_Wq", "L1_gnn_Wk", "L1_gnn_Wa", "L1_gnn_Wu", "L1_gnn_bu",
         "L2_gnn_W", "L2_gnn_b", "L2_gnn_bn_gamma", "L2_gnn_bn_beta", "L2_gnn_ln_gamma", "L2_gnn_ln_beta",
         "L3_gnn_W", "L3_gnn_b"]
STOP = None


def kernel(**inputs):
    import numpy as np
    import concourse.bacc as bacc
    from concourse.bass_utils import run_bass_kernel_spmd

    nc = bacc.Bacc("TRN2", target_bir_lowering=False, num_devices=1)
    arrays, ins = {}, {}
    for name in NAMES:
        a = np.ascontiguousarray(inputs[name])
        if a.shape[0] == N_REAL:
            padded = np.full((NP,) + a.shape[1:], NP - 1 if name in ("src", "dst") else 0, a.dtype)
            padded[:N_REAL] = a
            a = padded
        arrays[name] = a
        ins[name] = nc.dram_tensor(name, a.shape, mybir.dt.from_np(a.dtype), kind="ExternalInput").ap()
    out = nc.dram_tensor("out", (NP, D), F32, kind="ExternalOutput").ap()
    build(nc, ins, out, STOP)
    r = run_bass_kernel_spmd(nc, [arrays], core_ids=[0])
    return r.results[0]["out"][:N_REAL]
```

```python
from contextlib import ExitStack

import concourse.bass as bass
from concourse import mybir

F32 = mybir.dt.float32
BF16 = mybir.dt.bfloat16
F16 = mybir.dt.float16
I32 = mybir.dt.int32
ALU = mybir.AluOpType
ACT = mybir.ActivationFunctionType
AX = mybir.AxisListType

P = 128
N_REAL = 50000
D = 128
TILES = 392
NP = TILES * P
STEPS = 2 * TILES
GT = 4
GROUPS = TILES // GT
RING = 7
SPARE = 16
HALF = 4
REGION = 8
SPT = 16
SLOTS = RING * GT
LANDING = 2
EA = 70
EF = 65
ZW = 130
DEPTH = GT
AHEAD = 2
EPS = 1e-5
WARM = 16
CHUNKS = [(c * P, min(P, TILES - c * P)) for c in range((TILES + P - 1) // P)]


class Signal:

    def __init__(self, handle, base=WARM):
        self.sem, self.base = handle, base

    def at(self, n):
        return n + self.base

    def advance(self, n):
        self.base += n


class Chain:

    def __init__(self, signal, eng, rounds=0, per_round=0):
        self.counter, self.eng, self.start, self.n = signal, eng, rounds * per_round, 0

    def mark(self, ins):
        ins.then_inc(self.counter.sem, 1)
        self.n += 1
        return self.counter.at(self.start + self.n)

    def wait(self, value=None):
        self.eng.wait_ge(self.counter.sem, self.counter.at(self.start + self.n) if value is None else value)


class Signals:

    def __init__(self, make):
        self.all = []

        def sig(name):
            self.all.append(make(name))
            return self.all[-1]
        self.tiles_ready = sig("tiles_ready")
        self.idx_staged = sig("idx_staged")
        self.cols_staged = sig("cols_staged")
        self.onehot_ready = sig("onehot_ready")
        self.step_done = sig("step_done")
        self.acc_done = sig("acc_done")
        self.in_t = sig("in_t")
        self.in_copied = sig("in_copied")
        self.mm_done = sig("mm_done")
        self.mm_read = sig("mm_read")
        self.mm2_done = sig("mm2_done")
        self.out_ready = sig("out_ready")
        self.x_ready = sig("x_ready")
        self.h_ready = sig("h_ready")
        self.h_t = sig("h_t")
        self.h_copied = sig("h_copied")
        self.part_ready = sig("part_ready")
        self.mask_ready = sig("mask_ready")
        self.exp_ready = sig("exp_ready")
        self.f_ready = sig("f_ready")
        self.nj_copied, self.ea_copied = sig("nj_copied"), sig("ea_copied")
        self.m1_ready, self.w_ready, self.wz_ready = sig("m1_ready"), sig("w_ready"), sig("wz_ready")
        self.k_ready = sig("k_ready")
        self.q_ready = sig("q_ready")
        self.prod_ready = sig("prod_ready")
        self.u_ready = sig("u_ready")
        self.um_ready = sig("um_ready")
        self.a_ready = sig("a_ready")
        self.g_ready = sig("g_ready")
        self.z_ready = sig("z_ready")
        self.first_add = sig("first_add")
        self.second_add = sig("second_add")


class Program:
    pass


def rows(ap, first, tiles):
    return ap[bass.ds(first * P, tiles * P), :].rearrange("(t p) d -> p t d", p=P)


def setup(k, ctx):
    nc = k.nc

    def sb(name, shape, dt=F32):
        return ctx.enter_context(nc.sbuf_tensor(name, shape, dt))

    def sig(name, base=WARM):
        return Signal(ctx.enter_context(nc.semaphore(name)), base)

    def dram(name, shape, dt=F32):
        return nc.dram_tensor(name, shape, dt, kind="Internal").ap()

    k.ps = ctx.enter_context(nc.psum_tensor("ps", [P, 8, 512], F32))
    k.ident = sb("ident", [P, P])
    k.iota = sb("iota", [P, P])
    k.w = {n: sb("w_" + n, [P, P]) for n in
           ("self0", "neigh0", "self1", "neigh1", "ni", "nj", "ea", "q", "k", "u", "gcn", "g0", "g1", "g2")}
    k.wf_diff = sb("wf_diff", [P, P])
    k.wa = sb("w_a", [P, 1])
    k.bf = sb("b_f", [P, 1])
    k.b = {n: sb("b_" + n, [P, GT, D]) for n in
           ("b0", "b1", "u", "gcn", "ln_g", "ln_b", "g0", "g1", "g2", "bn_a", "bn_b")}
    k.bn_rows = sb("bn_rows", [1, 2, D])
    k.eps = sb("eps", [P, 1])
    k.rel = {o: sb("rel_" + o, [P, STEPS + SPT]) for o in ("dst", "src")}
    k.keep = {o: sb("keep_" + o, [P, STEPS + SPT]) for o in ("dst", "src")}
    k.weight = sb("weight_dst", [P, STEPS + SPT])
    k.idx = {o: sb("idx_" + o, [P, TILES + SLOTS], I32) for o in ("dst", "src")}
    k.edge_src = sb("edge_src", [P, TILES + SLOTS], I32)
    k.edge_dst = sb("edge_dst", [P, TILES + SLOTS], I32)
    k.ctl_slot = {o: sb("ctl_slot_" + o, [1, STEPS], I32) for o in ("dst", "src")}
    k.ctl_out = {o: sb("ctl_out_" + o, [1, 2, STEPS // 2], I32) for o in ("dst", "src")}
    k.ctl_ready = {o: sb("ctl_ready_" + o, [1, STEPS // REGION], I32) for o in ("dst", "src")}
    k.ctl_free = {o: sb("ctl_free_" + o, [1, GROUPS], I32) for o in ("dst", "src")}
    k.mean_scale = sb("mean_scale", [P, TILES])
    k.dinv_w = sb("dinv_w", [P, TILES])
    k.dinv_c = sb("dinv_c", [P, TILES])

    k.table = [dram(f"table{n}", [NP, D]) for n in range(2)]
    k.agg = dram("agg", [NP + SPARE * P, D])
    k.agg_src = dram("agg_src", [NP + SPARE * P, ZW])
    k.z = dram("z", [NP, ZW])
    k.res = [dram(f"residual{n}", [NP, D]) for n in range(2)]
    k.elu_out = dram("elu_out", [NP, D])
    k.rec = {"dst": dram("rec_dst", [NP, 4]), "src": dram("rec_src", [NP, 2])}
    k.last_step_dram = dram("last_step", [2, 512])

    k.sp_dma = [sig(f"sp_dma{n}", 0) for n in range(RING)]
    k.pool_dma = [sig(f"pool_dma{n}", 0) for n in range(RING)]
    k.pool_pair = [sig(f"pool_pair{n}", 0) for n in range(2)]
    k.sp_second = [sig(f"sp_second{n}", 0) for n in range(RING)]
    k.sp_store = [sig(f"sp_store{n}", 0) for n in range(SPT // HALF)]
    k.act_store = [sig(f"act_store{n}", 0) for n in range(SPT // HALF)]
    k.dve_chain = sig("dve_chain")
    k.pool_pass, k.dve_pass, k.sp_pass = (ctx.enter_context(nc.semaphore(n)) for n in
                                          ("pool_pass", "dve_pass", "sp_pass"))
    k.s = Signals(sig)
    k.norm_signals = [[sig(f"{name}{n}") for n in range(2)] for name in
                      ("bn_ready", "stat_ready", "root_ready", "inverse_ready", "scaled_ready", "factors_ready")]
    return k


def constants_and_loads(k, ins):
    nc, s = k.nc, k.s
    wf = ins["L1_gnn_Wf"]
    loads = [(k.w["self0"][:, :], ins["L0_gnn_W_self0"]), (k.w["neigh0"][:, :], ins["L0_gnn_W_neigh0"]),
             (k.w["self1"][:, :], ins["L0_gnn_W_self1"]), (k.w["neigh1"][:, :], ins["L0_gnn_W_neigh1"]),
             (k.w["ni"][:, :], wf[0:P, :]), (k.w["nj"][:, :], wf[P:2 * P, :]),
             (k.wf_diff[:, :], wf[2 * P:3 * P, :]), (k.w["ea"][0:EF, :], wf[3 * P:3 * P + EF, :]),
             (k.w["q"][:, :], ins["L1_gnn_Wq"]), (k.w["k"][:, :], ins["L1_gnn_Wk"]),
             (k.w["u"][:, :], ins["L1_gnn_Wu"]), (k.w["gcn"][:, :], ins["L2_gnn_W"]),
             (k.w["g0"][:, :], ins["L3_gnn_W"][0]), (k.w["g1"][:, :], ins["L3_gnn_W"][1]),
             (k.w["g2"][:, :], ins["L3_gnn_W"][2]), (k.wa[:, :], ins["L1_gnn_Wa"]),
             (k.bf[:, :], ins["L1_gnn_bf"].rearrange("(d a) -> d a", a=1)),
             (k.bn_rows[:, 0, :], ins["L2_gnn_bn_gamma"].rearrange("(a d) -> a d", a=1)),
             (k.bn_rows[:, 1, :], ins["L2_gnn_bn_beta"].rearrange("(a d) -> a d", a=1))]
    biases = {"b0": ins["L0_gnn_b0"], "b1": ins["L0_gnn_b1"], "u": ins["L1_gnn_bu"], "gcn": ins["L2_gnn_b"],
              "ln_g": ins["L2_gnn_ln_gamma"], "ln_b": ins["L2_gnn_ln_beta"],
              "g0": ins["L3_gnn_b"][0], "g1": ins["L3_gnn_b"][1], "g2": ins["L3_gnn_b"][2]}
    for name, b in biases.items():
        loads.append((k.b[name][:, 0, :], b.partition_broadcast(P)))
    sp_loads = loads[len(k.act_store):]
    first = k.sp_store + k.sp_dma + k.sp_second
    sp_signals = first + [k.sp_second[n % RING] for n in range(len(sp_loads) - len(first))]
    for signal in k.act_store + sp_signals:
        signal.advance(16)
    with ExitStack() as ctx:
        lane_i = ctx.enter_context(nc.sbuf_tensor("lane_i", [P, P], I32))
        diff_i = ctx.enter_context(nc.sbuf_tensor("diff_i", [P, P], I32))
        made = ctx.enter_context(nc.semaphore("consts_made"))
        block = ctx.enter_context(nc.Block())

        @block.sync
        def _(sp):
            for signal, (to, of) in zip(sp_signals, sp_loads):
                sp.dma_start(to, of).then_inc(signal.sem, 16)
            for signal in first:
                sp.wait_ge(signal.sem, signal.base)

        @block.scalar
        def _(act):
            for signal, (to, of) in zip(k.act_store, loads):
                act.dma_start(to, of).then_inc(signal.sem, 16)
            for signal in k.act_store:
                act.wait_ge(signal.sem, signal.base)

        @block.gpsimd
        def _(pool):
            pool.iota(lane_i[:, :], pattern=[[1, P]], base=0, channel_multiplier=0).then_inc(made, 1)
            pool.iota(diff_i[:, :], pattern=[[1, P]], base=0, channel_multiplier=-1).then_inc(made, 1)
            for n, signal in enumerate(k.pool_dma + k.pool_pair):
                pool.dma_start(k.z[n * P:(n + 1) * P, 0:D], ins["x"][0:P, :]).then_inc(signal.sem, 16)
                signal.base = 16
            for signal in k.pool_dma + k.pool_pair:
                pool.wait_ge(signal.sem, 16)
            both = [signal for pair in k.norm_signals for signal in pair]
            for signal in k.s.all + both + [k.dve_chain]:
                pool.sem_inc(signal.sem, WARM)

        @block.vector
        def _(dve):
            dve.wait_ge(made, 2)
            dve.tensor_copy(k.iota[:, :], lane_i[:, :])
            dve.tensor_scalar(k.ident[:, :], diff_i[:, :], 0.0, None, ALU.is_equal)
            dve.memset(k.eps[:, :], EPS)
            for signal in first + k.act_store:
                dve.wait_ge(signal.sem, signal.base)
            for name in biases:
                for t in range(1, GT):
                    dve.tensor_copy(k.b[name][:, t, :], k.b[name][:, 0, :])
            dve.tensor_tensor(k.w["ni"][:, :], k.w["ni"][:, :], k.wf_diff[:, :], ALU.add)
            dve.tensor_tensor(k.w["nj"][:, :], k.w["nj"][:, :], k.wf_diff[:, :], ALU.subtract)


def prepare(k, ins):
    with ExitStack() as ctx:
        starts = {o: ctx.enter_context(k.nc.sbuf_tensor("starts_" + o, [P, TILES + 1], F32))
                  for o in ("src", "dst")}
        order_edges(k, ins, starts)
        for n, o in enumerate(("src", "dst")):
            plan_steps(k, n, o, starts[o])


def order_edges(k, ins, starts):
    nc, s = k.nc, k.s
    keys = ("src", "dst")
    with ExitStack() as ctx:
        def sb(name, shape, dt=F32):
            return ctx.enter_context(nc.sbuf_tensor(name, shape, dt))

        def sem(name):
            return ctx.enter_context(nc.semaphore(name))

        node_i = {"src": k.edge_src, "dst": k.edge_dst}
        tile_i = {o: sb(f"tile_i_{o}", [P, TILES], I32) for o in keys}
        tile_f = {o: sb(f"tile_f_{o}", [P, TILES + AHEAD]) for o in keys}
        lane_i = sb("lane_dst_i", [P, TILES], I32)
        lane_f = sb("lane_dst_f", [P, TILES + AHEAD])
        ew = sb("ew", [P, TILES])
        part_b = sb("part_b", [P, TILES], BF16)
        ew_part = [sb(f"ew_part{n}", [P, TILES]) for n in range(3)]
        rest = [sb(f"ew_rest{n}", [P, TILES]) for n in range(2)]
        bins_i = sb("bins_i", [P, TILES + 1], I32)
        edge_i = sb("edge_i", [P, TILES], I32)
        bins = sb("bins", [P, TILES + 1], F16)
        lanes = sb("lanes", [P, P], F16)
        tri_i = sb("tri_i", [P, P], I32)
        before = sb("before", [P, P], BF16)
        from_on = sb("from_on", [P, P], BF16)
        onehot = sb("onehot_tile", [P, DEPTH, 2, TILES], BF16)
        lane_hot = sb("lane_hot", [P, DEPTH, 4, P], BF16)
        products = sb("products", [P, 2, GT, TILES], BF16)
        rec = {"dst": sb("recs_dst", [P, TILES, 4]), "src": sb("recs_src", [P, TILES, 2])}
        pos = sb("pos", [P, 2, 2, GT])
        pos_i = sb("pos_i", [P, 2, 2, GT], I32)
        pos_t = sb("pos_t", [P, 2, 2, GT], I32)
        pos_l = sb("pos_l", [P, 2, 2, GT], I32)
        place = sb("place", [P, 2, 2, GT], I32)
        staged = {"dst": sb("staged_dst", [P, 2, GT, 4]), "src": sb("staged_src", [P, 2, GT, 2])}
        iotas, loaded, prepared = sem("iotas"), sem("loaded"), sem("prepared")
        count_ps = {"src": k.ps[:, 0, 0:TILES + 1], "dst": k.ps[:, 1, 0:TILES + 1]}
        deg_ps = [k.ps[:, 2, 0:TILES], k.ps[:, 3, 0:TILES]]
        with nc.Block() as block:
            @block.sync
            def _(sp):
                sp.dma_start(k.edge_src[:, 0:TILES], ins["src"].rearrange("(p t) -> p t", p=P)).then_inc(loaded, 16)
                sp.dma_start(k.edge_dst[:, 0:TILES], ins["dst"].rearrange("(p t) -> p t", p=P)).then_inc(loaded, 16)
                sp.dma_start(ew[:, :], ins["edge_weight"].rearrange("(p t) -> p t", p=P)).then_inc(loaded, 16)
                sp.wait_ge(loaded, 48)

            @block.gpsimd
            def _(pool):
                pool.iota(bins_i[:, :], pattern=[[1, TILES + 1]], base=0, channel_multiplier=0).then_inc(iotas, 1)
                pool.iota(tri_i[:, :], pattern=[[1, P]], base=0, channel_multiplier=-1).then_inc(iotas, 1)
                pool.iota(edge_i[:, :], pattern=[[1, TILES]], base=0, channel_multiplier=TILES).then_inc(iotas, 1)

            @block.vector
            def _(dve):
                c = Chain(k.dve_chain, dve)
                dve.wait_ge(iotas, 3)
                dve.tensor_copy(bins[:, :], bins_i[:, :])
                dve.tensor_copy(lanes[:, :], bins_i[:, 0:P])
                dve.tensor_scalar(before[:, :], tri_i[:, :], 0.0, None, ALU.is_gt)
                dve.tensor_scalar(from_on[:, :], tri_i[:, :], 0.0, None, ALU.is_le)
                dve.tensor_copy(rec["src"][:, :, 1], edge_i[:, :])
                dve.memset(rec["dst"][:, :, 3], 0.0)
                for o in keys:
                    dve.memset(node_i[o][:, TILES:], 0)
                dve.wait_ge(loaded, 48)
                for o in keys:
                    dve.tensor_scalar(tile_i[o][:, :], node_i[o][:, 0:TILES], 7, None, ALU.arith_shift_right)
                dve.tensor_scalar(lane_i[:, :], node_i["dst"][:, 0:TILES], 127, None, ALU.bitwise_and)
                dve.tensor_copy(rec["src"][:, :, 0], node_i["src"][:, 0:TILES])
                dve.tensor_copy(rec["dst"][:, :, 0], node_i["dst"][:, 0:TILES])
                dve.tensor_copy(rec["dst"][:, :, 1], node_i["src"][:, 0:TILES])
                c.mark(dve.tensor_copy(rec["dst"][:, :, 2], ew[:, :]))
                c.mark(dve.tensor_copy(part_b[:, :], ew[:, :]))
                c.wait()
                for o in keys:
                    dve.memset(tile_f[o][:, TILES:], -1.0)
                    dve.tensor_copy(tile_f[o][:, 0:TILES], tile_i[o][:, :])
                dve.memset(lane_f[:, TILES:], -1.0)
                dve.tensor_copy(lane_f[:, 0:TILES], lane_i[:, :])
                c.mark(dve.tensor_copy(ew_part[0][:, :], part_b[:, :]))
                c.wait()
                c.mark(dve.tensor_tensor(rest[0][:, :], ew[:, :], ew_part[0][:, :], ALU.subtract))
                c.wait()
                c.mark(dve.tensor_copy(part_b[:, :], rest[0][:, :]))
                c.wait()
                c.mark(dve.tensor_copy(ew_part[1][:, :], part_b[:, :]))
                c.wait()
                c.mark(dve.tensor_tensor(rest[1][:, :], rest[0][:, :], ew_part[1][:, :], ALU.subtract))
                c.wait()
                c.mark(dve.tensor_copy(part_b[:, :], rest[1][:, :]))
                c.wait()
                ins_ = c.mark(dve.tensor_copy(ew_part[2][:, :], part_b[:, :]))
                c.wait()
                dve.sem_inc(prepared, 1)
                k.dve_chain.advance(c.n)

        tile_starts(k, keys, tile_i, bins, count_ps, starts)

        hot_ready, lane_ready, ranks_ready, weighted_ready = s.onehot_ready, s.part_ready, s.mm_done, s.w_ready
        ranked, counted = s.acc_done, s.step_done
        with nc.Block() as block:
            @block.vector
            def _(dve):
                per = 6

                def tile_hot(t, b, n, used):
                    if used:
                        dve.wait_ge(counted.sem, counted.at(t - (DEPTH - 1)))
                    dve.tensor_scalar(onehot[:, b, n, :], bins[:, 0:TILES], tile_f[keys[n]][:, bass.ds(t, 1)],
                                      None, ALU.is_equal).then_inc(hot_ready.sem, 1)

                def lanes_hot(t, b):
                    dve.tensor_scalar(lane_hot[:, b, 0, :], lanes[:, :], lane_f[:, bass.ds(t, 1)], None,
                                      ALU.is_equal).then_inc(lane_ready.sem, 1)

                def group(g, half, first):
                    c = Chain(k.dve_chain, dve, g, per)
                    for q in range(GT):
                        t = g * GT + q
                        ahead, b = t + AHEAD, (q + AHEAD) % DEPTH
                        if q == 0 and not first:
                            dve.wait_ge(k.pool_pair[half].sem, scattered(g, half))
                        for n, o in enumerate(keys):
                            dve.wait_ge(ranks_ready.sem, ranks_ready.at(t * 2 + n + 1))
                            dve.tensor_tensor_reduce(
                                products[:, n, q, :], onehot[:, q, n, :], count_ps[o][:, 0:TILES], 1.0, 0.0,
                                ALU.mult, ALU.add, pos[:, half, n, q:q + 1]).then_inc(ranked.sem, 1)
                        if q == GT - 1:
                            dve.wait_ge(ranked.sem, ranked.at((g + 1) * GT * 2))
                            c.mark(dve.tensor_copy(pos_i[:, half, :, :], pos[:, half, :, :]))
                            for o in keys:
                                c.mark(dve.tensor_copy(staged[o][:, half, :, :], rec[o][:, bass.ds(g * GT, GT), :]))
                        used = not first or q >= DEPTH - AHEAD
                        tile_hot(ahead, b, 0, used)
                        if q == GT - 1:
                            c.wait()
                            c.mark(dve.tensor_scalar(pos_t[:, half, :, :], pos_i[:, half, :, :], 7, None,
                                                     ALU.arith_shift_right))
                            c.mark(dve.tensor_scalar(pos_l[:, half, :, :], pos_i[:, half, :, :], 127, None,
                                                     ALU.bitwise_and))
                        tile_hot(ahead, b, 1, False)
                        lanes_hot(ahead, b)
                    c.wait()
                    c.mark(dve.scalar_tensor_tensor(place[:, half, :, :], pos_l[:, half, :, :], float(TILES),
                                                    pos_t[:, half, :, :], ALU.mult, ALU.add))
                    assert c.n == per

                def scattered(g, half):
                    return k.pool_pair[half].at((g - half) * (128 // 2))

                for t in range(AHEAD):
                    for n in range(2):
                        tile_hot(t, t, n, False)
                    lanes_hot(t, t)
                for half in range(2):
                    group(half, half, half == 0)
                with dve.Fori(1, GROUPS // 2) as it:
                    for half in range(2):
                        group(it * 2 + half, half, False)
                dve.wait_ge(counted.sem, counted.at(TILES))
                c = Chain(k.dve_chain, dve, GROUPS, per)
                c.mark(dve.tensor_scalar(k.mean_scale[:, :], deg_ps[0], 1.0, None, ALU.max))
                c.mark(dve.tensor_scalar(k.dinv_w[:, :], deg_ps[1], 1.0, None, ALU.add))
                c.mark(dve.tensor_scalar(k.dinv_c[:, :], deg_ps[0], 1.0, None, ALU.add))
                c.wait()
                dve.reciprocal(k.mean_scale[:, :], k.mean_scale[:, :])
                dve.reciprocal(k.dinv_w[:, :], k.dinv_w[:, :])
                c.mark(dve.reciprocal(k.dinv_c[:, :], k.dinv_c[:, :]))
                k.dve_end = k.dve_chain.at(GROUPS * per + c.n)
                k.dve_total = GROUPS * per + c.n

            @block.scalar
            def _(act):
                with act.Fori(0, TILES // DEPTH) as it:
                    for b in range(DEPTH):
                        t = it * DEPTH + b
                        act.wait_ge(lane_ready.sem, lane_ready.at(t + 1))
                        for part in range(3):
                            act.activation(lane_hot[:, b, 1 + part, :], lane_hot[:, b, 0, :], ACT.Copy,
                                           scale=ew_part[part][:, bass.ds(t, 1)]).then_inc(weighted_ready.sem, 1)
                act.wait_ge(k.dve_chain.sem, k.dve_end)
                act.activation(k.dinv_w[:, :], k.dinv_w[:, :], ACT.Sqrt)
                act.activation(k.dinv_c[:, :], k.dinv_c[:, :], ACT.Sqrt)

            @block.tensor
            def _(pe):
                def degrees(t, b, first):
                    for part in range(4):
                        if part == 0:
                            pe.wait_ge(lane_ready.sem, lane_ready.at(t + 1))
                        else:
                            pe.wait_ge(weighted_ready.sem, weighted_ready.at(t * 3 + part))
                        mm = pe.matmul(deg_ps[min(part, 1)], lane_hot[:, b, part, :], onehot[:, b, 1, :],
                                       start=first and part < 2, stop=True, skip_group_check=True)
                    mm.then_inc(counted.sem, 1)

                def tile(t, b, first):
                    for n, o in enumerate(keys):
                        if not (first and b == 0):
                            pe.wait_ge(ranked.sem, ranked.at(t * 2 + n - 1))
                            pe.matmul(count_ps[o][:, 0:TILES], from_on[:, :], onehot[:, (b - 1) % DEPTH, n, :],
                                      start=False, stop=True, skip_group_check=True)
                        pe.wait_ge(hot_ready.sem, hot_ready.at(t * 2 + n + 1))
                        pe.matmul(count_ps[o][:, 0:TILES], before[:, :], onehot[:, b, n, :], start=False,
                                  stop=True, skip_group_check=True).then_inc(ranks_ready.sem, 1)
                    if not (first and b == 0):
                        degrees(t - 1, (b - 1) % DEPTH, first and b == 1)
                for t in range(DEPTH):
                    tile(t, t, True)
                with pe.Fori(1, TILES // DEPTH) as it:
                    for b in range(DEPTH):
                        tile(it * DEPTH + b, b, False)
                degrees(TILES - 1, DEPTH - 1, False)

            @block.gpsimd
            def _(pool):
                with pool.Fori(0, GROUPS // 2) as it:
                    for half in range(2):
                        g = it * 2 + half
                        pool.wait_ge(k.dve_chain.sem, k.dve_chain.at(g * 6 + 6))
                        pool.sem_inc(k.pool_pass, 1)
                        for n, o in enumerate(keys):
                            for q in range(GT):
                                pool.indirect_dma_start(
                                    k.rec[o], bass.IndirectOffsetOnAxis(ap=place[:, half, n, q:q + 1], axis=0),
                                    staged[o][:, half, q, :], None).then_inc(k.pool_pair[half].sem, 16)
                for half in range(2):
                    pool.wait_ge(k.pool_pair[half].sem, k.pool_pair[half].at(128 * GROUPS // 2))
            for half in range(2):
                k.pool_pair[half].advance(128 * GROUPS // 2)
            k.dve_chain.advance(k.dve_total)
            hot_ready.advance(2 * (TILES + AHEAD))
            lane_ready.advance(TILES + AHEAD)
            weighted_ready.advance(3 * TILES)
            ranks_ready.advance(2 * TILES)
            ranked.advance(2 * TILES)
            counted.advance(TILES)


def tile_starts(k, keys, tile_i, bins, count_ps, starts):
    nc, s = k.nc, k.s
    LOW = 16
    JOINT = 4
    HIGH = P // JOINT
    PARTS = 7
    cut = TILES // PARTS
    with ExitStack() as ctx:
        def sb(name, shape, dt=F32):
            return ctx.enter_context(nc.sbuf_tensor(name, shape, dt))

        digit_i = sb("digit_i", [P, 2, 2, TILES], I32)
        digit = sb("digit", [P, 2, 2, TILES], F16)
        high, low = sb("high_hot", [P, 2, cut, HIGH], BF16), sb("low_hot", [P, 2, cut, LOW], BF16)
        first_i, first = sb("first_i", [P, LOW], I32), sb("first_f", [P, LOW])
        counts = sb("counts", [P, 2, LOW])
        bins_f = sb("bins_f", [P, TILES + 1])
        after = sb("after", [P, 4, TILES + 1])
        ones = sb("ones_starts", [P, P])
        counted, tiles_made, starts_done = (ctx.enter_context(nc.semaphore(n)) for n in (
            "highs_lows_counted", "tiles_made", "starts_done"))
        with nc.Block() as block:
            @block.gpsimd
            def _(pool):
                pool.iota(first_i[:, :], pattern=[[1, LOW]], base=0, channel_multiplier=LOW).then_inc(tiles_made, 1)

            @block.vector
            def _(dve):
                c = Chain(k.dve_chain, dve)
                for n, o in enumerate(keys):
                    dve.tensor_scalar(digit_i[:, n, 0, :], tile_i[o][:, :], 4, None, ALU.arith_shift_right)
                    c.mark(dve.tensor_scalar(digit_i[:, n, 1, :], tile_i[o][:, :], LOW - 1, None, ALU.bitwise_and))
                dve.memset(ones[:, :], 1.0)
                dve.tensor_copy(bins_f[:, :], bins[:, :])
                dve.wait_ge(tiles_made, 1)
                c.mark(dve.tensor_scalar(first_i[:, :], first_i[:, :], HIGH * LOW - 1, None, ALU.bitwise_and))
                c.wait()
                c.mark(dve.tensor_copy(first[:, :], first_i[:, :]))
                c.wait()
                c.mark(dve.tensor_copy(digit[:, :, :, :], digit_i[:, :, :, :]))
                c.wait()

                def hots(part, first):
                    for n in range(2):
                        if not first:
                            dve.wait_ge(s.step_done.sem, s.step_done.at(part * 2 + n - 1))
                        for d, (hot, size) in enumerate(((high, HIGH), (low, LOW))):
                            made = dve.tensor_tensor(
                                hot[:, n], bins[:, 0:size].unsqueeze(1).to_broadcast([P, cut, size]),
                                digit[:, n, d, bass.ds(part * cut, cut)].unsqueeze(2).to_broadcast([P, cut, size]),
                                ALU.is_equal)
                        made.then_inc(s.onehot_ready.sem, 1)
                hots(0, True)
                with dve.Fori(1, PARTS) as part:
                    hots(part, False)
                for n in range(2):
                    dve.wait_ge(s.step_done.sem, s.step_done.at(2 * PARTS - 1 + n))
                    for block_ in range(JOINT):
                        lanes = slice(block_ * HIGH, (block_ + 1) * HIGH)
                        c.mark(dve.tensor_copy(counts[lanes, n, :],
                                               k.ps[lanes, 4 + n, block_ * LOW:(block_ + 1) * LOW]))
                c.wait()
                for n in range(2):
                    for l in range(LOW):
                        if n * LOW + l >= 4:
                            dve.wait_ge(s.mm_done.sem, s.mm_done.at(n * LOW + l - 3))
                        dve.tensor_scalar(after[:, l % 4, :], bins_f[:, :], first[:, l:l + 1],
                                          counts[:, n, l:l + 1], ALU.is_gt, ALU.mult
                                          ).then_inc(s.part_ready.sem, 1)
                for n, o in enumerate(keys):
                    dve.wait_ge(s.mm_done.sem, s.mm_done.at((n + 1) * LOW))
                    dve.tensor_copy(starts[o][:, :], count_ps[o])
                k.dve_chain.advance(c.n)

            @block.tensor
            def _(pe):
                def count(part, first):
                    for n in range(2):
                        pe.wait_ge(s.onehot_ready.sem, s.onehot_ready.at(part * 2 + n + 1))
                        for m in range(0, cut, JOINT):
                            mm = pe.matmul(k.ps[:, 4 + n, 0:JOINT * LOW],
                                           high[:, n, m:m + JOINT].rearrange("p t d -> p (t d)"),
                                           low[:, n, m:m + JOINT].rearrange("p t d -> p (t d)"),
                                           start=first and m == 0, stop=True, skip_group_check=True)
                        mm.then_inc(s.step_done.sem, 1)
                count(0, True)
                with pe.Fori(1, PARTS) as part:
                    count(part, False)
                for n, o in enumerate(keys):
                    for l in range(LOW):
                        pe.wait_ge(s.part_ready.sem, s.part_ready.at(n * LOW + l + 1))
                        pe.matmul(count_ps[o], ones[:, :], after[:, l % 4, :], start=(l == 0), stop=True,
                                  skip_group_check=True).then_inc(s.mm_done.sem, 1)
        s.step_done.advance(2 * PARTS)
        s.onehot_ready.advance(2 * PARTS)
        s.part_ready.advance(2 * LOW)
        s.mm_done.advance(2 * LOW)


def plan_steps(k, number, o, starts):
    nc, s = k.nc, k.s
    with ExitStack() as ctx:
        def sb(name, shape, dt=F32):
            return ctx.enter_context(nc.sbuf_tensor(f"{name}_{o}", shape, dt))

        def sem(name):
            return ctx.enter_context(nc.semaphore(f"{name}_{o}"))

        width = 4 if o == "dst" else 2
        half = STEPS // 2
        recs = sb("sorted", [P, TILES, width])
        k_i, k_f = sb("k_i", [P, STEPS], I32), sb("k_f", [P, STEPS])
        thr_i = sb("thr_i", [P, 4], I32)
        thr = sb("thr", [P, 2, 4])
        junk = sb("junk_p", [P, TILES])
        last = sb("last", [P, 2, 4])
        index_i, index = sb("index_i", [P, 4], I32), sb("index", [P, 4])
        le = sb("le", [P, 4, STEPS])
        gt = sb("gt", [P, 4, STEPS])
        chosen = sb("chosen", [P, 4, STEPS])
        node_t = sb("node_t", [P, 4, P])
        w_t = sb("w_t", [P, 4, P])
        ones = sb("ones_f", [P, P])
        ik = sb("ik", [P, STEPS])
        jk = sb("jk", [P, STEPS])
        jk128 = sb("jk128", [P, STEPS])
        row = sb("row", [1, 6, STEPS])
        row_i = sb("row_i", [1, 3, STEPS], I32)
        ls_row = sb("ls_row", [1, 512])
        trash_i = sb("trash_i", [1, STEPS], I32)
        loaded, iotas, ready, transposed, copied = (sem(n) for n in ("recs", "iotas_p", "chosen_r", "trans", "copied"))
        summed, last_ready, last_out, last_in = (sem(n) for n in ("summed", "last_r", "last_out", "last_in"))
        cols = k.rel[o]
        values = [recs[:, :, 0]] + ([recs[:, :, 2]] if o == "dst" else [])
        with nc.Block() as block:
            @block.sync
            def _(sp):
                sp.dma_start(recs[:, :, :], k.rec[o].rearrange("(p t) c -> p t c", p=P)).then_inc(loaded, 16)
                sp.wait_ge(last_ready, 1)
                for c in range(4):
                    sp.dma_start(k.last_step_dram[number, c * P:(c + 1) * P].rearrange("(p a) -> p a", a=1),
                                 last[:, 0, c:c + 1]).then_inc(last_out, 16)
                sp.wait_ge(last_out, 64)
                sp.dma_start(ls_row[:, :], k.last_step_dram[number:number + 1, :]).then_inc(last_in, 16)
                sp.wait_ge(last_in, 16)
                sp.wait_ge(loaded, 16)

            @block.gpsimd
            def _(pool):
                pool.iota(k_i[:, :], pattern=[[1, STEPS]], base=0, channel_multiplier=0).then_inc(iotas, 1)
                pool.iota(thr_i[:, :], pattern=[[P * P, 4]], base=P - 1, channel_multiplier=P).then_inc(iotas, 1)
                pool.iota(index_i[:, :], pattern=[[P, 4]], base=0, channel_multiplier=1).then_inc(iotas, 1)
                pool.iota(trash_i[:, :], pattern=[[0, STEPS // SPARE], [1, SPARE]], base=TILES,
                          channel_multiplier=0).then_inc(iotas, 1)

            @block.vector
            def _(dve):
                c = Chain(k.dve_chain, dve)
                dve.wait_ge(iotas, 4)
                dve.tensor_copy(k_f[:, :], k_i[:, :])
                dve.tensor_copy(index[:, :], index_i[:, :])
                dve.memset(ones[:, :], 1.0)
                dve.memset(k.rel[o][:, STEPS:], -1.0)
                dve.memset(k.keep[o][:, STEPS:], 0.0)
                dve.memset(k.idx[o][:, TILES:], 0)
                if o == "dst":
                    dve.memset(k.weight[:, STEPS:], 0.0)
                c.mark(dve.tensor_copy(thr[:, 0, :], thr_i[:, :]))
                c.wait()
                c.mark(dve.tensor_scalar(thr[:, 1, :], thr[:, 0, :], -float(P), None, ALU.add))
                c.wait()
                for a in range(2):
                    for n in range(4):
                        c.mark(dve.tensor_scalar(junk[:, :], starts[:, 1:TILES + 1], thr[:, a, n:n + 1], 0.0,
                                                 ALU.is_le, ALU.add, accum_out=last[:, a, n:n + 1]))
                        c.wait()
                c.mark(dve.tensor_tensor(last[:, 0, :], last[:, 0, :], index[:, :], ALU.add))
                c.mark(dve.scalar_tensor_tensor(last[:, 1, :], last[:, 1, :], -1.0, index[:, :], ALU.add, ALU.add))
                c.wait()
                dve.sem_inc(last_ready, 1)
                for n, (_, size) in enumerate(CHUNKS):
                    dve.tensor_scalar(gt[:, n, :], k_f[:, :], last[:, 0, n:n + 1], None, ALU.is_gt)
                    c.mark(dve.tensor_scalar(le[:, n, :], k_f[:, :], last[:, 0, n:n + 1], None, ALU.is_le))
                    c.wait()
                    c.mark(dve.scalar_tensor_tensor(chosen[:, n, :], k_f[:, :], last[:, 1, n:n + 1], le[:, n, :],
                                                    ALU.is_gt, ALU.mult))
                c.wait()
                dve.sem_inc(ready, 1)
                dve.wait_ge(transposed, len(values))
                for v in range(len(values)):
                    for n, (_, size) in enumerate(CHUNKS):
                        to = (node_t, w_t)[v]
                        c.mark(dve.tensor_copy(to[0:size, n, :], k.ps[0:size, v, n * P:(n + 1) * P]))
                c.wait()
                dve.sem_inc(copied, 1)
                dve.wait_ge(summed, 1)
                for h in range(2):
                    c.mark(dve.tensor_copy(ik[:, h * half:(h + 1) * half], k.ps[:, 2 + h, 0:half]))
                c.wait()
                c.mark(dve.tensor_tensor(jk[:, :], k_f[:, :], ik[:, :], ALU.subtract))
                dve.memset(k.keep[o][:, 0:1], 0.0)
                dve.tensor_tensor(k.keep[o][:, 1:STEPS], ik[:, 1:], ik[:, 0:STEPS - 1], ALU.not_equal)
                dve.memset(row[:, 0, STEPS - 1:STEPS], 1.0)
                dve.tensor_tensor(row[:, 0, 0:STEPS - 1], ik[0:1, 1:], ik[0:1, 0:STEPS - 1], ALU.is_equal)
                dve.tensor_scalar(row[:, 1, :], ik[0:1, :], float(TILES - 1), None, ALU.min)
                c.mark(dve.tensor_copy(row[:, 2, :], trash_i[:, :]))
                c.wait()
                c.mark(dve.tensor_scalar(jk128[:, :], jk[:, :], float(P), None, ALU.mult))
                dve.tensor_tensor(row[:, 3, :], jk[0:1, :], row[:, 2, :], ALU.subtract)
                c.mark(dve.tensor_copy(row_i[:, 0, :], row[:, 1, :]))
                c.wait()
                for h in range(2):
                    cut = slice(h * half, (h + 1) * half)
                    dve.tensor_tensor(k.rel[o][:, cut], k.ps[:, 4 + h, 0:half], jk128[:, cut], ALU.subtract)
                    if o == "dst":
                        dve.tensor_copy(k.weight[:, cut], k.ps[:, 6 + h, 0:half])
                c.mark(dve.tensor_scalar(row_i[:, 2, :], row[:, 1, :], float(-(-65536 // SLOTS)), None, ALU.mult))
                c.wait()
                c.mark(dve.tensor_scalar(row_i[:, 2, :], row_i[:, 2, :], 16, None, ALU.arith_shift_right))
                c.wait()
                c.mark(dve.scalar_tensor_tensor(row_i[:, 2, :], row_i[:, 2, :], -float(SLOTS), row_i[:, 0, :],
                                                ALU.mult, ALU.add))
                c.wait()
                row_width = D if o == "dst" else ZW
                dve.tensor_scalar(k.ctl_slot[o][:, :], row_i[:, 2, :], float(row_width), None, ALU.mult)
                c.mark(dve.tensor_tensor(row[:, 4, :], row[:, 3, :], row[:, 0, :], ALU.mult))
                c.mark(dve.tensor_scalar(row_i[:, 1, :], row_i[:, 0, :], 2, None, ALU.arith_shift_right))
                c.wait()
                c.mark(dve.tensor_tensor(row[:, 5, :], row[:, 4, :], row[:, 2, :], ALU.add))
                dve.tensor_scalar(k.ctl_ready[o][:, :], row_i[:, 1, REGION - 1::REGION], 1.0 + LANDING, None,
                                  ALU.add)
                c.wait()
                for parity in range(2):
                    dve.tensor_scalar(k.ctl_out[o][:, parity, :], row[:, 5, parity::2], float(P), None, ALU.mult)
                dve.wait_ge(last_in, 16)
                lag = SLOTS // GT
                dve.memset(k.ctl_free[o][:, 0:lag], 0)
                dve.tensor_scalar(k.ctl_free[o][:, lag:], ls_row[:, GT - 1:(GROUPS - lag) * GT:GT], 1.0, None,
                                  ALU.add)
                dve.wait_ge(loaded, 16)
                dve.tensor_copy(k.idx[o][:, 0:TILES], recs[:, :, 1])
                k.dve_chain.advance(c.n)

            @block.tensor
            def _(pe):
                pe.wait_ge(loaded, 16)
                for v, value in enumerate(values):
                    for n, (first, size) in enumerate(CHUNKS):
                        mm = pe.transpose(k.ps[0:size, v, n * P:(n + 1) * P], value[:, first:first + size],
                                          k.ident[:, :])
                    mm.then_inc(transposed, 1)
                pe.wait_ge(ready, 1)
                pe.wait_ge(copied, 1)
                for h in range(2):
                    cut = slice(h * half, (h + 1) * half)
                    jobs = [(2, ones, gt), (4, node_t, chosen)] + ([(6, w_t, chosen)] if o == "dst" else [])
                    for bank, lhs, rhs in jobs:
                        for n, (_, size) in enumerate(CHUNKS):
                            l = ones[0:size, :] if lhs is ones else lhs[0:size, n, :]
                            mm = pe.matmul(k.ps[:, bank + h, 0:half], l, rhs[0:size, n, cut],
                                           start=(n == 0), stop=(n == len(CHUNKS) - 1))
                mm.then_inc(summed, 1)


def level(k, pool, signals):
    top = max(signal.base for signal in signals)
    for signal in signals:
        if signal.base < top:
            pool.sem_inc(signal.sem, top - signal.base)
            signal.base = top
    return top


def sum_over_nodes(k, o, table, width, out, weighted=False):
    nc, s = k.nc, k.s
    scores = width == ZW
    cols = D + 1 if scores else D
    turns = STEPS // SPT
    counted = (s.onehot_ready, s.step_done, s.acc_done)
    top = max(signal.base for signal in counted)
    with ExitStack() as ctx:
        def sb(name, shape, dt=F32):
            return ctx.enter_context(nc.sbuf_tensor(k.name(name), shape, dt))

        ring = sb("ring", [P, SLOTS * width])
        acc = sb("acc", [P, SPT, width])
        hot = sb("hot", [P, 2 * HALF, P])
        staged = sb("staged", [P, 2, SLOTS], I32)
        rel, keep = sb("rel_now", [P, SPT]), sb("keep_now", [P, SPT])
        weight = sb("weight_now", [P, SPT])
        block = ctx.enter_context(nc.Block())

        @block.gpsimd
        def _(pool):
            level(k, pool, counted)

            def stage(turn, b):
                pool.tensor_copy(staged[:, b, :], k.idx[o][:, bass.ds(turn * SLOTS, SLOTS)]
                                 ).then_inc(s.idx_staged.sem, 1)

            def announce(rounds, r):
                pool.wait_ge(k.pool_dma[r].sem, k.pool_dma[r].at(rounds * (GT * 16)))
                pool.sem_inc(s.tiles_ready.sem, 1)

            stage(0, 0)
            with pool.Fori(0, GROUPS // RING // 2) as pair:
                for b in range(2):
                    it = pair * 2 + b
                    for r in range(RING):
                        g = it * RING + r
                        free = pool.value_load(k.ctl_free[o][0:1, bass.ds(g, 1)], min_val=0, max_val=STEPS)
                        announce(it + (1 if r >= LANDING else 0), (r - LANDING) % RING)
                        if r == LANDING:
                            stage(it + 1, 1 - b)
                        if r == 0:
                            pool.wait_ge(s.idx_staged.sem, s.idx_staged.at(it + 1))
                            pool.sem_inc(k.pool_pass, 1)
                        pool.wait_ge(s.step_done.sem, s.step_done.at(free))
                        pool.sem_inc(k.pool_pass, 1)
                        for q in range(r * GT, (r + 1) * GT):
                            pool.indirect_dma_start(
                                ring[:, q * width:(q + 1) * width], None, table,
                                bass.IndirectOffsetOnAxis(ap=staged[:, b, q:q + 1], axis=0)
                            ).then_inc(k.pool_dma[r].sem, 16)
            for r in range(RING - LANDING, RING):
                announce(GROUPS // RING, r)

        @block.vector
        def _(dve):
            def onehot(step):
                q = step % SPT
                scale = (weight[:, q:q + 1], ALU.mult) if weighted else (None, ALU.bypass)
                dve.tensor_scalar(hot[:, q % (2 * HALF), :], k.iota[:, :], rel[:, q:q + 1], scale[0],
                                  ALU.is_equal, scale[1]).then_inc(s.onehot_ready.sem, 1)

            dve.memset(acc[:, SPT - 1, :], 0.0)
            dve.wait_ge(s.cols_staged.sem, s.cols_staged.at(1))
            for n in range(HALF):
                onehot(n)
            with dve.Fori(0, turns) as it:
                now = dve.snap(it * SPT + top)
                count = [dve.snap(now + q) if q else now for q in range(SPT + 1)]
                regions = dve.snap(it * 2 + s.cols_staged.base)
                stored = dve.snap(it * (HALF // 2 * 16) + k.sp_store[0].base)
                for half in range(SPT // HALF):
                    region = {1: 2, 3: 3}.get(half)
                    if region:
                        dve.wait_ge(s.cols_staged.sem, regions + region)
                    dve.wait_ge(s.step_done.sem, count[half * HALF])
                    dve.wait_ge(k.sp_store[half].sem, stored)
                    dve.wait_ge(k.act_store[half].sem, stored)
                    for n in range(HALF):
                        q = half * HALF + n
                        onehot(q + HALF)
                        dve.wait_ge(s.step_done.sem, count[q + 1])
                        dve.wait_ge(s.acc_done.sem, count[q])
                        dve.scalar_tensor_tensor(acc[:, q, 0:cols], acc[:, (q - 1) % SPT, 0:cols],
                                                 keep[:, q:q + 1], k.ps[:, q % 8, 0:cols],
                                                 ALU.mult, ALU.add).then_inc(s.acc_done.sem, 1)

        @block.tensor
        def _(pe):
            with pe.Fori(0, turns * 2) as m:
                now = pe.snap(m * REGION + top)
                need = pe.value_load(k.ctl_ready[o][0:1, bass.ds(m, 1)], min_val=1, max_val=GROUPS + LANDING)
                places = nc.values_load_multi_w_load_instructions(
                    k.ctl_slot[o][0:1, bass.ds(m * REGION, REGION)], engines=[pe.engine], min_val=0,
                    max_val=(SLOTS - 1) * width, skip_runtime_bounds_check_because="worked out by plan_steps")[1]
                pe.wait_ge(s.tiles_ready.sem, s.tiles_ready.at(need))
                for q in range(REGION):
                    pe.wait_ge(s.onehot_ready.sem, now + (q + 1))
                    if q % HALF == 0:
                        pe.wait_ge(s.acc_done.sem, now + (q - HALF))
                    pe.matmul(k.ps[:, q, 0:cols], hot[:, q, :], ring[:, bass.ds(places[q], cols)],
                              start=True, stop=True).then_inc(s.step_done.sem, 1)

        @block.sync
        def _(sp):
            with sp.Fori(0, turns) as it:
                now = sp.snap(it * SPT + top)
                if scores:
                    exps = sp.snap(it * (SPT // HALF) + s.exp_ready.base)
                for region in range(2):
                    rows_to = nc.values_load_multi_w_load_instructions(
                        k.ctl_out[o][0:1, 0, bass.ds((it * 2 + region) * HALF, HALF)], engines=[sp.engine],
                        min_val=0, max_val=NP + SPARE * P - P, skip_runtime_bounds_check_because="worked out by plan_steps")[1]
                    for n, to in enumerate(rows_to):
                        q = region * REGION + 2 * n
                        if scores:
                            sp.wait_ge(s.exp_ready.sem, exps + (q // HALF + 1))
                        else:
                            sp.wait_ge(s.acc_done.sem, now + (q + 1))
                        sp.sem_inc(k.sp_pass, 1)
                        sp.dma_start(out[bass.ds(to, P), 0:width], acc[:, q, :]
                                     ).then_inc(k.sp_store[q // HALF].sem, 16)
            for half in range(SPT // HALF):
                sp.wait_ge(k.sp_store[half].sem, k.sp_store[half].at(turns * (HALF // 2 * 16)))

        @block.scalar
        def _(act):
            def stage_columns(step, region):
                cut = slice(region * REGION, (region + 1) * REGION)
                act.copy(rel[:, cut], k.rel[o][:, bass.ds(step, REGION)])
                if weighted:
                    act.copy(weight[:, cut], k.weight[:, bass.ds(step, REGION)])
                act.copy(keep[:, cut], k.keep[o][:, bass.ds(step, REGION)]).then_inc(s.cols_staged.sem, 1)

            for region in range(2):
                stage_columns(region * REGION, region)
            with act.Fori(0, turns) as it:
                now = act.snap(it * SPT + top)
                if scores:
                    exps = act.snap(it * (SPT // HALF) + s.exp_ready.base)
                for region in range(2):
                    rows_to = nc.values_load_multi_w_load_instructions(
                        k.ctl_out[o][0:1, 1, bass.ds((it * 2 + region) * HALF, HALF)], engines=[act.engine],
                        min_val=0, max_val=NP + SPARE * P - P, skip_runtime_bounds_check_because="worked out by plan_steps")[1]
                    for n, to in enumerate(rows_to):
                        q = region * REGION + 2 * n + 1
                        if scores:
                            half = q // HALF
                            if q % HALF == 1:
                                act.wait_ge(s.acc_done.sem, now + (half + 1) * HALF)
                                act.activation(acc[:, half * HALF:(half + 1) * HALF, D + 1],
                                               acc[:, half * HALF:(half + 1) * HALF, D], ACT.Exp, scale=-1.0
                                               ).then_inc(s.exp_ready.sem, 1)
                            act.wait_ge(s.exp_ready.sem, exps + (half + 1))
                        else:
                            act.wait_ge(s.acc_done.sem, now + (q + 1))
                        act.dma_start(out[bass.ds(to, P), 0:width], acc[:, q, :]
                                      ).then_inc(k.act_store[q // HALF].sem, 16)
                    stage_columns((it + 1) * SPT + region * REGION, region)
            for half in range(SPT // HALF):
                act.wait_ge(k.act_store[half].sem, k.act_store[half].at(turns * (HALF // 2 * 16)))

        for r in range(RING):
            k.pool_dma[r].advance(GT * 16 * (GROUPS // RING))
        for half in range(SPT // HALF):
            k.sp_store[half].advance(turns * (HALF // 2 * 16))
            k.act_store[half].advance(turns * (HALF // 2 * 16))
        s.idx_staged.advance(GROUPS // RING + 1)
        s.cols_staged.advance(2 * turns + 2)
        s.tiles_ready.advance(GROUPS + LANDING)
        s.onehot_ready.advance(STEPS + HALF)
        s.step_done.advance(STEPS)
        s.acc_done.advance(STEPS)
        if scores:
            s.exp_ready.advance(STEPS // HALF)


class Turn:

    def __init__(self, loop, g, r, it, n):
        self.loop, self.g, self.r, self.it, self.n = loop, g, r, it, n

    @property
    def b(self):
        return self.r % 2

    @property
    def done(self):
        return self.loop.count(self.n + 1)

    @property
    def prior(self):
        return self.loop.count(self.n)

    @property
    def free(self):
        return self.loop.count(self.n if self.r == 0 else self.n - 1)

    @property
    def slot_before(self):
        return self.loop.count(self.n + 1 - RING)

    def landed(self, dmas):
        return self.loop.rounds(self.loop.k.sp_dma[self.r].base, dmas, (self.n - self.r) // RING + 1)

    def gathered(self, dmas):
        return self.loop.rounds(self.loop.k.pool_dma[self.r].base, dmas, (self.n - self.r) // RING + 1)

    def rounds_of(self, signals, dmas):
        return self.loop.rounds(signals[self.r].base, dmas, (self.n - self.r) // RING)

    def stored(self, dmas):
        return self.loop.rounds(self.loop.k.pool_dma[self.r].base, dmas, (self.n - self.r) // RING)


class Round:

    def __init__(self, k, eng, it):
        self.k, self.eng, self.it, self.known = k, eng, it, {}

    def value(self, key, make):
        if isinstance(self.it, int):
            return make()
        if key not in self.known:
            self.known[key] = self.eng.snap(make())
        return self.known[key]

    def count(self, n):
        first = self.value("first", lambda: self.it * RING + self.k.top)
        return first if n == 0 else self.value(n, lambda: first + n)

    def rounds(self, base, dmas, more):
        return self.value((base, dmas, more), lambda: (self.it + more) * (16 * dmas) + base)


def by_groups(k, eng, *parts):
    def turn(loop, r, ends):
        for lag, part in parts:
            n = r - lag
            if not ends or 0 <= loop.it * RING + n < GROUPS:
                part(Turn(loop, loop.it * RING + n, n % RING, loop.it + n // RING, n))
    first = Round(k, eng, 0)
    for r in range(RING):
        turn(first, r, True)
    with eng.Fori(1, GROUPS // RING) as it:
        loop = Round(k, eng, it)
        for r in range(RING):
            turn(loop, r, False)
    end = Round(k, eng, GROUPS // RING)
    for r in range(max(lag for lag, _ in parts)):
        turn(end, r, True)


def node_pass(k, loads, stores, engines, tallies, used_up=()):
    nc, s = k.nc, k.s
    counted = k.s.all + [signal for pair in k.norm_signals for signal in pair]
    k.top = max(signal.base for signal in counted)
    with nc.Block() as block:
        @block.sync
        def _(sp):
            def body(t):
                for signal in used_up:
                    sp.wait_ge(signal.sem, t.slot_before)
                if not used_up:
                    sp.wait_ge(k.pool_dma[t.r].sem, t.stored(len(stores)))
                sp.sem_inc(k.sp_pass, 1)
                for buf, table, *cols in loads:
                    c = cols[0] if cols else D
                    sp.dma_start(buf[:, t.r, :, 0:c], rows(table, t.g * GT, GT)[:, :, 0:c]
                                 ).then_inc(k.sp_dma[t.r].sem, 16)
            by_groups(k, sp, (0, body))

        @block.gpsimd
        def _(pool):
            level(k, pool, counted)

            def body(t):
                pool.wait_ge(s.out_ready.sem, t.done)
                pool.sem_inc(k.pool_pass, 1)
                for buf, table in stores:
                    pool.dma_start(rows(table, t.g * GT, GT), buf[:, t.r]).then_inc(k.pool_dma[t.r].sem, 16)
            if "gpsimd" in engines:
                by_groups(k, pool, (0, lambda t: engines["gpsimd"](pool, t)), (4, body))
            else:
                by_groups(k, pool, (0, body))
            for r in range(RING):
                pool.wait_ge(k.pool_dma[r].sem, k.pool_dma[r].at(16 * len(stores) * (GROUPS // RING)))

        if "tensor" in engines:
            block.tensor(engines["tensor"])
        block.vector(engines["vector"])
        block.scalar(engines["scalar"])
    for r in range(RING):
        k.sp_dma[r].advance(16 * len(loads) * (GROUPS // RING))
        k.pool_dma[r].advance(16 * len(stores) * (GROUPS // RING))
    for signal, n in tallies:
        signal.advance(n * GROUPS)


class Norm:

    def __init__(self, k, ctx, number=0):
        self.k = k
        self.bn, self.stat, self.root_sig, self.inverse, self.scaled, self.factor = (x[number] for x in k.norm_signals)

        def sb(name, shape):
            return ctx.enter_context(k.nc.sbuf_tensor(k.name(name), shape, F32))
        self.stats, self.mv = sb("bn_stats", [P, RING, GT, 6]), sb("mean_var", [P, RING, GT, 2])
        self.root, self.scale = sb("root", [P, RING, GT]), sb("rstd", [P, RING, GT])
        self.shift = sb("shift", [P, RING, GT])

    def moments(self, dve, x, t):
        for q in range(GT):
            ins = dve.bn_stats(self.stats[:, t.r, q, :], x[:, t.r, q, :])
        ins.then_inc(self.bn.sem, 1)

    def mean_variance(self, dve, t):
        dve.wait_ge(self.bn.sem, t.done)
        dve.sem_inc(self.k.dve_pass, 1)
        for q in range(GT):
            ins = dve.bn_aggr(self.mv[:, t.r, q, :], self.stats[:, t.r, q, :])
        ins.then_inc(self.stat.sem, 1)

    def statistics(self, dve, x, t):
        self.moments(dve, x, t)
        self.mean_variance(dve, t)

    def square_root(self, act, t):
        act.wait_ge(self.stat.sem, t.done)
        act.activation(self.root[:, t.r, :], self.mv[:, t.r, :, 1], ACT.Sqrt,
                       bias=self.k.eps[:, 0:1]).then_inc(self.root_sig.sem, 1)

    def inverse_root(self, dve, t):
        dve.wait_ge(self.root_sig.sem, t.done)
        dve.reciprocal(self.scale[:, t.r, :], self.root[:, t.r, :]).then_inc(self.inverse.sem, 1)

    def scale_by(self, dve, t, extra):
        dve.wait_ge(self.inverse.sem, t.done)
        dve.tensor_tensor(self.scale[:, t.r, :], self.scale[:, t.r, :], extra, ALU.mult
                          ).then_inc(self.scaled.sem, 1)

    def row_shift(self, dve, t, scaled):
        dve.wait_ge((self.scaled if scaled else self.inverse).sem, t.done)
        dve.scalar_tensor_tensor(self.shift[:, t.r, :], self.mv[:, t.r, :, 0], -1.0, self.scale[:, t.r, :],
                                 ALU.mult, ALU.mult).then_inc(self.factor.sem, 1)

    def factors(self, dve, t, extra=None):
        self.inverse_root(dve, t)
        if extra is not None:
            self.scale_by(dve, t, extra)
        self.row_shift(dve, t, extra is not None)

    def apply(self, act, t, out, x, func):
        act.wait_ge(self.factor.sem, t.done)
        for q in range(GT):
            ins = act.activation(out[:, t.r, q, :], x[:, t.r, q, :], func, bias=self.shift[:, t.r, q:q + 1],
                                 scale=self.scale[:, t.r, q:q + 1])
        return ins

    def tallies(self, extra=False):
        return [(x, 1) for x in (self.bn, self.stat, self.root_sig, self.inverse, self.factor)
                + ((self.scaled,) if extra else ())]


def ring_buffer(k, ctx, name, width=D):
    return ctx.enter_context(k.nc.sbuf_tensor(k.name(name), [P, RING, GT, width], F32))


def pair_buffer(k, ctx, name):
    return ctx.enter_context(k.nc.sbuf_tensor(k.name(name), [P, 2, GT, D], F32))


def bank(k, n):
    return k.ps[:, n, :].rearrange("p (t d) -> p t d", t=GT)


def norm_pass(k, x, out):
    s = k.s
    with ExitStack() as ctx:
        xb, hb = ring_buffer(k, ctx, "x"), ring_buffer(k, ctx, "h")
        norm = Norm(k, ctx)

        def vector(dve):
            def moments(t):
                dve.wait_ge(k.sp_dma[t.r].sem, t.landed(1))
                norm.moments(dve, xb, t)
            by_groups(k, dve, (0, moments), (2, lambda t: norm.inverse_root(dve, t)),
                      (0, lambda t: norm.mean_variance(dve, t)), (2, lambda t: norm.row_shift(dve, t, False)))

        def scalar(act):
            def apply(t):
                act.wait_ge(k.pool_dma[t.r].sem, t.stored(1))
                norm.apply(act, t, hb, xb, ACT.Relu).then_inc(s.out_ready.sem, 1)
            by_groups(k, act, (1, lambda t: norm.square_root(act, t)), (3, apply))

        node_pass(k, [(xb, x)], [(hb, out)], {"vector": vector, "scalar": scalar},
                  [(s.out_ready, 1)] + norm.tallies(), (s.out_ready,))


def sage_pass(k, h, w_self, w_neigh, bias, out, x=None, x_out=None):
    s = k.s
    with ExitStack() as ctx:
        hb, ab = ring_buffer(k, ctx, "h"), ring_buffer(k, ctx, "agg")
        yb, ob = ring_buffer(k, ctx, "y"), ring_buffer(k, ctx, "out")
        xb = ring_buffer(k, ctx, "x") if x is not None else None
        mean = pair_buffer(k, ctx, "mean")
        h_t, a_t = pair_buffer(k, ctx, "h_t"), pair_buffer(k, ctx, "mean_t")
        norm = Norm(k, ctx)
        loads = [(hb, h), (ab, k.agg)] + ([(xb, x)] if x is not None else [])
        stores = [(ob, out)] + ([(yb, x_out)] if x is not None else [])

        def landed(eng, t):
            eng.wait_ge(k.sp_dma[t.r].sem, t.landed(len(loads)))

        def scalar(act):
            def means(t):
                b = t.b
                landed(act, t)
                act.wait_ge(s.h_t.sem, t.free)
                for q in range(GT):
                    ins = act.activation(mean[:, b, q, :], ab[:, t.r, q, :], ACT.Copy,
                                         scale=k.mean_scale[:, bass.ds(t.g * GT + q, 1)])
                ins.then_inc(s.part_ready.sem, 1)

            def copy(t):
                b = t.b
                act.wait_ge(s.in_t.sem, t.done)
                act.wait_ge(s.mm_done.sem, t.free)
                act.copy(h_t[:, b], bank(k, b)).then_inc(s.in_copied.sem, 1)

            def relu(t):
                act.wait_ge(s.mm_read.sem, t.done)
                act.activation(ob[:, t.r], yb[:, t.r], ACT.Relu).then_inc(s.out_ready.sem, 1)

            def normed(t):
                norm.apply(act, t, ob, yb, ACT.Relu).then_inc(s.out_ready.sem, 1)
            if x is None:
                by_groups(k, act, (0, means), (1, copy), (3, relu))
            else:
                by_groups(k, act, (3, lambda t: norm.square_root(act, t)), (0, means), (1, copy), (4, normed))

        def tensor(pe):
            def turn(t):
                b = t.b
                landed(pe, t)
                pe.wait_ge(s.in_copied.sem, t.free)
                for q in range(GT):
                    mm = pe.transpose(bank(k, b)[:, q, :], hb[:, t.r, q, :], k.ident[:, :])
                mm.then_inc(s.in_t.sem, 1)
                pe.wait_ge(s.part_ready.sem, t.done)
                pe.wait_ge(s.h_copied.sem, t.free)
                for q in range(GT):
                    mm = pe.transpose(bank(k, 2 + b)[:, q, :], mean[:, b, q, :], k.ident[:, :])
                mm.then_inc(s.h_t.sem, 1)

            def multiply(t):
                b = t.b
                pe.wait_ge(s.in_copied.sem, t.done)
                pe.wait_ge(s.h_copied.sem, t.done)
                pe.wait_ge(s.mm_read.sem, t.free)
                for q in range(GT):
                    pe.matmul(bank(k, 4 + b)[:, q, :], h_t[:, b, q, :], w_self[:, :], start=True, stop=False)
                    mm = pe.matmul(bank(k, 4 + b)[:, q, :], a_t[:, b, q, :], w_neigh[:, :],
                                   start=False, stop=True)
                mm.then_inc(s.mm_done.sem, 1)
            by_groups(k, pe, (1, turn), (2, multiply))

        def vector(dve):
            def copy(t):
                b = t.b
                dve.wait_ge(s.h_t.sem, t.done)
                dve.wait_ge(s.mm_done.sem, t.free)
                dve.tensor_copy(a_t[:, b], bank(k, 2 + b)).then_inc(s.h_copied.sem, 1)

            def add(t):
                dve.wait_ge(s.mm_done.sem, t.done)
                dve.wait_ge(k.pool_dma[t.r].sem, t.stored(len(stores)))
                dve.tensor_tensor(yb[:, t.r], bank(k, 4 + t.b), bias[:, :, :], ALU.add).then_inc(s.mm_read.sem, 1)

            def residual(t):
                landed(dve, t)
                dve.wait_ge(s.mm_read.sem, t.done)
                dve.tensor_tensor(yb[:, t.r], yb[:, t.r], xb[:, t.r], ALU.add).then_inc(s.x_ready.sem, 1)

            def moments(t):
                dve.wait_ge(s.x_ready.sem, t.done)
                norm.moments(dve, yb, t)
            if x is None:
                by_groups(k, dve, (1, copy), (2, add))
            else:
                by_groups(k, dve, (4, lambda t: norm.inverse_root(dve, t)), (2, add), (1, copy), (2, residual),
                          (4, lambda t: norm.row_shift(dve, t, False)), (2, moments),
                          (2, lambda t: norm.mean_variance(dve, t)))

        node_pass(k, loads, stores, {"vector": vector, "scalar": scalar, "tensor": tensor},
                  [(s.out_ready, 1), (s.h_t, 1), (s.part_ready, 1), (s.in_t, 1),
                   (s.mm_done, 1), (s.in_copied, 1), (s.h_copied, 1), (s.mm_read, 1)]
                  + (norm.tallies() + [(s.x_ready, 1)] if x is not None else []),
                  (s.in_t, s.part_ready) + ((s.x_ready,) if x is not None else ()))


def attention_pass(k, h, x, x_out, out):
    s = k.s
    with ExitStack() as ctx:
        hb, ab = ring_buffer(k, ctx, "h"), ring_buffer(k, ctx, "agg", ZW)
        xb, yb, ob = (ring_buffer(k, ctx, n) for n in ("x", "y", "out"))
        h_t, n_t = pair_buffer(k, ctx, "h_t"), pair_buffer(k, ctx, "n_t")
        nb = hb
        norm = Norm(k, ctx)
        loads = [(hb, h), (ab, k.agg_src, ZW), (xb, x)]

        def landed(eng, t):
            eng.wait_ge(k.sp_dma[t.r].sem, t.landed(len(loads)))

        def scalar(act):
            def first(t):
                b = t.b
                act.wait_ge(s.in_t.sem, t.done)
                act.wait_ge(s.mm_done.sem, t.free)
                act.copy(h_t[:, b], bank(k, b)).then_inc(s.in_copied.sem, 1)

            def normed(t):
                norm.apply(act, t, nb, yb, ACT.Relu).then_inc(s.h_ready.sem, 1)

            def stored(t):
                act.wait_ge(s.mm2_done.sem, t.done)
                act.copy(ob[:, t.r], bank(k, 6 + t.b)).then_inc(s.out_ready.sem, 1)
            by_groups(k, act, (2, lambda t: norm.square_root(act, t)), (0, first), (6, stored), (3, normed))

        def tensor(pe):
            def turn(t):
                b = t.b
                landed(pe, t)
                pe.wait_ge(s.in_copied.sem, t.free)
                for q in range(GT):
                    mm = pe.transpose(bank(k, b)[:, q, :], hb[:, t.r, q, :], k.ident[:, :])
                mm.then_inc(s.in_t.sem, 1)

            def multiply(t):
                b = t.b
                pe.wait_ge(s.in_copied.sem, t.done)
                pe.wait_ge(s.mm_read.sem, t.free)
                for q in range(GT):
                    mm = pe.matmul(bank(k, 4 + b)[:, q, :], h_t[:, b, q, :], k.w["u"][:, :],
                                   start=True, stop=True)
                mm.then_inc(s.mm_done.sem, 1)

            def turn_normed(t):
                b = t.b
                pe.wait_ge(s.h_ready.sem, t.done)
                pe.wait_ge(s.h_copied.sem, t.free)
                for q in range(GT):
                    mm = pe.transpose(bank(k, 2 + b)[:, q, :], nb[:, t.r, q, :], k.ident[:, :])
                mm.then_inc(s.h_t.sem, 1)

            def multiply_normed(t):
                b = t.b
                pe.wait_ge(s.h_copied.sem, t.done)
                pe.wait_ge(s.out_ready.sem, t.free)
                for q in range(GT):
                    mm = pe.matmul(bank(k, 6 + b)[:, q, :], n_t[:, b, q, :], k.w["gcn"][:, :],
                                   start=True, stop=True)
                mm.then_inc(s.mm2_done.sem, 1)
            by_groups(k, pe, (1, multiply), (4, turn_normed), (0, turn), (5, multiply_normed))

        def vector(dve):
            def weigh(t):
                landed(dve, t)
                for q in range(GT):
                    ins = dve.scalar_tensor_tensor(xb[:, t.r, q, :], ab[:, t.r, q, 0:D], ab[:, t.r, q, D + 1:D + 2],
                                                   xb[:, t.r, q, :], ALU.mult, ALU.add)
                ins.then_inc(s.second_add.sem, 1)

            def bias(t):
                dve.wait_ge(s.mm_done.sem, t.done)
                dve.wait_ge(k.pool_dma[t.r].sem, t.stored(2))
                dve.tensor_tensor(yb[:, t.r], bank(k, 4 + t.b), k.b["u"][:, :, :], ALU.add
                                  ).then_inc(s.mm_read.sem, 1)

            def total(t):
                dve.wait_ge(s.mm_read.sem, t.done)
                dve.wait_ge(s.second_add.sem, t.done)
                dve.tensor_tensor(yb[:, t.r], yb[:, t.r], xb[:, t.r], ALU.add).then_inc(s.x_ready.sem, 1)

            def moments(t):
                dve.wait_ge(s.x_ready.sem, t.done)
                norm.moments(dve, yb, t)

            def scale(t):
                norm.scale_by(dve, t, k.dinv_w[:, bass.ds(t.g * GT, GT)])

            def copy(t):
                b = t.b
                dve.wait_ge(s.h_t.sem, t.done)
                dve.wait_ge(s.mm2_done.sem, t.free)
                dve.tensor_copy(n_t[:, b], bank(k, 2 + b)).then_inc(s.h_copied.sem, 1)
            by_groups(k, dve, (3, lambda t: norm.inverse_root(dve, t)), (1, bias), (3, scale), (0, weigh),
                      (3, lambda t: norm.row_shift(dve, t, True)), (1, total), (4, copy), (1, moments),
                      (1, lambda t: norm.mean_variance(dve, t)))

        node_pass(k, loads, [(ob, out), (yb, x_out)], {"vector": vector, "scalar": scalar, "tensor": tensor},
                  [(s.out_ready, 1), (s.h_t, 1), (s.in_t, 1), (s.mm_done, 1), (s.in_copied, 1),
                   (s.h_copied, 1), (s.mm_read, 1), (s.x_ready, 1), (s.h_ready, 1),
                   (s.mm2_done, 1), (s.second_add, 1)] + norm.tallies(extra=True), (s.h_t, s.x_ready))


def elu_pass(k, table, out):
    s, nc = k.s, k.nc
    with ExitStack() as ctx:
        ab, tb = ring_buffer(k, ctx, "agg"), ring_buffer(k, ctx, "own")
        eb, qb = ring_buffer(k, ctx, "exp"), ring_buffer(k, ctx, "square")
        ones = ctx.enter_context(nc.sbuf_tensor("ones_col", [P, 1], F32))
        ones_ready = ctx.enter_context(nc.semaphore("ones_col_ready"))

        def vector(dve):
            dve.memset(ones[:, :], 1.0).then_inc(ones_ready, 1)

            def first(t):
                dve.wait_ge(k.sp_dma[t.r].sem, t.landed(2))
                dve.tensor_tensor(ab[:, t.r], ab[:, t.r], tb[:, t.r], ALU.add).then_inc(s.first_add.sem, 1)

            def scaled(t):
                dve.wait_ge(s.first_add.sem, t.done)
                for q in range(GT):
                    ins = dve.scalar_tensor_tensor(tb[:, t.r, q, :], ab[:, t.r, q, :],
                                                   k.dinv_w[:, bass.ds(t.g * GT + q, 1)], k.b["gcn"][:, q, :],
                                                   ALU.mult, ALU.add)
                ins.then_inc(s.x_ready.sem, 1)

            def less_one(t):
                dve.wait_ge(s.exp_ready.sem, t.done)
                dve.tensor_scalar(eb[:, t.r], eb[:, t.r], 1.0, -1.0, ALU.min, ALU.add).then_inc(s.second_add.sem, 1)

            def larger(t):
                dve.wait_ge(s.second_add.sem, t.done)
                dve.tensor_tensor(eb[:, t.r], eb[:, t.r], tb[:, t.r], ALU.max).then_inc(s.h_ready.sem, 1)
            by_groups(k, dve, (2, less_one), (0, first), (2, larger), (0, scaled))

        def scalar(act):
            def exponential(t):
                act.wait_ge(s.x_ready.sem, t.done)
                act.wait_ge(k.pool_dma[t.r].sem, t.stored(1))
                act.activation(eb[:, t.r], tb[:, t.r], ACT.Exp).then_inc(s.exp_ready.sem, 1)

            def square(t):
                act.wait_ge(s.h_ready.sem, t.done)
                act.activation(qb[:, t.r], eb[:, t.r], ACT.Square).then_inc(s.part_ready.sem, 1)
            by_groups(k, act, (1, exponential), (3, square))

        def tensor(pe):
            pe.wait_ge(ones_ready, 1)

            def total(t):
                pe.wait_ge(s.part_ready.sem, t.done)
                first = isinstance(t.g, int) and t.g == 0
                for n, buf in enumerate((eb, qb)):
                    mm = pe.matmul(k.ps[0:1, n, :], ones[:, :], buf[:, t.r].rearrange("p t d -> p (t d)"),
                                   start=first, stop=True, skip_group_check=True)
                mm.then_inc(s.out_ready.sem, 1)

            def tail(t):
                pe.wait_ge(s.part_ready.sem, t.done)
                for n, buf in enumerate((eb, qb)):
                    for q in range(GT):
                        real = min(P, N_REAL - (t.g * GT + q) * P)
                        if real > 0:
                            mm = pe.matmul(k.ps[0:1, n, q * P:(q + 1) * P], ones[0:real, :], buf[0:real, t.r, q, :],
                                           start=False, stop=True, skip_group_check=True)
                mm.then_inc(s.out_ready.sem, 1)

            for r in range(RING):
                total(Turn(Round(k, pe, 0), r, r, 0, r))
            with pe.Fori(1, GROUPS // RING - 1) as it:
                loop = Round(k, pe, it)
                for r in range(RING):
                    total(Turn(loop, it * RING + r, r, it, r))
            for r in range(RING):
                last = Turn(Round(k, pe, GROUPS // RING - 1), GROUPS - RING + r, r, GROUPS // RING - 1, r)
                (tail if r == RING - 1 else total)(last)

        node_pass(k, [(ab, k.agg), (tb, table)], [(eb, out)],
                  {"vector": vector, "scalar": scalar, "tensor": tensor},
                  [(s.out_ready, 1), (s.first_add, 1), (s.second_add, 1), (s.x_ready, 1), (s.exp_ready, 1),
                   (s.h_ready, 1), (s.part_ready, 1)], (s.h_ready,))


def batch_factors(k):
    nc = k.nc
    with ExitStack() as ctx:
        def sb(name, shape):
            return ctx.enter_context(nc.sbuf_tensor(name, shape, F32))

        means, sq = sb("bn_means", [1, 2, D]), sb("bn_sq", [1, D])
        factor = sb("bn_factor", [1, 2, D])
        ones = sb("ones_row", [1, P])
        var_ready, root_ready, rows_ready, spread = (ctx.enter_context(nc.semaphore(n)) for n in (
            "var_ready", "root_ready_bn", "rows_ready", "spread"))
        with nc.Block() as block:
            @block.vector
            def _(dve):
                c = Chain(k.dve_chain, dve)
                dve.memset(ones[:, :], 1.0)
                for n in range(2):
                    c.mark(dve.tensor_reduce(means[:, n, :], k.ps[0:1, n, :].rearrange("p (t d) -> p d t", t=GT),
                                             AX.X, ALU.add))
                c.wait()
                c.mark(dve.tensor_scalar(means[:, :, :], means[:, :, :], 1.0 / N_REAL, None, ALU.mult))
                c.wait()
                c.mark(dve.tensor_tensor(sq[:, :], means[:, 0, :], means[:, 0, :], ALU.mult))
                c.wait()
                c.mark(dve.tensor_tensor(sq[:, :], means[:, 1, :], sq[:, :], ALU.subtract))
                c.wait()
                dve.tensor_scalar(sq[:, :], sq[:, :], 0.0, None, ALU.max).then_inc(var_ready, 1)
                dve.wait_ge(root_ready, 1)
                c.mark(dve.reciprocal(sq[:, :], sq[:, :]))
                c.wait()
                c.mark(dve.tensor_tensor(factor[:, 0, :], sq[:, :], k.bn_rows[:, 0, :], ALU.mult))
                c.wait()
                c.mark(dve.tensor_tensor(sq[:, :], means[:, 0, :], factor[:, 0, :], ALU.mult))
                c.wait()
                dve.tensor_tensor(factor[:, 1, :], k.bn_rows[:, 1, :], sq[:, :], ALU.subtract
                                  ).then_inc(rows_ready, 1)
                dve.wait_ge(spread, 1)
                for n, name in enumerate(("bn_a", "bn_b")):
                    for t in range(GT):
                        dve.tensor_copy(k.b[name][:, t, :], k.ps[:, 2, n * D:(n + 1) * D])
                k.dve_chain.advance(c.n)

            @block.scalar
            def _(act):
                act.wait_ge(var_ready, 1)
                act.activation(sq[:, :], sq[:, :], ACT.Sqrt, bias=k.eps[0:1, 0:1]).then_inc(root_ready, 1)

            @block.tensor
            def _(pe):
                pe.wait_ge(rows_ready, 1)
                pe.matmul(k.ps[:, 2, 0:2 * D], ones[:, :], factor[:, :, :].rearrange("p n d -> p (n d)"),
                          start=True, stop=True).then_inc(spread, 1)


def batch_pass(k, o, x, x_out, out):
    s = k.s
    with ExitStack() as ctx:
        eb, xb, yb, ob = (ring_buffer(k, ctx, n) for n in ("o", "x", "y", "out"))
        inner, outer = Norm(k, ctx, 0), Norm(k, ctx, 1)

        def gpsimd(pool, t):
            pool.wait_ge(k.sp_dma[t.r].sem, t.landed(2))
            pool.sem_inc(k.pool_pass, 1)
            pool.tensor_tensor(eb[:, t.r], eb[:, t.r], k.b["bn_a"][:, :, :], ALU.mult).then_inc(s.first_add.sem, 1)
            pool.tensor_tensor(xb[:, t.r], xb[:, t.r], k.b["ln_b"][:, :, :], ALU.add).then_inc(s.g_ready.sem, 1)

        def vector(dve):
            def shift(t):
                dve.wait_ge(s.first_add.sem, t.done)
                dve.tensor_tensor(eb[:, t.r], eb[:, t.r], k.b["bn_b"][:, :, :], ALU.add).then_inc(s.second_add.sem, 1)

            def inner_moments(t):
                dve.wait_ge(s.second_add.sem, t.done)
                inner.moments(dve, eb, t)

            def gamma(t):
                dve.wait_ge(s.h_ready.sem, t.done)
                dve.tensor_tensor(yb[:, t.r], yb[:, t.r], k.b["ln_g"][:, :, :], ALU.mult).then_inc(s.f_ready.sem, 1)

            def residual(t):
                dve.wait_ge(s.f_ready.sem, t.done)
                dve.wait_ge(s.g_ready.sem, t.done)
                dve.tensor_tensor(yb[:, t.r], yb[:, t.r], xb[:, t.r], ALU.add).then_inc(s.x_ready.sem, 1)

            def outer_moments(t):
                dve.wait_ge(s.x_ready.sem, t.done)
                outer.moments(dve, yb, t)
            by_groups(k, dve, (2, gamma), (1, lambda t: inner.inverse_root(dve, t)),
                      (3, lambda t: outer.inverse_root(dve, t)), (0, shift),
                      (1, lambda t: inner.row_shift(dve, t, False)),
                      (3, lambda t: outer.scale_by(dve, t, k.dinv_c[:, bass.ds(t.g * GT, GT)])),
                      (2, residual), (3, lambda t: outer.row_shift(dve, t, True)), (0, inner_moments),
                      (2, outer_moments), (0, lambda t: inner.mean_variance(dve, t)),
                      (2, lambda t: outer.mean_variance(dve, t)))

        def scalar(act):
            def inner_norm(t):
                inner.apply(act, t, yb, eb, ACT.Identity).then_inc(s.h_ready.sem, 1)

            def roots(t):
                inner.square_root(act, t)

            def outer_roots(t):
                outer.square_root(act, t)

            def outer_norm(t):
                outer.apply(act, t, ob, yb, ACT.Relu).then_inc(s.out_ready.sem, 1)
            by_groups(k, act, (1, roots), (3, outer_roots), (1, inner_norm), (3, outer_norm))

        node_pass(k, [(eb, o), (xb, x)], [(ob, out), (yb, x_out)],
                  {"vector": vector, "scalar": scalar, "gpsimd": gpsimd},
                  [(s.out_ready, 1), (s.first_add, 1), (s.second_add, 1), (s.x_ready, 1), (s.h_ready, 1),
                   (s.f_ready, 1), (s.g_ready, 1)]
                  + inner.tallies() + outer.tallies(extra=True))


def gcn_pass(k, table, w, bias, out, x=None):
    s = k.s
    with ExitStack() as ctx:
        ab, tb, ob = (ring_buffer(k, ctx, n) for n in ("agg", "own", "out"))
        xb = ring_buffer(k, ctx, "x") if x is not None else None
        sum_t = pair_buffer(k, ctx, "sum_t")
        loads = [(ab, k.agg), (tb, table)] + ([(xb, x)] if x is not None else [])

        def landed(eng, t):
            eng.wait_ge(k.sp_dma[t.r].sem, t.landed(len(loads)))

        def vector(dve):
            def add(t):
                landed(dve, t)
                dve.tensor_tensor(ab[:, t.r], ab[:, t.r], tb[:, t.r], ALU.add).then_inc(s.first_add.sem, 1)

            def finish(t):
                dve.wait_ge(s.mm_done.sem, t.done)
                for q in range(GT):
                    ins = dve.scalar_tensor_tensor(tb[:, t.r, q, :], bank(k, 4 + t.b)[:, q, :],
                                                   k.dinv_c[:, bass.ds(t.g * GT + q, 1)], bias[:, q, :],
                                                   ALU.mult, ALU.add)
                ins.then_inc(s.mm_read.sem, 1)
                if x is not None:
                    dve.wait_ge(s.mm_read.sem, t.done)
                    dve.wait_ge(k.pool_dma[t.r].sem, t.stored(1))
                    dve.tensor_tensor(ob[:, t.r], tb[:, t.r], xb[:, t.r], ALU.add).then_inc(s.out_ready.sem, 1)
            by_groups(k, dve, (0, add), (2, finish))

        def scalar(act):
            def copy(t):
                act.wait_ge(s.in_t.sem, t.done)
                act.wait_ge(s.mm_done.sem, t.free)
                act.copy(sum_t[:, t.b], bank(k, t.b)).then_inc(s.in_copied.sem, 1)

            def scale(t):
                act.wait_ge(s.mm_read.sem, t.done)
                act.wait_ge(k.pool_dma[t.r].sem, t.stored(1))
                for q in range(GT):
                    ins = act.activation(ob[:, t.r, q, :], tb[:, t.r, q, :], ACT.Copy,
                                         scale=k.dinv_c[:, bass.ds(t.g * GT + q, 1)])
                ins.then_inc(s.out_ready.sem, 1)
            if x is None:
                by_groups(k, act, (1, copy), (3, scale))
            else:
                by_groups(k, act, (1, copy))

        def tensor(pe):
            def turn(t):
                pe.wait_ge(s.first_add.sem, t.done)
                pe.wait_ge(s.in_copied.sem, t.free)
                for q in range(GT):
                    mm = pe.transpose(bank(k, t.b)[:, q, :], ab[:, t.r, q, :], k.ident[:, :])
                mm.then_inc(s.in_t.sem, 1)

            def multiply(t):
                pe.wait_ge(s.in_copied.sem, t.done)
                pe.wait_ge(s.mm_read.sem, t.free)
                for q in range(GT):
                    mm = pe.matmul(bank(k, 4 + t.b)[:, q, :], sum_t[:, t.b, q, :], w[:, :],
                                   start=True, stop=True)
                mm.then_inc(s.mm_done.sem, 1)
            by_groups(k, pe, (1, turn), (2, multiply))

        node_pass(k, loads, [(ob, out)], {"vector": vector, "scalar": scalar, "tensor": tensor},
                  [(s.out_ready, 1), (s.first_add, 1), (s.mm_done, 1), (s.mm_read, 1), (s.in_t, 1),
                   (s.in_copied, 1)], (s.out_ready,))


def edge_pass(k, h, ins):
    nc, s = k.nc, k.s
    scale = float(D) ** -0.5
    turns = GROUPS // RING
    used = (s.in_t, s.in_copied, s.nj_copied, s.ea_copied, s.h_t, s.mm_done, s.k_ready, s.g_ready, s.u_ready,
            s.q_ready, s.exp_ready, s.a_ready, s.w_ready, s.wz_ready, s.mask_ready, s.m1_ready, s.f_ready,
            s.prod_ready, s.um_ready, s.z_ready)
    k.top = max(signal.base for signal in used)
    with ExitStack() as ctx:
        def sb(name, shape, dt=F32):
            return ctx.enter_context(nc.sbuf_tensor(name, shape, dt))

        ni, nj = sb("ni", [P, RING, GT * D]), sb("nj", [P, RING, GT * D])
        ea = sb("ea", [P, RING, GT, EA])
        zb = sb("zb", [P, RING, GT, ZW])
        staged = sb("staged_ij", [P, 2, 2, SLOTS], I32)
        ni_t, nj_t, ea_t, f_t = (sb(n, [P, RING, GT * P]) for n in ("ni_t", "nj_t", "ea_t", "f_t"))
        ex, m1, q_t, prod = (sb(n, [P, 2, GT * P]) for n in ("ex", "m1", "q_t", "prod"))
        mask, um, a, exp_a, wz = (sb(n, [P, RING, GT]) for n in ("mask", "um", "score", "exp_a", "wz"))
        ea_in = ins["edge_attr_70"].rearrange("(p t) c -> p t c", p=P)
        z_out = k.z.rearrange("(p t) c -> p t c", p=P)
        B_NI, B_NJ, B_EA, B_PRE, B_Q, B_K, B_U, B_G = range(8)
        ps = k.ps

        with nc.Block() as block:
            @block.gpsimd
            def _(pool):
                level(k, pool, used)

                def stage(turn, b):
                    for n, table in enumerate((k.edge_src, k.edge_dst)):
                        ins_ = pool.tensor_copy(staged[:, b, n, :], table[:, bass.ds(turn * SLOTS, SLOTS)])
                    ins_.then_inc(s.idx_staged.sem, 1)

                stage(0, 0)
                with pool.Fori(0, turns // 2) as pair:
                    for b in range(2):
                        it = pair * 2 + b
                        for r in range(RING):
                            if r == 0:
                                pool.wait_ge(s.idx_staged.sem, s.idx_staged.at(it + 1))
                                pool.sem_inc(k.pool_pass, 1)
                            if r == 1:
                                pool.wait_ge(s.in_t.sem, k.top + it * RING)
                                pool.sem_inc(k.pool_pass, 1)
                                stage(it + 1, 1 - b)
                            pool.wait_ge(s.in_t.sem, it * RING + (k.top + r + 1 - RING))
                            pool.sem_inc(k.pool_pass, 1)
                            for n, buf in enumerate((ni, nj)):
                                for q in range(GT):
                                    pool.indirect_dma_start(
                                        buf[:, r, q * D:(q + 1) * D], None, h, bass.IndirectOffsetOnAxis(
                                            ap=staged[:, b, n, r * GT + q:r * GT + q + 1], axis=0)
                                    ).then_inc(k.pool_dma[r].sem, 16)

            @block.sync
            def _(sp):
                def load(t):
                    sp.wait_ge(k.sp_second[t.r].sem, t.rounds_of(k.sp_second, 1))
                    sp.sem_inc(k.sp_pass, 1)
                    sp.dma_start(ea[:, t.r], ea_in[:, bass.ds(t.g * GT, GT), :]).then_inc(k.sp_dma[t.r].sem, 16)

                def store(t):
                    sp.wait_ge(s.z_ready.sem, t.done)
                    sp.sem_inc(k.sp_pass, 1)
                    sp.dma_start(z_out[:, bass.ds(t.g * GT, GT), :], zb[:, t.r]
                                 ).then_inc(k.sp_second[t.r].sem, 16)
                by_groups(k, sp, (0, load), (5, store))
                for r in range(RING):
                    sp.wait_ge(k.sp_second[r].sem, k.sp_second[r].at(16 * turns))

            @block.tensor
            def _(pe):
                def turn(t):
                    pe.wait_ge(k.pool_dma[t.r].sem, t.gathered(2 * GT))
                    pe.wait_ge(k.sp_dma[t.r].sem, t.landed(1))
                    pe.wait_ge(s.in_copied.sem, t.prior)
                    pe.wait_ge(s.nj_copied.sem, t.prior)
                    pe.wait_ge(s.ea_copied.sem, t.prior)
                    for q in range(GT):
                        cut = slice(q * P, (q + 1) * P)
                        pe.transpose(ps[:, B_NI, cut], ni[:, t.r, cut], k.ident[:, :])
                        pe.transpose(ps[:, B_NJ, cut], nj[:, t.r, cut], k.ident[:, :])
                        mm = pe.transpose(ps[0:EF, B_EA, cut], ea[:, t.r, q, 0:EF], k.ident[:, :])
                    mm.then_inc(s.in_t.sem, 1)

                def project(t):
                    pe.wait_ge(s.in_copied.sem, t.done)
                    pe.wait_ge(s.q_ready.sem, t.prior)
                    pe.matmul(ps[:, B_Q, :], k.w["q"][:, :], ni_t[:, t.r, :], start=True,
                              stop=True).then_inc(s.h_t.sem, 1)
                    pe.wait_ge(s.nj_copied.sem, t.done)
                    pe.wait_ge(s.ea_copied.sem, t.done)
                    pe.wait_ge(s.f_ready.sem, t.prior)
                    pe.matmul(ps[:, B_PRE, :], k.w["ni"][:, :], ni_t[:, t.r, :], start=True, stop=False)
                    pe.matmul(ps[:, B_PRE, :], k.w["nj"][:, :], nj_t[:, t.r, :], start=False, stop=False)
                    pe.matmul(ps[:, B_PRE, :], k.w["ea"][0:EF, :], ea_t[0:EF, t.r, :], start=False,
                              stop=True).then_inc(s.mm_done.sem, 1)

                def key(t):
                    pe.wait_ge(s.f_ready.sem, t.done)
                    pe.wait_ge(s.prod_ready.sem, t.prior)
                    pe.matmul(ps[:, B_K, :], k.w["k"][:, :], f_t[:, t.r, :], start=True,
                              stop=True).then_inc(s.k_ready.sem, 1)

                def score(t):
                    pe.wait_ge(s.prod_ready.sem, t.done)
                    pe.wait_ge(s.um_ready.sem, t.prior)
                    for q in range(GT):
                        mm = pe.matmul(ps[:, B_U, q:q + 1], prod[:, t.b, q * P:(q + 1) * P], k.wa[:, :],
                                       start=True, stop=True)
                    mm.then_inc(s.u_ready.sem, 1)
                    pe.wait_ge(s.z_ready.sem, t.prior)
                    for q in range(GT):
                        cut = slice(q * P, (q + 1) * P)
                        mm = pe.matmul(ps[:, B_G, cut], f_t[:, t.r, cut], k.w["u"][:, :], start=True, stop=True)
                    mm.then_inc(s.g_ready.sem, 1)
                by_groups(k, pe, (3, score), (2, key), (1, project), (0, turn))

            @block.scalar
            def _(act):
                def scores(t):
                    act.wait_ge(s.um_ready.sem, t.done)
                    act.activation(a[:, t.r, :], um[:, t.r, :], ACT.Tanh).then_inc(s.a_ready.sem, 1)
                    act.wait_ge(s.a_ready.sem, t.done)
                    act.activation(exp_a[:, t.r, :], a[:, t.r, :], ACT.Exp).then_inc(s.w_ready.sem, 1)

                def exponentials(t):
                    act.wait_ge(s.h_t.sem, t.done)
                    act.wait_ge(s.prod_ready.sem, t.free)
                    act.activation(q_t[:, t.b, :], ps[:, B_Q, :], ACT.Copy, scale=scale
                                   ).then_inc(s.q_ready.sem, 1)
                    act.wait_ge(s.mm_done.sem, t.done)
                    act.wait_ge(s.m1_ready.sem, t.free)
                    act.activation(ex[:, t.b, :], ps[:, B_PRE, :], ACT.Exp, bias=k.bf[:, 0:1]
                                   ).then_inc(s.exp_ready.sem, 1)

                def copy(t):
                    act.wait_ge(s.in_t.sem, t.done)
                    act.copy(ni_t[:, t.r, :], ps[:, B_NI, :]).then_inc(s.in_copied.sem, 1)
                    act.copy(ea_t[0:EF, t.r, :], ps[0:EF, B_EA, :]).then_inc(s.ea_copied.sem, 1)
                by_groups(k, act, (3, scores), (1, exponentials), (0, copy))

            @block.vector
            def _(dve):
                dve.memset(zb[:, :, :, D + 1:], 0.0)

                def product(t):
                    dve.wait_ge(s.k_ready.sem, t.done)
                    dve.wait_ge(s.q_ready.sem, t.done)
                    dve.wait_ge(s.u_ready.sem, t.free)
                    dve.tensor_tensor(prod[:, t.b, :], q_t[:, t.b, :], ps[:, B_K, :], ALU.mult
                                      ).then_inc(s.prod_ready.sem, 1)

                def masked(t):
                    dve.wait_ge(s.u_ready.sem, t.done)
                    dve.tensor_tensor(um[:, t.r, :], ps[:, B_U, 0:GT], mask[:, t.r, :], ALU.mult
                                      ).then_inc(s.um_ready.sem, 1)

                def features(t):
                    dve.wait_ge(s.exp_ready.sem, t.done)
                    dve.tensor_scalar(m1[:, t.b, :], ex[:, t.b, :], 1.0, -1.0, ALU.min, ALU.add
                                      ).then_inc(s.m1_ready.sem, 1)
                    dve.wait_ge(s.m1_ready.sem, t.done)
                    dve.scalar_tensor_tensor(f_t[:, t.r, :], ps[:, B_PRE, :], k.bf[:, 0:1], m1[:, t.b, :], ALU.add,
                                             ALU.max).then_inc(s.f_ready.sem, 1)

                def results(t):
                    dve.wait_ge(s.w_ready.sem, t.done)
                    dve.tensor_tensor(wz[:, t.r, :], exp_a[:, t.r, :], mask[:, t.r, :], ALU.mult
                                      ).then_inc(s.wz_ready.sem, 1)
                    dve.tensor_copy(zb[:, t.r, :, D], a[:, t.r, :])
                    dve.wait_ge(s.wz_ready.sem, t.done)
                    dve.wait_ge(s.g_ready.sem, t.done)
                    for q in range(GT):
                        z = dve.tensor_scalar(zb[:, t.r, q, 0:D], ps[:, B_G, q * P:(q + 1) * P],
                                              wz[:, t.r, q:q + 1], None, ALU.mult)
                    z.then_inc(s.z_ready.sem, 1)

                def copy(t):
                    dve.wait_ge(s.in_t.sem, t.done)
                    dve.tensor_copy(nj_t[:, t.r, :], ps[:, B_NJ, :]).then_inc(s.nj_copied.sem, 1)
                    dve.wait_ge(k.sp_dma[t.r].sem, t.landed(1))
                    dve.tensor_scalar(mask[:, t.r, :], ea[:, t.r, :, 0], 8.0, None, ALU.is_lt
                                      ).then_inc(s.mask_ready.sem, 1)
                by_groups(k, dve, (3, masked), (2, product), (3, results), (1, features), (0, copy))

        for r in range(RING):
            k.pool_dma[r].advance(16 * 2 * GT * turns)
            k.sp_dma[r].advance(16 * turns)
            k.sp_second[r].advance(16 * turns)
        s.idx_staged.advance(turns + 1)
        for signal in used:
            signal.advance(GROUPS)


def build(nc, ins, out, stop=None):
    k = Program()
    k.nc, k.names = nc, 0

    def name(text):
        k.names += 1
        return f"{text}_{k.names}"
    k.name = name
    with ExitStack() as ctx:
        setup(k, ctx)
        t0, t1 = k.table
        r0, r1 = k.res
        w, b = k.w, k.b
        steps = [
            lambda: constants_and_loads(k, ins),
            lambda: prepare(k, ins),
            lambda: norm_pass(k, ins["x"], t0),
            lambda: sum_over_nodes(k, "dst", t0, D, k.agg),
            lambda: sage_pass(k, t0, w["self0"], w["neigh0"], b["b0"], t1),
            lambda: sum_over_nodes(k, "dst", t1, D, k.agg),
            lambda: sage_pass(k, t1, w["self1"], w["neigh1"], b["b1"], t0, ins["x"], r0),
            lambda: edge_pass(k, t0, ins),
            lambda: sum_over_nodes(k, "src", k.z, ZW, k.agg_src),
            lambda: attention_pass(k, t0, r0, r1, t1),
            lambda: sum_over_nodes(k, "dst", t1, D, k.agg, weighted=True),
            lambda: elu_pass(k, t1, k.elu_out),
            lambda: batch_factors(k),
            lambda: batch_pass(k, k.elu_out, r1, r0, t0),
            lambda: sum_over_nodes(k, "dst", t0, D, k.agg),
            lambda: gcn_pass(k, t0, w["g0"], b["g0"], t1),
            lambda: sum_over_nodes(k, "dst", t1, D, k.agg),
            lambda: gcn_pass(k, t1, w["g1"], b["g1"], t0),
            lambda: sum_over_nodes(k, "dst", t0, D, k.agg),
            lambda: gcn_pass(k, t0, w["g2"], b["g2"], out, x=r0),
        ]
        for n, step in enumerate(steps[:stop]):
            step()


NAMES = ["x", "src", "dst", "edge_attr_70", "edge_weight",
         "L0_gnn_W_self0", "L0_gnn_W_neigh0", "L0_gnn_b0", "L0_gnn_W_self1", "L0_gnn_W_neigh1", "L0_gnn_b1",
         "L1_gnn_Wf", "L1_gnn_bf", "L1_gnn_Wq", "L1_gnn_Wk", "L1_gnn_Wa", "L1_gnn_Wu", "L1_gnn_bu",
         "L2_gnn_W", "L2_gnn_b", "L2_gnn_bn_gamma", "L2_gnn_bn_beta", "L2_gnn_ln_gamma", "L2_gnn_ln_beta",
         "L3_gnn_W", "L3_gnn_b"]
STOP = None


def kernel(**inputs):
    import numpy as np
    import concourse.bacc as bacc
    from concourse.bass_utils import run_bass_kernel_spmd

    nc = bacc.Bacc("TRN2", target_bir_lowering=False, num_devices=1)
    arrays, ins = {}, {}
    for name in NAMES:
        a = np.ascontiguousarray(inputs[name])
        if a.shape[0] == N_REAL:
            padded = np.full((NP,) + a.shape[1:], NP - 1 if name in ("src", "dst") else 0, a.dtype)
            padded[:N_REAL] = a
            a = padded
        arrays[name] = a
        ins[name] = nc.dram_tensor(name, a.shape, mybir.dt.from_np(a.dtype), kind="ExternalInput").ap()
    out = nc.dram_tensor("out", (NP, D), F32, kind="ExternalOutput").ap()
    build(nc, ins, out, STOP)
    r = run_bass_kernel_spmd(nc, [arrays], core_ids=[0])
    return r.results[0]["out"][:N_REAL]
```
